# Optimizing a Trainium2 kernel written in Bass

```python
import numpy as np
import jax
import jax.numpy as jnp

def _softmax(x, axis=-1):
    return jax.nn.softmax(x, axis=axis)

def _gelu(x):
    return jax.nn.gelu(x, approximate=True)

def _silu(x):
    return jax.nn.silu(x)

def _sigmoid(x):
    return jax.nn.sigmoid(x)

def _layernorm(x, axis=-1, eps=1e-05):
    m = jnp.mean(x, axis=axis, keepdims=True)
    v = jnp.var(x, axis=axis, keepdims=True)
    return (x - m) / jnp.sqrt(v + eps)

def _scatter_add(tgt, idx, src, axis=0):
    return tgt.at[idx].add(src)

def _segment_sum(src, seg, n):
    return jax.ops.segment_sum(src, seg, n)
kernel_name = 'mk_sandwich_d1_jaxref_r8_8b0386'

def setup_inputs(seed: int=0):
    np.random.seed(seed)
    _w = jnp.asarray

    def _L0_attn_setup():
        import jax, jax.numpy as jnp
        import numpy as np
        EMBED = 256
        HEADS = 16
        HEAD_DIM = EMBED // HEADS
        CHUNK = 128
        BASE = 10000.0
        EPS = 1e-06

        def _alibi_log_decay(h):
            slopes = 2.0 ** (-8.0 * (jnp.arange(h, dtype=jnp.float32) + 1.0) / h)
            return -slopes

        def _lrpe_rotate(x):
            b, n, h, d = x.shape
            half = d // 2
            theta = BASE ** (-2.0 * jnp.arange(half, dtype=jnp.float32) / d)
            ang = jnp.arange(n, dtype=jnp.float32)[:, None] * theta[None, :]
            cos = jnp.cos(ang)[None, :, None, :]
            sin = jnp.sin(ang)[None, :, None, :]
            x1, x2 = (x[..., :half], x[..., half:])
            return jnp.concatenate([x1 * cos - x2 * sin, x1 * sin + x2 * cos], axis=-1)

        def _lightning_attn(q, k, v, log_lam):
            b, n, h, d = q.shape
            C = CHUNK
            nc = n // C
            qc = q.reshape(b, nc, C, h, d).transpose(1, 0, 2, 3, 4)
            kc = k.reshape(b, nc, C, h, d).transpose(1, 0, 2, 3, 4)
            vc = v.reshape(b, nc, C, h, d).transpose(1, 0, 2, 3, 4)
            i = jnp.arange(C, dtype=jnp.float32)
            diff = i[:, None] - i[None, :]
            D = jnp.where(diff[None] >= 0, jnp.exp(log_lam[:, None, None] * diff[None]), 0.0)
            decay_q = jnp.exp(log_lam[None, :] * (i[:, None] + 1.0))
            decay_k = jnp.exp(log_lam[None, :] * (C - 1.0 - i[:, None]))
            lam_C = jnp.exp(log_lam * C)

            def step(S, qkv):
                qi, ki, vi = qkv
                scores = jnp.einsum('bthd,bshd->bhts', qi, ki) * D[None]
                o_intra = jnp.einsum('bhts,bshd->bthd', scores, vi)
                o_inter = jnp.einsum('bthd,bhde->bthe', qi * decay_q[None, :, :, None], S)
                S_new = lam_C[None, :, None, None] * S + jnp.einsum('bshd,bshe->bhde', ki * decay_k[None, :, :, None], vi)
                return (S_new, o_intra + o_inter)
            S0 = jnp.zeros((b, h, d, d), q.dtype)
            _, o = jax.lax.scan(step, S0, (qc, kc, vc))
            return o.transpose(1, 0, 2, 3, 4).reshape(b, n, h, d)

        def _gated_group_rmsnorm(o, gate, weight):
            b, n, d = o.shape
            x = o * jax.nn.sigmoid(gate)
            xg = x.reshape(b, n, HEADS, HEAD_DIM)
            ms = jnp.mean(xg * xg, axis=-1, keepdims=True)
            xg = xg * jax.lax.rsqrt(ms + EPS)
            return xg.reshape(b, n, d) * weight
        key = jax.random.key(seed)
        ks = jax.random.split(key, 8)
        b, n, d = (2, 256, EMBED)
        std = 0.02
        return {'x': jax.random.normal(ks[0], (b, n, d), jnp.float32), 'Wq': jax.random.normal(ks[1], (d, d), jnp.float32) * std, 'Wk': jax.random.normal(ks[2], (d, d), jnp.float32) * std, 'Wv': jax.random.normal(ks[3], (d, d), jnp.float32) * std, 'Wo': jax.random.normal(ks[4], (d, d), jnp.float32) * std, 'Wg1': jax.random.normal(ks[5], (d, HEAD_DIM), jnp.float32) * std, 'Wg2': jax.random.normal(ks[6], (HEAD_DIM, d), jnp.float32) * std, 'norm_weight': jnp.ones((d,), jnp.float32)}
    _L0_attn_in = _L0_attn_setup()

    def _L0_ffn_setup():
        import jax, jax.numpy as jnp
        import numpy as np
        B, S, H = (4, 256, 256)
        INTER = 512
        E = 8
        TOPK = 2
        SHARED_I = INTER * 2

        def moe_forward(hidden_states, router_w, w1, w2, w_gate, w_up, w_down):
            b, s, h = hidden_states.shape
            x = hidden_states.reshape(-1, h)
            T = x.shape[0]
            logits = x @ router_w
            top_logits, top_indices = jax.lax.top_k(logits, TOPK)
            scores = jax.nn.softmax(top_logits, axis=-1)
            flat_idx = top_indices.reshape(-1)
            sorted_pos = jnp.argsort(flat_idx, stable=True)
            permuted = x[sorted_pos // TOPK]
            expert_ids = flat_idx[sorted_pos]
            out = jnp.zeros((T * TOPK, h), x.dtype)
            for e in range(E):
                mask = (expert_ids == e)[:, None]
                f1 = permuted * mask @ w1[e]
                g, u = jnp.split(f1, 2, axis=-1)
                act = jax.nn.silu(g) * u
                out = out + jnp.where(mask, act @ w2[e], 0.0)
            unperm = jnp.zeros_like(out).at[sorted_pos].set(out)
            combined = (unperm.reshape(T, TOPK, h) * scores[..., None]).sum(axis=1)
            shared = jax.nn.silu(x @ w_gate) * (x @ w_up) @ w_down
            return (combined + shared).reshape(b, s, h)
        key = jax.random.key(seed)
        ks = jax.random.split(key, 7)
        s = 0.02
        return {'hidden_states': jax.random.normal(ks[0], (B, S, H), jnp.float32), 'router_w': jax.random.normal(ks[1], (H, E), jnp.float32) * s, 'w1': jax.random.normal(ks[2], (E, H, 2 * INTER), jnp.float32) * s, 'w2': jax.random.normal(ks[3], (E, INTER, H), jnp.float32) * s, 'w_gate': jax.random.normal(ks[4], (H, SHARED_I), jnp.float32) * s, 'w_up': jax.random.normal(ks[5], (H, SHARED_I), jnp.float32) * s, 'w_down': jax.random.normal(ks[6], (SHARED_I, H), jnp.float32) * s}
    _L0_ffn_in = _L0_ffn_setup()
    _d = {'L0_attn_x': _L0_attn_in['x'], 'L0_attn_Wq': _L0_attn_in['Wq'], 'L0_attn_Wk': _L0_attn_in['Wk'], 'L0_attn_Wv': _L0_attn_in['Wv'], 'L0_attn_Wo': _L0_attn_in['Wo'], 'L0_attn_Wg1': _L0_attn_in['Wg1'], 'L0_attn_Wg2': _L0_attn_in['Wg2'], 'L0_attn_norm_weight': _L0_attn_in['norm_weight'], 'L0_ffn_router_w': _L0_ffn_in['router_w'], 'L0_ffn_w1': _L0_ffn_in['w1'], 'L0_ffn_w2': _L0_ffn_in['w2'], 'L0_ffn_w_gate': _L0_ffn_in['w_gate'], 'L0_ffn_w_up': _L0_ffn_in['w_up'], 'L0_ffn_w_down': _L0_ffn_in['w_down']}
    _x0 = _d['L0_attn_x']
    _d['L0_attn_x'] = jax.random.normal(jax.random.fold_in(jax.random.key(seed), 1), (8, 512, 256), dtype=_x0.dtype)
    del _x0
    return _d

def reference(L0_attn_x, L0_attn_Wq, L0_attn_Wk, L0_attn_Wv, L0_attn_Wo, L0_attn_Wg1, L0_attn_Wg2, L0_attn_norm_weight, L0_ffn_router_w, L0_ffn_w1, L0_ffn_w2, L0_ffn_w_gate, L0_ffn_w_up, L0_ffn_w_down):

    def _L0_attn_ref(x, Wq, Wk, Wv, Wo, Wg1, Wg2, norm_weight):
        import jax, jax.numpy as jnp
        import numpy as np
        EMBED = 256
        HEADS = 16
        HEAD_DIM = EMBED // HEADS
        CHUNK = 128
        BASE = 10000.0
        EPS = 1e-06

        def _alibi_log_decay(h):
            slopes = 2.0 ** (-8.0 * (jnp.arange(h, dtype=jnp.float32) + 1.0) / h)
            return -slopes

        def _lrpe_rotate(x):
            b, n, h, d = x.shape
            half = d // 2
            theta = BASE ** (-2.0 * jnp.arange(half, dtype=jnp.float32) / d)
            ang = jnp.arange(n, dtype=jnp.float32)[:, None] * theta[None, :]
            cos = jnp.cos(ang)[None, :, None, :]
            sin = jnp.sin(ang)[None, :, None, :]
            x1, x2 = (x[..., :half], x[..., half:])
            return jnp.concatenate([x1 * cos - x2 * sin, x1 * sin + x2 * cos], axis=-1)

        def _lightning_attn(q, k, v, log_lam):
            b, n, h, d = q.shape
            C = CHUNK
            nc = n // C
            qc = q.reshape(b, nc, C, h, d).transpose(1, 0, 2, 3, 4)
            kc = k.reshape(b, nc, C, h, d).transpose(1, 0, 2, 3, 4)
            vc = v.reshape(b, nc, C, h, d).transpose(1, 0, 2, 3, 4)
            i = jnp.arange(C, dtype=jnp.float32)
            diff = i[:, None] - i[None, :]
            D = jnp.where(diff[None] >= 0, jnp.exp(log_lam[:, None, None] * diff[None]), 0.0)
            decay_q = jnp.exp(log_lam[None, :] * (i[:, None] + 1.0))
            decay_k = jnp.exp(log_lam[None, :] * (C - 1.0 - i[:, None]))
            lam_C = jnp.exp(log_lam * C)

            def step(S, qkv):
                qi, ki, vi = qkv
                scores = jnp.einsum('bthd,bshd->bhts', qi, ki) * D[None]
                o_intra = jnp.einsum('bhts,bshd->bthd', scores, vi)
                o_inter = jnp.einsum('bthd,bhde->bthe', qi * decay_q[None, :, :, None], S)
                S_new = lam_C[None, :, None, None] * S + jnp.einsum('bshd,bshe->bhde', ki * decay_k[None, :, :, None], vi)
                return (S_new, o_intra + o_inter)
            S0 = jnp.zeros((b, h, d, d), q.dtype)
            _, o = jax.lax.scan(step, S0, (qc, kc, vc))
            return o.transpose(1, 0, 2, 3, 4).reshape(b, n, h, d)

        def _gated_group_rmsnorm(o, gate, weight):
            b, n, d = o.shape
            x = o * jax.nn.sigmoid(gate)
            xg = x.reshape(b, n, HEADS, HEAD_DIM)
            ms = jnp.mean(xg * xg, axis=-1, keepdims=True)
            xg = xg * jax.lax.rsqrt(ms + EPS)
            return xg.reshape(b, n, d) * weight
        b, n, d = x.shape
        q = (x @ Wq).reshape(b, n, HEADS, HEAD_DIM)
        k = (x @ Wk).reshape(b, n, HEADS, HEAD_DIM)
        v = (x @ Wv).reshape(b, n, HEADS, HEAD_DIM)
        q = jax.nn.silu(q)
        k = jax.nn.silu(k)
        q = _lrpe_rotate(q)
        k = _lrpe_rotate(k)
        log_lam = _alibi_log_decay(HEADS)
        o = _lightning_attn(q, k, v, log_lam).reshape(b, n, d)
        gate = x @ Wg1 @ Wg2
        o = _gated_group_rmsnorm(o, gate, norm_weight)
        return o @ Wo

    def _L0_ffn_ref(hidden_states, router_w, w1, w2, w_gate, w_up, w_down):
        import jax, jax.numpy as jnp
        import numpy as np
        B, S, H = (4, 256, 256)
        INTER = 512
        E = 8
        TOPK = 2
        SHARED_I = INTER * 2

        def moe_forward(hidden_states, router_w, w1, w2, w_gate, w_up, w_down):
            b, s, h = hidden_states.shape
            x = hidden_states.reshape(-1, h)
            T = x.shape[0]
            logits = x @ router_w
            top_logits, top_indices = jax.lax.top_k(logits, TOPK)
            scores = jax.nn.softmax(top_logits, axis=-1)
            flat_idx = top_indices.reshape(-1)
            sorted_pos = jnp.argsort(flat_idx, stable=True)
            permuted = x[sorted_pos // TOPK]
            expert_ids = flat_idx[sorted_pos]
            out = jnp.zeros((T * TOPK, h), x.dtype)
            for e in range(E):
                mask = (expert_ids == e)[:, None]
                f1 = permuted * mask @ w1[e]
                g, u = jnp.split(f1, 2, axis=-1)
                act = jax.nn.silu(g) * u
                out = out + jnp.where(mask, act @ w2[e], 0.0)
            unperm = jnp.zeros_like(out).at[sorted_pos].set(out)
            combined = (unperm.reshape(T, TOPK, h) * scores[..., None]).sum(axis=1)
            shared = jax.nn.silu(x @ w_gate) * (x @ w_up) @ w_down
            return (combined + shared).reshape(b, s, h)
        return moe_forward(hidden_states, router_w, w1, w2, w_gate, w_up, w_down)
    x = L0_attn_x
    x = x + _layernorm(_L0_attn_ref(_layernorm(x, axis=-1), L0_attn_Wq, L0_attn_Wk, L0_attn_Wv, L0_attn_Wo, L0_attn_Wg1, L0_attn_Wg2, L0_attn_norm_weight), axis=-1)
    x = x + _layernorm(_L0_ffn_ref(_layernorm(x, axis=-1), L0_ffn_router_w, L0_ffn_w1, L0_ffn_w2, L0_ffn_w_gate, L0_ffn_w_up, L0_ffn_w_down), axis=-1)
    return x

_drawn_inputs = setup_inputs


def setup_inputs(seed=0):
    import zlib

    import numpy as np

    out = dict(_drawn_inputs(seed))
    spreads = {'L0_attn_norm_weight': (1.0, 0.2)}
    factors = {'L0_attn_Wg1': 2.7}
    for name, (base, spread) in spreads.items():
        noise = np.random.default_rng([zlib.crc32(name.encode()), seed]).standard_normal(out[name].shape)
        drawn = base * np.exp(spread * noise) if base else spread * noise
        out[name] = jnp.asarray(drawn.astype(out[name].dtype))
    for name, factor in factors.items():
        out[name] = (out[name] * factor).astype(out[name].dtype)
    return out
```

```python
from contextlib import ExitStack

import concourse.bass as bass
import numpy as np
from concourse import mybir

P = 128
SEQS, SEQ, D = 8, 512, 256
TOKENS = SEQS * SEQ
C = P
CPS = SEQ // C
CHUNKS = TOKENS // C
HEADS, HD = 16, 16
KT = D // P
EXPERTS, TOPK, INTER = 8, 2, 512
SHARED = 2 * INTER
UNITS = CHUNKS // 2
PIECES = 10
TILES = TOKENS * TOPK // P + EXPERTS - 1
LN_EPS, RMS_EPS = 1e-5, 1e-6
XS = 2.0 ** 10
NS = 2.0 ** 12
FAR = 1 << 20

F32, F16, I32, U32 = mybir.dt.float32, mybir.dt.float16, mybir.dt.int32, mybir.dt.uint32
ACT, ALU = mybir.ActivationFunctionType, mybir.AluOpType
X = mybir.AxisListType.X
ABSMAX = bass.bass_isa.ReduceOp.absmax

_F32 = [("ident", P), ("decay", HEADS * C), ("qdec", KT * C), ("block", KT * P), ("blocklam", KT * P),
        ("kdec", HEADS), ("cos", CPS * 8), ("sin", CPS * 8), ("iota8", EXPERTS), ("tok", TOPK),
        ("mhalf", HEADS), ("iotat", TILES + 1)]
_F16 = [("ident", P), ("before", P), ("ones", P), ("iota", P)]


def offsets(parts):
    out, at = {}, 0
    for name, n in parts:
        out[name] = (at, at + n)
        at += n
    return out, at


C32, N32 = offsets(_F32)
C16, N16 = offsets(_F16)


def tables():
    f = np.float32
    lam = -(f(2.0) ** (f(-8.0) * (np.arange(HEADS, dtype=f) + f(1.0)) / f(HEADS)))
    i = np.arange(C, dtype=f)
    t32 = {}
    diff = i[None, :] - i[:, None]
    dec = np.where(diff[:, None, :] >= 0, np.exp(lam[None, :, None] * np.maximum(diff, 0)[:, None, :]), 0)
    t32["decay"] = dec.reshape(P, HEADS * C)
    head = (np.arange(D) // HD).reshape(KT, P).T
    t32["qdec"] = np.exp(lam[head][:, :, None] * (i[None, None, :] + f(1))).reshape(P, KT * C)
    same = (np.arange(P)[:, None] // HD == np.arange(P)[None, :] // HD).astype(f)
    t32["block"] = np.repeat(same[:, None, :], KT, 1).reshape(P, KT * P)
    t32["blocklam"] = (same[:, None, :] * np.exp(lam * f(C))[head][:, :, None]).reshape(P, KT * P)
    t32["kdec"] = np.exp(lam[None, :] * (f(C - 1) - i[:, None]))
    theta = (f(10000.0) ** (f(-2.0) * np.arange(8, dtype=f) / f(HD))).astype(f)
    ang = (np.arange(SEQ, dtype=f)[:, None] * theta[None, :]).astype(f).reshape(CPS, C, 8).transpose(1, 0, 2)
    t32["cos"], t32["sin"] = np.cos(ang).reshape(P, -1), np.sin(ang).reshape(P, -1)
    t32["ident"] = np.eye(P)
    t32["iota8"] = np.broadcast_to(np.arange(EXPERTS), (P, EXPERTS))
    t32["tok"] = 2 * np.arange(P)[:, None] + np.arange(TOPK)[None, :] + 1
    t32["mhalf"] = np.full((P, HEADS), -0.5)
    t32["iotat"] = np.broadcast_to(np.arange(TILES + 1), (P, TILES + 1))
    t16 = {"ident": np.eye(P), "before": np.triu(np.ones((P, P)), 1), "ones": np.ones((P, P)),
           "iota": np.broadcast_to(np.arange(P), (P, P))}
    return (np.concatenate([np.asarray(t32[n], f) for n, _ in _F32], 1),
            np.concatenate([np.asarray(t16[n], np.float16) for n, _ in _F16], 1))


def layer_kernel(nc, x, wq, wk, wv, wo, wg1, wg2, norm_w, router, w1, w2, w_gate, w_up, w_down, c32d, c16d, out):
    whole = ExitStack()
    first = ExitStack()

    def sb(name, shape, dt=F32, stack=whole):
        return stack.enter_context(nc.sbuf_tensor(name, shape, dt))

    def sem(name):
        return whole.enter_context(nc.semaphore(name))

    rows_d = nc.dram_tensor("rows_d", (TOKENS, D), F32, kind="Internal").ap()
    res_d = nc.dram_tensor("res_d", (TOKENS, D), F32, kind="Internal").ap()
    shared_d = nc.dram_tensor("shared_d", (TOKENS, D), F32, kind="Internal").ap()
    picked_d = nc.dram_tensor("picked_d", (TOKENS * TOPK, D), F32, kind="Internal").ap()
    xf = x.rearrange("b n d -> (b n) d")
    outf = out.rearrange("b n d -> (b n) d")

    with whole:
        c32 = sb("c32", [P, N32])
        c16 = sb("c16", [P, N16], F16)

        def k32(name):
            return c32[:, C32[name][0]:C32[name][1]]

        def k16(name):
            return c16[:, C16[name][0]:C16[name][1]]

        w1s = sb("w1s", [P, EXPERTS, 2, KT, 2 * INTER], F16)
        w2s = sb("w2s", [P, EXPERTS, 2, INTER // P, D], F16)
        exp_scale = sb("exp_scale", [P, EXPERTS, 4])
        top_v = sb("top_v", [P, CHUNKS, TOPK])
        top_i = sb("top_i", [P, CHUNKS, TOPK])
        pmax = sb("pmax", [P, 4])
        gmax = sb("gmax", [P, 4])
        pw = sb("pw", [P, 4])
        rp = sb("rp", [P, 4])
        sc = sb("sc", [P, 16])
        (S_A, C_A, C_AH, S_Q, C_S, S_O, C_O, C_O2, S_F, C_F, C_FU, C_FD, T0_, T1_) = range(14)

        def s(col):
            return sc[:, col:col + 1]

        psum = [whole.enter_context(nc.psum_tensor(f"bank{i}", [P, 512], F32)) for i in range(8)]
        A0, A1, A2, A3, A4, A5, FB0, FB1 = psum
        FB = [FB0, FB1]


        const_in = [sem(f"const_in{i}") for i in range(4)]
        set_in = [sem(f"set_in{i}") for i in range(3)]
        zeroed, nw_folded, wg1_T, wg1_copied, wg_made, wg_copied = (sem("zeroed"), sem("nw_folded"), sem("wg1_T"),
            sem("wg1_copied"), sem("wg_made"), sem("wg_copied"))
        set_max, set_all, scale_step, set_hi, set_lo = (sem("set_max"), sem("set_all"), sem("scale_step"),
            sem("set_hi"), sem("set_lo"))
        x_in = [sem(f"x_in{i}") for i in range(CPS)]
        ln1_stats, ln1_mv, ln1_var, ln1_pow, xs_ready = (sem("ln1_stats"), sem("ln1_mv"), sem("ln1_var"),
            sem("ln1_pow"), sem("xs_ready"))
        xT_ready, xT_hi, xT_lo = sem("xT_ready"), sem("xT_hi"), sem("xT_lo")
        proj_ready, qk_act, gate_act, v_copied, v_spread = (sem("proj_ready"), sem("qk_act"), sem("gate_act"),
            sem("v_copied"), sem("v_spread"))
        rope_cos, rope_sin, rotated = sem("rope_cos"), sem("rope_sin"), sem("rotated")
        qk_hi, qk_lo, stacked = sem("qk_hi"), sem("qk_lo"), sem("stacked")
        k_decayed, stack_T, kT_copied, qT_copied, q_decayed = (sem("k_decayed"), sem("stack_T"),
            sem("kT_copied"), sem("qT_copied"), sem("q_decayed"))
        scores_ready, decayed, values_done, oT_ready = (sem("scores_ready"), sem("decayed"),
            sem("values_done"), sem("oT_ready"))
        update_ready, state_old, state_masked, state_new = (sem("update_ready"), sem("state_old"),
            sem("state_masked"), sem("state_new"))
        oT_copied, o_ready, gated, squared, summed = (sem("oT_copied"), sem("o_ready"), sem("gated"),
            sem("squared"), sem("summed"))
        rms_mean, rms_pow, normed = sem("rms_mean"), sem("rms_pow"), sem("normed")
        nT_ready, nT_hi, nT_lo, attn_ready = sem("nT_ready"), sem("nT_hi"), sem("nT_lo"), sem("attn_ready")
        ln2_stats, ln2_mv, ln2_step, attn_normed, x1_ready = (sem("ln2_stats"), sem("ln2_mv"), sem("ln2_step"),
            sem("attn_normed"), sem("x1_ready"))
        ln3_stats, ln3_mv, ln3_step, rows_ready = sem("ln3_stats"), sem("ln3_mv"), sem("ln3_step"), sem("rows_ready")
        rowsT_ready, rowsT_hi, rowsT_lo = sem("rowsT_ready"), sem("rowsT_hi"), sem("rowsT_lo")
        logits_ready, logits_copied, top_step = sem("logits_ready"), sem("logits_copied"), sem("top_step")
        x1_out = [sem(f"x1_out{i}") for i in range(2)]
        rows_out = [sem(f"rows_out{i}") for i in range(2)]
        shared_out = sem("shared_out")
        piece_ready, piece_act, piece_free, act_hi, act_lo = (sem("piece_ready"), sem("piece_act"),
            sem("piece_free"), sem("act_hi"), sem("act_lo"))
        stage_in, stage_max, exp_max, exp_all, exp_scaled, exp_step, stage_ws, stage_hi, stage_lo = (
            sem("stage_in"), sem("stage_max"), sem("exp_max"), sem("exp_all"), sem("exp_scaled"), sem("exp_step"),
            sem("stage_ws"), sem("stage_hi"), sem("stage_lo"))

        route, route_pe, route_act, route_pool = sem("route"), sem("route_pe"), sem("route_act"), sem("route_pool")
        hot_ready, hot_pool, hot_used, owners_ready, ids_ready = (sem("hot_ready"), sem("hot_pool"), sem("hot_used"),
            sem("owners_ready"), sem("ids_ready"))
        index_set = sem("index_set")
        gathered = [sem(f"gathered{i}") for i in range(4)]
        scattered = [sem(f"scattered{i}") for i in range(4)]
        eT_ready, eT_hi, eT_lo, gu_ready, e_silu, e_act = (sem("eT_ready"), sem("eT_hi"), sem("eT_lo"), sem("gu_ready"),
            sem("e_silu"), sem("e_act"))
        aT_ready, ea_hi, ea_lo, res_ready, res_copied = (sem("aT_ready"), sem("ea_hi"), sem("ea_lo"), sem("res_ready"),
            sem("res_copied"))
        c_in = [sem(f"c_in{i}") for i in range(2)]
        c_sum, c_stats, c_mv, c_var, c_rstd, c_shift, c_norm, c_done = (sem("c_sum"), sem("c_stats"), sem("c_mv"),
            sem("c_var"), sem("c_rstd"), sem("c_shift"), sem("c_norm"), sem("c_done"))
        c_out = [sem(f"c_out{i}") for i in range(2)]

        passed = [sem("passed_dve"), sem("passed_pool")]

        wF = sb("wF", [P, 2, 2 * KT * SHARED + SHARED // P * D + KT * EXPERTS], F16)
        rT = sb("rT", [P, 2, 2, KT, 2 * C], F16)
        sg = sb("sg", [P, 2, 2 * C])
        aT = sb("aT", [P, 2, SHARED // P, 2 * C], F16)
        ysh = sb("ysh", [P, D])

        def fb(name, shape, dt=F32):
            return sb(name, shape, dt, first)

        wA = fb("wA", [P, 2, KT, 4 * D], F16)
        wO = fb("wO", [P, 2, KT, D], F16)
        wGU = wF[:, :, 0:2 * KT * SHARED].rearrange("p a (k n) -> p a k n", k=KT)
        wDn = wF[:, :, 2 * KT * SHARED:2 * KT * SHARED + SHARED // P * D].rearrange("p a (k n) -> p a k n", n=D)
        wR = wF[:, :, 2 * KT * SHARED + SHARED // P * D:].rearrange("p a (k n) -> p a k n", n=EXPERTS)
        stage = fb("stage", [P, 1024])
        escale = fb("escale", [P, 8])
        xin = fb("xin", [P, CPS, D])
        xs = fb("xs", [P, D])
        xT = fb("xT", [P, 2, KT, C], F16)
        qk = fb("qk", [P, 2 * D])
        th = fb("th", [P, 2, D])
        vw = fb("vw", [P, HEADS, 2 * HD])
        vn = fb("vn", [P, D])
        rc = fb("rc", [P, 2 * D])
        rs = fb("rs", [P, 2 * D])
        st = fb("st", [P, 2, HEADS, 4, HD], F16)
        kd = fb("kd", [P, D])
        qd = fb("qd", [P, KT, C])
        kT = fb("kT", [P, HEADS // 2, C], F16)
        qT = fb("qT", [P, HEADS // 2, 2, C], F16)
        sd = fb("sd", [P, 2, 4, C])
        state, sold, smask = fb("state", [P, KT, P]), fb("sold", [P, KT, P]), fb("smask", [P, KT, P])
        oT = fb("oT", [P, KT, C])
        y = fb("y", [P, D])
        sq = fb("sq", [P, D])
        nT = fb("nT", [P, 2, KT, C], F16)
        x1 = fb("x1", [P, 2, D])
        rows = fb("rows", [P, 2, D])
        small = fb("small", [P, 96])
        lg = fb("lg", [P, EXPERTS])
        m8 = fb("m8", [P, 8])
        i8 = fb("i8", [P, 8], U32)
        st1, mv1, r1 = small[:, 0:6], small[:, 6:8], small[:, 8:10]
        st2, mv2, r2 = small[:, 10:16], small[:, 16:18], small[:, 18:22]
        st3, mv3, r3 = small[:, 22:28], small[:, 28:30], small[:, 30:32]
        ssum, smean, srms = small[:, 32:48], small[:, 48:64], small[:, 64:80]
        mhalf = k32("mhalf")
        first.close()

        picks = [sb(f"pick{k}", [P, CHUNKS, EXPERTS]) for k in range(TOPK)]
        both = sb("both", [P, CHUNKS * EXPERTS], F16)
        counts = [sb(f"counts{i}", [P, CHUNKS, EXPERTS]) for i in range(3)]
        place_of = sb("place_of", [P, CHUNKS, EXPERTS])
        filled = [sb(f"filled{i}", [P, EXPERTS]) for i in range(4)]
        filled_i = sb("filled_i", [P, EXPERTS], I32)
        spot = sb("spot", [P, TOPK, CHUNKS])
        spot_i, spot_t, spot_r = (sb("spot_i", [P, TOPK, CHUNKS], I32), sb("spot_t", [P, TOPK, CHUNKS], I32),
                                  sb("spot_r", [P, TOPK, CHUNKS], I32))
        tile_f, row_f = sb("tile_f", [P, TOPK, CHUNKS]), sb("row_f", [P, TOPK, CHUNKS])
        prod = sb("prod", [P, CHUNKS, EXPERTS])
        diff = sb("diff", [P, CHUNKS])
        weight = sb("weight", [P, CHUNKS, TOPK])
        cmp = sb("cmp", [P, TILES + 1, EXPERTS - 1])
        owner_f, owner = sb("owner_f", [P, TILES + 1]), sb("owner", [P, TILES + 1], I32)
        hot_r = sb("hot_r", [P, 4, P], F16)
        hot_t = sb("hot_t", [P, 4, 2, TILES + 1], F16)
        ids2, idv, idz = sb("ids2", [P, 2, TILES + 1]), sb("idv", [P, TILES + 1]), sb("idz", [P, TILES + 1])
        gat_i, gat, sca = (sb("gat_i", [P, TILES + 1], I32), sb("gat", [P, TILES + 1], I32), sb("sca", [P, TILES + 1], I32))
        gidx, sidx = sb("gidx", [P, 4], I32), sb("sidx", [P, 4], I32)
        got = [sb(f"got{i}", [P, D]) for i in range(4)]
        eT = sb("eT", [P, 2, 2, KT, C], F16)
        eg = sb("eg", [P, 2, INTER])
        eaT = sb("eaT", [P, 2, 2, INTER // P, C], F16)
        res = [sb(f"res{i}", [P, D]) for i in range(4)]
        cx, cs = sb("cx", [P, 2, 4, D]), sb("cs", [P, 2, 4, D])
        cst, cmv, cr = sb("cst", [P, 4, 6]), sb("cmv", [P, 4, 2]), sb("cr", [P, 4, 3])

        def halves(ap):
            return ap.rearrange("p (h a e) -> p h a e", a=2, e=HD // 2)

        raw = w1s[:, 1:, :, :, :].rearrange("p a b c d -> p (a b c d)").bitcast(F32)
        cp = raw[:, 0:2 * 4 * TOPK * D].rearrange("p (a q k n) -> p a q k n", a=2, q=4, k=TOPK)
        cz = raw[:, 2 * 4 * TOPK * D:2 * 4 * (TOPK + 1) * D].rearrange("p (a q n) -> p a q n", a=2, q=4)
        nA, nO, nF = KT * 4 * D, KT * D, 2 * KT * SHARED + SHARED // P * D + KT * EXPERTS
        rawA, rawO, rawF = raw[:, 0:nA], raw[:, nA:nA + nO], raw[:, nA + nO:nA + nO + nF]
        rawA3 = rawA.rearrange("p (k n) -> p k n", k=KT)
        rawGU = rawF[:, 0:2 * KT * SHARED].rearrange("p (k n) -> p k n", k=KT)
        rawDn = rawF[:, 2 * KT * SHARED:2 * KT * SHARED + SHARED // P * D].rearrange("p (k n) -> p k n", n=D)
        rawR = rawF[:, 2 * KT * SHARED + SHARED // P * D:].rearrange("p (k n) -> p k n", n=EXPERTS)
        rawG1 = raw[:, nA + nO + nF:nA + nO + nF + KT * HD].rearrange("p (k e) -> p k e", e=HD)
        rest = nA + nO + nF + KT * HD
        rawG1T, rawG2, rawNW = raw[0:HD, rest:rest + D], raw[0:HD, rest + D:rest + 2 * D], raw[:, rest + 2 * D:rest + 2 * D + KT]
        row = "(k p) n -> p k n"

        block = whole.enter_context(nc.Block())

        def alone(eng):
            eng.sem_inc(passed[0] if eng.engine == nc.vector.engine else passed[1], 1)

        def at(b, c):
            return b * CPS + c

        def prev(b, c):
            return (b, c - 1) if c else (b - 1, CPS - 1)

        def pieces(b, c, places):
            unit, parity = [(2 * b - 2, 0), (2 * b - 1, 1), (2 * b - 1, 1), (2 * b, 0)][c]
            return unit, parity, ([[0], [1], [2], [3], [4], [5]] if c % 2 else [[6], [7], [], [8], [9], []])[places]

        def run_slots(eng, slot):
            for c in range(CPS):
                slot(0, c, True, True, c >= 1, c == 3)
            with eng.Fori(1, SEQS - 1) as b:
                for c in range(CPS):
                    slot(b, c, True, True, True, True)
            for c in range(CPS):
                slot(SEQS - 1, c, True, c < CPS - 1, True, True)
            for c in range(3):
                slot(SEQS, c, False, False, c == 0, True)

        def run_tiles(eng, slot):
            for j in range(8):
                slot(j, j % 4, j // 4)
            with eng.Fori(2, TILES // 4) as m:
                for i in range(4):
                    slot(m * 4 + i, i, m)
            for j in range(TILES // 4 * 4, TILES + 2):
                slot(j, j % 4, j // 4)

        def has(j, shift):
            return not isinstance(j, int) or 0 <= j + shift < TILES

        @block.sync
        def _(sp):
            def load_x(b, c):
                sp.dma_start(xin[:, c, :], xf[bass.ds(at(b, c) * C, C), :]).then_inc(x_in[c], 16)

            load_x(0, 0)
            for i, w in enumerate((wq, wk, wv)):
                sp.dma_start(rawA3[:, :, i * D:(i + 1) * D], w.rearrange(row, p=P)).then_inc(set_in[0], 16)
            sp.dma_start(rawG1, wg1.rearrange(row, p=P)).then_inc(const_in[2], 16)
            sp.dma_start(rawG2, wg2).then_inc(const_in[2], 16)
            sp.dma_start(c32[:, :], c32d).then_inc(const_in[0], 16)
            sp.dma_start(c16[:, :], c16d).then_inc(const_in[1], 16)
            sp.dma_start(rawO.rearrange("p (k n) -> p k n", k=KT), wo.rearrange(row, p=P)).then_inc(set_in[1], 16)
            with nc.allow_non_contiguous_dma(reason="256 values"):
                sp.dma_start(rawNW, norm_w.rearrange("(k p) -> p k", p=P)).then_inc(set_in[1], 16)
            for c in range(1, CPS):
                load_x(0, c)
            for i, w in enumerate((w_gate, w_up)):
                sp.dma_start(rawGU[:, :, i * SHARED:(i + 1) * SHARED], w.rearrange(row, p=P)).then_inc(set_in[2], 16)
            sp.dma_start(rawDn, w_down.rearrange(row, p=P)).then_inc(set_in[2], 16)
            sp.dma_start(rawR, router.rearrange(row, p=P)).then_inc(set_in[2], 16)

            def load_expert(e, i):
                if i == 0:
                    if not isinstance(e, int) or e:
                        sp.wait_ge(stage_lo, e * 3)
                elif i <= 3:
                    sp.wait_ge(stage_max, e * 3 + i)
                else:
                    sp.wait_ge(stage_lo, e * 3 + (i - 3))
                j = i % 3
                src = w1[bass.ds(e, 1), j * P:(j + 1) * P, :].rearrange("a p n -> p (a n)") if j < KT else \
                    w2[bass.ds(e, 1), :, :].rearrange("a (k p) n -> p (a k) n", p=P)
                dst = stage[:, :] if j < KT else stage[:, :].rearrange("p (k n) -> p k n", n=D)
                sp.dma_start(dst, src).then_inc(stage_in, 16)

            def store_shared(unit, i):
                sp.wait_ge(piece_free, unit * PIECES + 9 + i)
                sp.dma_start(shared_d[bass.ds(unit * 2 * C + i * C, C), :], ysh[:, :]).then_inc(shared_out, 16)

            def slot(b, c, front, nxt, tail, ffn):
                if front:
                    for i in ([0, 1], [2], [3, 4], [5])[c]:
                        load_expert(b, i)
                if tail:
                    tb, tc = prev(b, c)
                    t = at(tb, tc)
                    sp.wait_ge(x1_ready, t + 1)
                    sp.dma_start(res_d[bass.ds(t * C, C), :], x1[:, tc % 2, :]).then_inc(x1_out[tc % 2], 16)
                    if not isinstance(tb, int) or tb < SEQS - 1:
                        load_x(tb + 1, tc)
                if ffn and c % 2 == 0:
                    store_shared(pieces(b, c, 0)[0], 0)
                if tail:
                    sp.wait_ge(rows_ready, t + 1)
                    sp.dma_start(rows_d[bass.ds(t * C, C), :], rows[:, tc % 2, :]).then_inc(rows_out[tc % 2], 16)
                if ffn and c % 2 == 0:
                    store_shared(pieces(b, c, 0)[0], 1)

            run_slots(sp, slot)
            for i in range(2):
                sp.wait_ge(x1_out[i], 16 * CHUNKS // 2)
                sp.wait_ge(rows_out[i], 16 * CHUNKS // 2)
            sp.wait_ge(shared_out, 16 * CHUNKS)

            sp.wait_ge(ids_ready, 1)
            four = "(q p) n -> p q n"

            def load_known(g, par):
                at_g = bass.ds(g * 4 * C, 4 * C)
                sp.dma_start(cx[:, par, :, :], res_d[at_g, :].rearrange(four, p=P)).then_inc(c_in[par], 16)
                sp.dma_start(cs[:, par, :, :], shared_d[at_g, :].rearrange(four, p=P)).then_inc(c_in[par], 16)

            def load_picked(g, par):
                sp.dma_start(cp[:, par, :, :, :].rearrange("p q k n -> p q (k n)"),
                             picked_d[bass.ds(g * 8 * C, 8 * C), :].rearrange("(q p k) n -> p q (k n)", p=P, k=TOPK))\
                    .then_inc(c_in[par], 16)

            for par in range(2):
                load_known(par, par)
            for i in range(4):
                sp.wait_ge(scattered[i], 16 * ((TILES - i + 3) // 4))
            for par in range(2):
                load_picked(par, par)

            def store(g, par, n):
                sp.wait_ge(c_done, 4 * g + 4)
                sp.dma_start(outf[bass.ds(g * 4 * C, 4 * C), :].rearrange(four, p=P), cz[:, par, :, :]).then_inc(c_out[par], 16)

            with sp.Fori(0, SEQS // 2 - 1) as n:
                for par in range(2):
                    store(n * 2 + par, par, n)
                    load_known(n * 2 + par + 2, par)
                    load_picked(n * 2 + par + 2, par)
            for par in range(2):
                store(SEQS - 2 + par, par, SEQS // 2 - 1)
            for par in range(2):
                sp.wait_ge(c_out[par], 16 * SEQS // 2)

        @block.tensor
        def _(pe):
            ident, ident16 = k32("ident"), k16("ident")

            def product(bank, pairs):
                steps = [(left[a], right[b_]) for left, right in pairs for a, b_ in ((0, 0), (0, 1), (1, 0))]
                for i, (left, right) in enumerate(steps):
                    last = nc.tensor.matmul(bank, left, right, start=i == 0, stop=i == len(steps) - 1)
                return last

            pe.wait_ge(const_in[2], 32)
            pe.wait_ge(const_in[0], 16)
            for k in range(KT):
                last = nc.tensor.transpose(A0[0:HD, k * P:(k + 1) * P], rawG1[:, k, :], ident)
            last.then_inc(wg1_T, 1)
            pe.wait_ge(wg1_copied, 1)
            for k in range(KT):
                last = nc.tensor.matmul(A1[:, k * D:(k + 1) * D], rawG1T[:, k * P:(k + 1) * P], rawG2, start=True, stop=True)
            last.then_inc(wg_made, 1)
            pe.wait_ge(const_in[1], 16)
            pe.wait_ge(zeroed, 3)

            def piece(unit, parity, p):
                n = unit * PIECES + p
                bank = FB[p % 2]
                if not (isinstance(n, int) and n < 2):
                    pe.wait_ge(piece_free, n - 1)
                if p < 8:
                    if p == 0:
                        pe.wait_ge(rowsT_lo, unit * 2 + 2)
                        if isinstance(unit, int) and unit == 0:
                            pe.wait_ge(set_lo, 3)
                    for half in range(2):
                        cols = slice(half * SHARED + p * P, half * SHARED + (p + 1) * P)
                        last = product(bank[:, half * 2 * C:(half + 1) * 2 * C],
                                       [([wGU[:, a, k, cols] for a in range(2)], [rT[:, parity, a, k, :] for a in range(2)])
                                        for k in range(KT)])
                else:
                    pe.wait_ge(act_lo, unit * 8 + 8)
                    tok = slice((p - 8) * C, (p - 7) * C)
                    last = product(bank[:, 0:D], [([aT[:, a, j, tok] for a in range(2)], [wDn[:, a, j, :] for a in range(2)])
                                                  for j in range(SHARED // P)])
                last.then_inc(piece_ready, 1)

            def slot(b, c, front, nxt, tail, ffn):
                t = at(b, c)
                tb, tc = prev(b, c)
                tt = at(tb, tc)

                def place(i):
                    if ffn:
                        unit, parity, ps = pieces(b, c, i)
                        for p in ps:
                            piece(unit, parity, p)

                if front:
                    pe.wait_ge(xs_ready, t + 1)
                    if not isinstance(t, int) or t:
                        pe.wait_ge(oT_copied, t)
                    for k in range(KT):
                        last = nc.tensor.transpose(A0[:, k * P:(k + 1) * P], xs[:, k * P:(k + 1) * P], ident)
                    last.then_inc(xT_ready, 1)
                if tail:
                    pe.wait_ge(oT_copied, tt + 1)
                    if not isinstance(tt, int) or tt:
                        pe.wait_ge(logits_copied, tt)
                    for k in range(KT):
                        last = nc.tensor.transpose(A5[:, k * P:(k + 1) * P], oT[:, k, :], ident)
                    last.then_inc(o_ready, 1)
                place(0)
                if front:
                    pe.wait_ge(xT_lo, t + 1)
                    if isinstance(t, int) and t == 0:
                        pe.wait_ge(set_lo, 1)
                    else:
                        pe.wait_ge(decayed, t * 4)
                    for h, bank in enumerate((A1, A2)):
                        last = product(bank[:, :], [([xT[:, a, k, :] for a in range(2)],
                                                     [wA[:, a, k, h * 2 * D:(h + 1) * 2 * D] for a in range(2)]) for k in range(KT)])
                    last.then_inc(proj_ready, 1)
                place(1)
                if tail:
                    pe.wait_ge(normed, tt + 1)
                    for k in range(KT):
                        last = nc.tensor.transpose(A5[:, k * P:(k + 1) * P], y[:, k * P:(k + 1) * P], ident)
                    last.then_inc(nT_ready, 1)
                place(2)
                if front:
                    pe.wait_ge(stacked, 3 * t + 3)
                    pe.wait_ge(v_copied, t + 1)
                    for half, bank in ((0, A1), (1, A2)):
                        b16 = bank[:, :].bitcast(F16)
                        for j in range(HEADS // 2):
                            nc.tensor.transpose(b16[:, j * P:(j + 1) * P],
                                                st[:, half, 2 * j:2 * j + 2, :, :].rearrange("p h a e -> p (h a e)"), ident16)
                    for k in range(KT):
                        last = nc.tensor.transpose(A0[:, k * P:(k + 1) * P], qk[:, k * P:(k + 1) * P], ident)
                    last.then_inc(stack_T, 1)
                if tail:
                    pe.wait_ge(nT_lo, tt + 1)
                    if isinstance(tt, int) and tt == 0:
                        pe.wait_ge(set_lo, 2)
                    product(A5[:, 0:D], [([nT[:, a, k, :] for a in range(2)], [wO[:, a, k, :] for a in range(2)])
                                         for k in range(KT)]).then_inc(attn_ready, 1)
                place(3)
                if front:
                    pe.wait_ge(kT_copied, t + 1)
                    pe.wait_ge(qT_copied, 2 * t + 2)
                    pe.wait_ge(q_decayed, t + 1)
                    pe.wait_ge(v_spread, t + 1)

                    def scores(g):
                        if g >= 2:
                            pe.wait_ge(decayed, 4 * t + g - 1)
                        elif not isinstance(t, int) or t:
                            if g == 0 and c:
                                pe.wait_ge(state_masked, 3 * b + c)
                            elif g == 1:
                                pe.wait_ge(decayed, 4 * t)
                        for j in range(2):
                            m = 2 * g + j
                            last = nc.tensor.matmul((A3, A4)[g % 2][:, j * 2 * C:(j + 1) * 2 * C], kT[:, m, :],
                                                    qT[:, m, :, :].rearrange("p a t -> p (a t)"), start=True, stop=True)
                        last.then_inc(scores_ready, 1)

                    def values(g):
                        k = g // 2
                        pe.wait_ge(decayed, 4 * t + g + 1)
                        if g % 2 == 0 and c:
                            pe.wait_ge(state_new, 3 * b + c)
                            nc.tensor.matmul(A0[:, k * P:(k + 1) * P], state[:, k, :], qd[:, k, :],
                                             start=True, stop=False, skip_group_check=True)
                        for i in range(4):
                            h = 4 * g + i
                            q = 32 * ((h // 2) % 4)
                            last = nc.tensor.matmul(A0[q:q + 32, k * P:(k + 1) * P], vw[:, h, :], sd[:, g % 2, i, :],
                                                    start=(c == 0 and h % 2 == 0), stop=h % 2 == 1,
                                                    skip_group_check=True)
                        last.then_inc(values_done, 1)

                    scores(0)
                    scores(1)
                    place(4)
                    values(0)
                    scores(2)
                    values(1)
                    scores(3)
                    values(2)
                    values(3)
                    if c < CPS - 1:
                        pe.wait_ge(k_decayed, t + 1)
                        pe.wait_ge(v_copied, t + 1)
                        for k in range(KT):
                            last = nc.tensor.matmul(A3[:, k * P:(k + 1) * P], kd[:, k * P:(k + 1) * P],
                                                    vn[:, k * P:(k + 1) * P], start=True, stop=True)
                        last.then_inc(update_ready, 1)
                else:
                    place(4)
                if tail:
                    pe.wait_ge(rows_ready, tt + 1)
                    pe.wait_ge(attn_normed, tt + 1)
                    for k in range(KT):
                        last = nc.tensor.transpose(A5[:, k * P:(k + 1) * P], rows[:, tc % 2, k * P:(k + 1) * P], ident)
                    last.then_inc(rowsT_ready, 1)
                place(5)
                if tail:
                    pe.wait_ge(rowsT_lo, tt + 1)
                    if isinstance(tt, int) and tt == 0:
                        pe.wait_ge(set_lo, 3)
                    par, tok = tc // 2, slice(tc % 2 * C, (tc % 2 + 1) * C)
                    product(A5[:, 0:EXPERTS], [([rT[:, par, a, k, tok] for a in range(2)], [wR[:, a, k, :] for a in range(2)])
                                               for k in range(KT)]).then_inc(logits_ready, 1)

            run_slots(pe, slot)

            pe.wait_ge(route, 3)
            n = CHUNKS * EXPERTS
            nc.tensor.matmul(A0[:, 0:n], k16("before"), both[:, :], start=True, stop=True)
            nc.tensor.matmul(A1[:, 0:n], k16("ones"), both[:, :], start=True, stop=True).then_inc(route_pe, 1)
            for i in range(TOPK * CHUNKS):
                pe.wait_ge(hot_ready, 2 * i + 2)
                pe.wait_ge(hot_pool, i + 1)
                nc.tensor.matmul(A2[:, 0:2 * (TILES + 1)], hot_r[:, i % 4, :], hot_t[:, i % 4, :, :].rearrange("p a t -> p (a t)"),
                                 start=i == 0, stop=i == TOPK * CHUNKS - 1).then_inc(hot_used, 1)

            pe.wait_ge(stage_lo, 3 * EXPERTS)
            pe.wait_ge(owners_ready, 1)
            pe.wait_ge(ids_ready, 1)

            def rows_T(j, i, m):
                pe.wait_ge(gathered[i % 4], 16 * (m + i // 4 + 1))
                if not isinstance(j, int) or j:
                    pe.wait_ge(eT_lo, j)
                for k in range(KT):
                    last = nc.tensor.transpose(A5[:, k * P:(k + 1) * P], got[i % 4][:, k * P:(k + 1) * P], ident)
                last.then_inc(eT_ready, 1)

            rows_T(0, 0, 0)

            def tile_slot(j, i, m):
                if has(j, 0):
                    e = pe.value_load(owner[0:1, bass.ds(j, 1)], min_val=0, max_val=EXPERTS - 1)
                    pe.wait_ge(eT_lo, j + 1)
                    if not isinstance(j, int) or j >= 2:
                        pe.wait_ge(e_act, j - 1)
                    for half in range(2):
                        product((A0, A1, A2, A3)[2 * (i % 2) + half][:, :],
                                [([eT[:, i % 2, a, k, :] for a in range(2)],
                                  [w1s[:, bass.ds(e, 1), a, k, half * INTER:(half + 1) * INTER] for a in range(2)])
                                 for k in range(KT)]).then_inc(gu_ready, 1)
                if has(j, -1):
                    pe.wait_ge(e_act, j)
                    if not isinstance(j, int) or j >= 2:
                        pe.wait_ge(ea_lo, j - 1)
                    for q in range(INTER // P):
                        last = nc.tensor.transpose(A4[:, q * P:(q + 1) * P], eg[:, (i - 1) % 2, q * P:(q + 1) * P], ident)
                    last.then_inc(aT_ready, 1)
                if has(j, 1):
                    rows_T(j + 1, i + 1, m)
                if has(j, -2):
                    e = pe.value_load(owner[0:1, bass.ds(j - 2, 1)], min_val=0, max_val=EXPERTS - 1)
                    pe.wait_ge(ea_lo, j - 1)
                    if isinstance(j, int) and j == 2:
                        pe.wait_ge(piece_free, UNITS * PIECES)
                    if not isinstance(j, int) or j >= 4:
                        pe.wait_ge(res_copied, j - 3)
                    product(FB[i % 2][:, 0:D], [([eaT[:, i % 2, a, q, :] for a in range(2)],
                                                 [w2s[:, bass.ds(e, 1), a, q, :] for a in range(2)])
                                                for q in range(INTER // P)]).then_inc(res_ready, 1)

            run_tiles(pe, tile_slot)

        @block.scalar
        def _(act):
            act.wait_ge(wg1_T, 1)
            nc.scalar.activation(rawG1T, A0[0:HD, 0:D], ACT.Copy).then_inc(wg1_copied, 1)
            act.wait_ge(wg_made, 1)
            nc.scalar.activation(rawA3[:, :, 3 * D:], A1[:, :].rearrange("p (k n) -> p k n", k=KT), ACT.Copy).then_inc(wg_copied, 1)
            for i, (dst, src, col) in enumerate(((wA[:, 0, :, :].rearrange("p k n -> p (k n)"), rawA, S_A),
                                                 (wO[:, 0, :, :].rearrange("p k n -> p (k n)"), rawO, S_O), (wF[:, 0, :], rawF, S_F))):
                act.wait_ge(scale_step, 8)
                nc.scalar.activation(dst, src, ACT.Copy, scale=s(col)).then_inc(set_hi, 1)

            def piece(unit, p):
                if 1 <= p <= 8:
                    act.wait_ge(piece_free, unit * PIECES + p)
                    nc.scalar.activation(aT[:, 0, p - 1, :], sg[:, (p - 1) % 2, :], ACT.Copy).then_inc(act_hi, 1)
                if p < 8:
                    act.wait_ge(piece_ready, unit * PIECES + p + 1)
                    if not (isinstance(unit, int) and unit * 8 + p < 2):
                        act.wait_ge(act_lo, unit * 8 + p - 1)
                    nc.scalar.activation(sg[:, p % 2, :], FB[p % 2][:, 0:2 * C], ACT.Silu, scale=s(C_F)).then_inc(piece_act, 1)

            def slot(b, c, front, nxt, tail, ffn):
                t = at(b, c)
                tb, tc = prev(b, c)
                tt = at(tb, tc)

                def place(i):
                    if ffn:
                        for p in pieces(b, c, i)[2]:
                            piece(pieces(b, c, i)[0], p)

                def expert_hi(j):
                    act.wait_ge(stage_ws, b * 3 + j + 1)
                    dst = w1s[:, bass.ds(b, 1), 0, j, :] if j < KT else \
                        w2s[:, bass.ds(b, 1), 0, :, :].rearrange("p a k n -> p (a k n)")
                    nc.scalar.activation(dst, stage[:, :], ACT.Copy).then_inc(stage_hi, 1)

                if front:
                    act.wait_ge(xT_ready, t + 1)
                    nc.scalar.activation(xT[:, 0, :, :].rearrange("p k t -> p (k t)"), A0[:, 0:D], ACT.Copy).then_inc(xT_hi, 1)
                place(0)
                if tail:
                    act.wait_ge(gated, tt + 1)
                    nc.scalar.activation(sq[:, :], y[:, :], ACT.Square).then_inc(squared, 1)
                if front:
                    act.wait_ge(proj_ready, t + 1)
                    if not isinstance(t, int) or t:
                        act.wait_ge(k_decayed, t)
                    nc.scalar.activation(qk[:, :], A1[:, :], ACT.Silu, scale=s(C_A)).then_inc(qk_act, 1)
                    nc.scalar.activation(th[:, c % 2, :], A2[:, D:], ACT.Tanh, scale=s(C_AH)).then_inc(gate_act, 1)
                    if c == 2:
                        expert_hi(0)
                    if c == 3:
                        expert_hi(2)
                place(1)
                if tail:
                    act.wait_ge(nT_ready, tt + 1)
                    nc.scalar.activation(nT[:, 0, :, :].rearrange("p k t -> p (k t)"), A5[:, 0:D], ACT.Copy).then_inc(nT_hi, 1)
                if front:
                    act.wait_ge(rotated, 2 * t + 2)
                    if not isinstance(t, int) or t:
                        act.wait_ge(stack_T, t)
                    nc.scalar.activation(st[:, :, :, 0, :].rearrange("p a h e -> p (a h) e"),
                                         qk[:, :].rearrange("p (h e) -> p h e", e=HD), ACT.Copy, scale=s(S_Q)).then_inc(qk_hi, 1)
                place(2)
                if front:
                    act.wait_ge(stack_T, t + 1)
                    nc.scalar.activation(kT[:, :, :].rearrange("p j t -> p (j t)"), A2[:, :].bitcast(F16), ACT.Copy).then_inc(kT_copied, 1)
                place(3)
                if tail:
                    act.wait_ge(ln2_step, 4 * tt + 4)
                    if not isinstance(tt, int) or tt >= 2:
                        act.wait_ge(x1_out[tc % 2], 16 * ((tb * CPS + tc - tc % 2) // 2 if isinstance(tb, int) else tb * 2 + tc // 2))
                    nc.scalar.activation(x1[:, tc % 2, :], A5[:, 0:D], ACT.Identity, scale=r2[:, 2:3], bias=r2[:, 3:4])\
                        .then_inc(attn_normed, 1)
                if front and c == 2:
                    expert_hi(1)
                place(4)
                if tail:
                    act.wait_ge(rowsT_ready, tt + 1)
                    nc.scalar.activation(rT[:, tc // 2, 0, :, tc % 2 * C:(tc % 2 + 1) * C],
                                         A5[:, 0:D].rearrange("p (k t) -> p k t", k=KT), ACT.Copy).then_inc(rowsT_hi, 1)
                if front:
                    act.wait_ge(values_done, 4 * t + 4)
                    nc.scalar.activation(oT[:, :, :].rearrange("p k t -> p (k t)"), A0[:, 0:D], ACT.Copy).then_inc(oT_copied, 1)
                place(5)

            run_slots(act, slot)

            act.wait_ge(route, 4)
            nc.scalar.activation(diff[:, :], diff[:, :], ACT.Tanh, scale=0.5).then_inc(route_act, 1)

            act.wait_ge(exp_scaled, EXPERTS)
            act.wait_ge(owners_ready, 1)

            def rows_hi(j, i):
                act.wait_ge(eT_ready, j + 1)
                nc.scalar.activation(eT[:, i % 2, 0, :, :].rearrange("p k t -> p (k t)"), A5[:, 0:D], ACT.Copy).then_inc(eT_hi, 1)

            rows_hi(0, 0)

            def tile_slot(j, i, m):
                if has(j, 0):
                    e = act.value_load(owner[0:1, bass.ds(j, 1)], min_val=0, max_val=EXPERTS - 1)
                    act.wait_ge(gu_ready, 2 * j + 1)
                    nc.scalar.activation(eg[:, i % 2, :], (A0, A2)[i % 2][:, :], ACT.Silu,
                                         scale=exp_scale[:, bass.ds(e, 1), 1:2].rearrange("p a b -> p (a b)")).then_inc(e_silu, 1)
                if has(j, -1):
                    act.wait_ge(aT_ready, j)
                    nc.scalar.activation(eaT[:, (i - 1) % 2, 0, :, :].rearrange("p q t -> p (q t)"), A4[:, :], ACT.Copy).then_inc(ea_hi, 1)
                if has(j, 1):
                    rows_hi(j + 1, i + 1)
                if has(j, -2):
                    e = act.value_load(owner[0:1, bass.ds(j - 2, 1)], min_val=0, max_val=EXPERTS - 1)
                    act.wait_ge(res_ready, j - 1)
                    if not isinstance(j, int) or j >= 6:
                        act.wait_ge(scattered[(i - 2) % 4], 16 * (m + (i - 2) // 4))
                    nc.scalar.activation(res[(i - 2) % 4][:, :], FB[i % 2][:, 0:D], ACT.Copy,
                                         scale=exp_scale[:, bass.ds(e, 1), 3:4].rearrange("p a b -> p (a b)")).then_inc(res_copied, 1)

            run_tiles(act, tile_slot)

            def normalize(g, par):
                act.wait_ge(c_shift, g + 1)
                for q in range(4):
                    nc.scalar.activation(cz[:, par, q, :], cz[:, par, q, :], ACT.Identity, scale=cr[:, q, 1:2],
                                         bias=cr[:, q, 2:3]).then_inc(c_norm, 1)

            with act.Fori(0, SEQS // 2) as n:
                for par in range(2):
                    normalize(n * 2 + par, par)

        @block.vector
        def _(dve):
            dve.wait_ge(const_in[0], 16)
            nc.vector.memset(vw[:, :, :], 0.0).then_inc(zeroed, 1)
            nc.vector.memset(qT[:, :, :, :], 0.0).then_inc(zeroed, 1)
            nc.vector.memset(pmax[:, :], 0.0).then_inc(zeroed, 1)
            dve.wait_ge(zeroed, 3)
            dve.wait_ge(set_in[1], 32)
            for k in range(KT):
                nc.vector.tensor_scalar(rawO[:, k * D:(k + 1) * D], rawO[:, k * D:(k + 1) * D], rawNW[:, k:k + 1], None,
                                        ALU.mult).then_inc(nw_folded, 1)
            dve.wait_ge(nw_folded, 2)
            dve.wait_ge(set_in[0], 48)
            dve.wait_ge(wg_copied, 1)
            dve.wait_ge(set_in[2], 64)
            for i, w in enumerate((rawA, rawO, rawF)):
                nc.vector.tensor_reduce(pmax[:, i:i + 1], w, axis=X, op=ALU.max, apply_absolute_value=True).then_inc(set_max, 1)
            dve.wait_ge(set_all, 1)
            step = [0]

            def chain(ins):
                step[0] += 1
                ins.then_inc(scale_step, 1)
                dve.wait_ge(scale_step, step[0])

            chain(nc.vector.tensor_scalar(gmax[:, 0:3], gmax[:, 0:3], 2.0 ** -30, 2.0 ** 30, ALU.max, ALU.min))
            chain(nc.vector.tensor_scalar(pw[:, 0:3].bitcast(I32), gmax[:, 0:3].bitcast(I32), 0x7F800000, None, ALU.bitwise_and))
            chain(nc.vector.reciprocal(rp[:, 0:3], pw[:, 0:3]))
            chain(nc.vector.tensor_tensor(sc[:, T0_:T0_ + 1], pw[:, 0:1], pw[:, 0:1], ALU.mult))
            chain(nc.vector.tensor_tensor(sc[:, T1_:T1_ + 1], pw[:, 2:3], pw[:, 2:3], ALU.mult))
            for dst, src, f in ((S_A, rp[:, 0:1], 2.0 ** 14), (C_A, pw[:, 0:1], 2.0 ** -24), (C_AH, pw[:, 0:1], 2.0 ** -25),
                                (S_Q, rp[:, 0:1], 2.0 ** 5), (C_S, s(T0_), 2.0 ** -10), (S_O, rp[:, 1:2], 2.0 ** 14),
                                (C_O, pw[:, 1:2], 2.0 ** -26), (S_F, rp[:, 2:3], 2.0 ** 14), (C_F, pw[:, 2:3], 2.0 ** -24),
                                (C_FU, rp[:, 2:3], 2.0 ** -27)):
                last = nc.vector.tensor_scalar(s(dst), src, f, None, ALU.mult)
            chain(last)
            chain(nc.vector.tensor_tensor(s(C_O2), s(C_O), s(C_O), ALU.mult))
            chain(nc.vector.scalar_tensor_tensor(s(C_FD), s(T1_), 2.0 ** -11, pw[:, 2:3], ALU.mult, ALU.mult))
            for i, (dst, hi, src, col) in enumerate((
                    (wA[:, 1, :, :].rearrange("p k n -> p (k n)"), wA[:, 0, :, :].rearrange("p k n -> p (k n)"), rawA, S_A),
                    (wO[:, 1, :, :].rearrange("p k n -> p (k n)"), wO[:, 0, :, :].rearrange("p k n -> p (k n)"), rawO, S_O),
                    (wF[:, 1, :], wF[:, 0, :], rawF, S_F))):
                dve.wait_ge(set_hi, i + 1)
                nc.vector.scalar_tensor_tensor(dst, src, s(col), hi, ALU.mult, ALU.subtract).then_inc(set_lo, 1)

            def ln1(b, c):
                t = at(b, c)
                dve.wait_ge(x_in[c], (b + 1) * 16)
                nc.vector.bn_stats(st1, xin[:, c, :]).then_inc(ln1_stats, 1)
                dve.wait_ge(ln1_stats, t + 1)
                if not isinstance(t, int) or t:
                    dve.wait_ge(xs_ready, t)
                alone(dve)
                nc.vector.bn_aggr(mv1, st1).then_inc(ln1_mv, 1)

            def lo(unit, p):
                dve.wait_ge(act_hi, unit * 8 + p + 1)
                nc.vector.tensor_tensor(aT[:, 1, p, :], sg[:, p % 2, :], aT[:, 0, p, :], ALU.subtract).then_inc(act_lo, 1)

            def piece(unit, p):
                if 1 <= p <= 8:
                    lo(unit, p - 1)
                if p < 8:
                    dve.wait_ge(piece_act, unit * 8 + p + 1)
                    nc.vector.scalar_tensor_tensor(sg[:, p % 2, :], FB[p % 2][:, 2 * C:], s(C_FU), sg[:, p % 2, :],
                                                   ALU.mult, ALU.mult).then_inc(piece_free, 1)
                else:
                    dve.wait_ge(piece_ready, unit * PIECES + p + 1)
                    if not (isinstance(unit, int) and unit == 0 and p == 8):
                        dve.wait_ge(shared_out, (unit * 2 + p - 8) * 16)
                    nc.vector.tensor_scalar(ysh[:, :], FB[p % 2][:, 0:D], s(C_FD), None, ALU.mult).then_inc(piece_free, 1)

            ln1(0, 0)

            def slot(b, c, front, nxt, tail, ffn):
                t = at(b, c)
                tb, tc = prev(b, c)
                tt = at(tb, tc)

                def place(i):
                    if ffn:
                        for p in pieces(b, c, i)[2]:
                            piece(pieces(b, c, i)[0], p)

                def expert_max(j):
                    dve.wait_ge(stage_in, (b * 6 + j + 1) * 16)
                    nc.vector.tensor_reduce(escale[:, 4 + j:5 + j], stage[:, :], axis=X, op=ALU.max,
                                            apply_absolute_value=True).then_inc(stage_max, 1)

                if front:
                    dve.wait_ge(xT_hi, t + 1)
                    nc.vector.tensor_tensor(xT[:, 1, :, :].rearrange("p k t -> p (k t)"), A0[:, 0:D],
                                            xT[:, 0, :, :].rearrange("p k t -> p (k t)"), ALU.subtract).then_inc(xT_lo, 1)
                if tail:
                    dve.wait_ge(o_ready, tt + 1)
                    dve.wait_ge(gate_act, tt + 1)
                    nc.vector.scalar_tensor_tensor(y[:, :], th[:, tc % 2, :], 1.0, A5[:, 0:D], ALU.add, ALU.mult).then_inc(gated, 1)
                place(0)
                if tail:
                    dve.wait_ge(squared, tt + 1)
                    nc.vector.tensor_reduce(ssum, sq[:, :].rearrange("p (h e) -> p h e", e=HD), axis=X, op=ALU.add).then_inc(summed, 1)
                if front:
                    dve.wait_ge(gate_act, t + 1)
                    nc.vector.tensor_scalar(vn[:, :], A2[:, 0:D], s(C_A), None, ALU.mult).then_inc(v_copied, 1)
                    a, r, o4 = halves(qk[:, :]), halves(rs[:, :]), halves(rc[:, :])
                    sin = k32("sin")[:, c * 8:(c + 1) * 8].unsqueeze(1).broadcast_to((P, 2 * HEADS, HD // 2))
                    nc.vector.tensor_tensor(r[:, :, 0, :], a[:, :, 1, :], sin, ALU.mult).then_inc(rope_sin, 1)
                    nc.vector.tensor_tensor(r[:, :, 1, :], a[:, :, 0, :], sin, ALU.mult).then_inc(rope_sin, 1)
                    dve.wait_ge(v_copied, t + 1)
                    nc.vector.tensor_copy(
                        vw[:, :, :].rearrange("p (j a) (b e) -> p j (a b) e", a=2, b=2)[:, :, 0:4:3, :],
                        vn[:, :].rearrange("p (j a e) -> p j a e", a=2, e=HD)).then_inc(v_spread, 1)
                    if c <= 1:
                        expert_max(2 * c)
                    dve.wait_ge(rope_cos, t + 1)
                    dve.wait_ge(rope_sin, 2 * t + 2)
                    nc.vector.tensor_tensor(a[:, :, 0, :], o4[:, :, 0, :], r[:, :, 0, :], ALU.subtract).then_inc(rotated, 1)
                    nc.vector.tensor_tensor(a[:, :, 1, :], o4[:, :, 1, :], r[:, :, 1, :], ALU.add).then_inc(rotated, 1)
                place(1)
                if tail:
                    dve.wait_ge(nT_hi, tt + 1)
                    nc.vector.tensor_tensor(nT[:, 1, :, :].rearrange("p k t -> p (k t)"), A5[:, 0:D],
                                            nT[:, 0, :, :].rearrange("p k t -> p (k t)"), ALU.subtract).then_inc(nT_lo, 1)
                if front:
                    dve.wait_ge(qk_hi, t + 1)
                    flat = st[:, :, :, :, :].rearrange("p a h i e -> p (a h) i e")
                    nc.vector.scalar_tensor_tensor(flat[:, :, 1, :], qk[:, :].rearrange("p (h e) -> p h e", e=HD), s(S_Q),
                                                   flat[:, :, 0, :], ALU.mult, ALU.subtract).then_inc(qk_lo, 1)
                    nc.vector.tensor_copy(st[:, 0, :, 3, :], st[:, 0, :, 0, :]).then_inc(stacked, 1)
                    dve.wait_ge(qk_lo, t + 1)
                    nc.vector.tensor_copy(st[:, 0, :, 2, :], st[:, 0, :, 1, :]).then_inc(stacked, 1)
                    nc.vector.tensor_copy(st[:, 1, :, 2:4, :], st[:, 1, :, 0:2, :]).then_inc(stacked, 1)
                place(2)
                if nxt:
                    ln1(*((b, c + 1) if c < CPS - 1 else (b + 1, 0)))
                if front:
                    dve.wait_ge(stack_T, t + 1)
                    b16 = A1[:, :].bitcast(F16).rearrange("p (j t) -> p j t", t=C)
                    nc.vector.tensor_copy(qT[0:64, :, 0, :], b16[0:64, :, :]).then_inc(qT_copied, 1)
                    nc.vector.tensor_copy(qT[64:128, :, 1, :], b16[64:128, :, :]).then_inc(qT_copied, 1)
                    nc.vector.tensor_tensor(qd[:, :, :].rearrange("p k t -> p (k t)"), A0[:, 0:D], k32("qdec"), ALU.mult)\
                        .then_inc(q_decayed, 1)
                if tail:
                    dve.wait_ge(attn_ready, tt + 1)
                    nc.vector.bn_stats(st2, A5[:, 0:D]).then_inc(ln2_stats, 1)
                    dve.wait_ge(ln2_stats, tt + 1)
                    alone(dve)
                    nc.vector.bn_aggr(mv2, st2).then_inc(ln2_mv, 1)
                place(3)

                def decay(g):
                    dve.wait_ge(scores_ready, 4 * t + g + 1)
                    if g >= 2 or not isinstance(t, int) or t:
                        dve.wait_ge(values_done, 4 * t + g - 1)
                    nc.vector.scalar_tensor_tensor(sd[:, g % 2, :, :].rearrange("p h t -> p (h t)"), (A3, A4)[g % 2][:, :], s(C_S),
                                                   k32("decay")[:, 4 * g * C:4 * (g + 1) * C], ALU.mult, ALU.mult).then_inc(decayed, 1)

                if front:
                    decay(0)
                    decay(1)
                    if c == 0:
                        expert_max(1)
                place(4)
                if front:
                    decay(2)
                    decay(3)
                if tail:
                    dve.wait_ge(x1_ready, tt + 1)
                    nc.vector.bn_stats(st3, x1[:, tc % 2, :]).then_inc(ln3_stats, 1)
                    dve.wait_ge(ln3_stats, tt + 1)
                    alone(dve)
                    nc.vector.bn_aggr(mv3, st3).then_inc(ln3_mv, 1)
                if front and c == 1:
                    dve.wait_ge(stage_max, b * 3 + 3)
                    nc.vector.tensor_reduce(escale[:, 7:8], escale[:, 4:7], axis=X, op=ALU.max).then_inc(exp_max, 1)
                if front and c < CPS - 1:
                    dve.wait_ge(update_ready, 3 * b + c + 1)
                    flat = [x_[:, :, :].rearrange("p k t -> p (k t)") for x_ in (state, sold, smask)]
                    if c == 0:
                        nc.vector.tensor_tensor(flat[0], A3[:, 0:D], k32("block"), ALU.mult).then_inc(state_masked, 1)
                        dve.wait_ge(state_masked, 3 * b + 1)
                        dve.sem_inc(state_new, 1)
                    else:
                        nc.vector.tensor_tensor(flat[2], A3[:, 0:D], k32("block"), ALU.mult).then_inc(state_masked, 1)
                        dve.wait_ge(state_masked, 3 * b + c + 1)
                        dve.wait_ge(state_old, 2 * b + c)
                        nc.vector.tensor_tensor(flat[0], flat[1], flat[2], ALU.add).then_inc(state_new, 1)
                if front and c == 1:
                    e = escale
                    n0 = b * 5
                    dve.wait_ge(exp_all, b + 1)

                    def link(i, ins):
                        ins.then_inc(exp_step, 1)
                        dve.wait_ge(exp_step, n0 + i)

                    link(1, nc.vector.tensor_scalar(e[:, 4:5], e[:, 4:5], 2.0 ** -30, 2.0 ** 30, ALU.max, ALU.min))
                    link(2, nc.vector.tensor_scalar(e[:, 5:6].bitcast(I32), e[:, 4:5].bitcast(I32), 0x7F800000, None, ALU.bitwise_and))
                    link(3, nc.vector.reciprocal(e[:, 6:7], e[:, 5:6]))
                    nc.vector.tensor_scalar(e[:, 0:1], e[:, 6:7], 2.0 ** 14, None, ALU.mult)
                    nc.vector.tensor_scalar(e[:, 1:2], e[:, 5:6], 2.0 ** -24, None, ALU.mult)
                    nc.vector.tensor_scalar(e[:, 2:3], e[:, 6:7], 2.0 ** -27, None, ALU.mult)
                    link(4, nc.vector.tensor_tensor(e[:, 3:4], e[:, 5:6], e[:, 5:6], ALU.mult))
                    link(5, nc.vector.scalar_tensor_tensor(e[:, 3:4], e[:, 3:4], 2.0 ** -11, e[:, 5:6], ALU.mult, ALU.mult))
                    nc.vector.tensor_copy(exp_scale[:, bass.ds(b, 1), :], e[:, 0:4].unsqueeze(1)).then_inc(exp_scaled, 1)
                if tail:
                    dve.wait_ge(rowsT_hi, tt + 1)
                    tok = slice(tc % 2 * C, (tc % 2 + 1) * C)
                    nc.vector.tensor_tensor(rT[:, tc // 2, 1, :, tok], A5[:, 0:D].rearrange("p (k t) -> p k t", k=KT),
                                            rT[:, tc // 2, 0, :, tok], ALU.subtract).then_inc(rowsT_lo, 1)
                place(5)
                if tail:
                    dve.wait_ge(logits_ready, tt + 1)
                    nc.vector.tensor_scalar(lg[:, :], A5[:, 0:EXPERTS], s(C_F), None, ALU.mult).then_inc(logits_copied, 1)
                    dve.wait_ge(logits_copied, tt + 1)
                    alone(dve)
                    nc.vector.max(m8[:, :], lg[:, :]).then_inc(top_step, 1)
                    dve.wait_ge(top_step, 3 * tt + 1)
                    alone(dve)
                    nc.vector.max_index(i8[:, :], m8[:, :], lg[:, :]).then_inc(top_step, 1)
                    nc.vector.tensor_copy(top_v[:, bass.ds(tt, 1), :], m8[:, 0:TOPK].unsqueeze(1))
                    dve.wait_ge(top_step, 3 * tt + 2)
                    nc.vector.tensor_copy(top_i[:, bass.ds(tt, 1), :], i8[:, 0:TOPK].unsqueeze(1)).then_inc(top_step, 1)

            run_slots(dve, slot)

            pool_width = TILES + 1
            done = [0]

            def then(ins, after=True):
                done[0] += 1
                ins.then_inc(route, 1)
                if after:
                    dve.wait_ge(route, done[0])

            dve.wait_ge(top_step, 3 * CHUNKS)
            for k in range(TOPK):
                then(nc.vector.tensor_tensor(picks[k][:, :, :], k32("iota8").unsqueeze(1).broadcast_to((P, CHUNKS, EXPERTS)),
                                             top_i[:, :, k].unsqueeze(2).broadcast_to((P, CHUNKS, EXPERTS)), ALU.is_equal))
            then(nc.vector.tensor_tensor(both[:, :].rearrange("p (c e) -> p c e", e=EXPERTS), picks[0][:, :, :], picks[1][:, :, :],
                                         ALU.add))
            then(nc.vector.tensor_tensor(diff[:, :], top_v[:, :, 0], top_v[:, :, 1], ALU.subtract))
            dve.wait_ge(route_act, 1)
            then(nc.vector.tensor_scalar(weight[:, :, 0], diff[:, :], 0.5, 0.5, ALU.mult, ALU.add))
            then(nc.vector.tensor_scalar(weight[:, :, 1], diff[:, :], -0.5, 0.5, ALU.mult, ALU.add))
            dve.wait_ge(route_pe, 1)
            total, a, b_ = counts
            psum3 = [bank[:, 0:CHUNKS * EXPERTS].rearrange("p (c e) -> p c e", e=EXPERTS) for bank in (A0, A1)]
            then(nc.vector.tensor_copy(total[:, :, :], psum3[1]))

            def running(src, bufs, n):
                step = 1
                k = 0
                while step < n:
                    dst = bufs[k % 2]
                    then(nc.vector.tensor_copy(dst[:, 0:step], src[:, 0:step]))
                    then(nc.vector.tensor_tensor(dst[:, step:n], src[:, step:n], src[:, 0:n - step], ALU.add))
                    src, step, k = dst, step * 2, k + 1
                return src

            summed_c = running(total, (a, b_), CHUNKS)
            spare = a if summed_c is b_ else b_
            count = summed_c[:, CHUNKS - 1, :]
            then(nc.vector.tensor_scalar(filled_i[:, :], count, float(P - 1), None, ALU.add))
            then(nc.vector.tensor_scalar(filled_i[:, :], filled_i[:, :], 7, None, ALU.logical_shift_right))
            then(nc.vector.tensor_copy(filled[0][:, :], filled_i[:, :]))
            until = running(filled[0], (filled[1], filled[2]), EXPERTS)
            then(nc.vector.tensor_tensor(filled[3][:, :], until[:, :], filled[0][:, :], ALU.subtract))
            then(nc.vector.tensor_scalar(filled[3][:, :], filled[3][:, :], float(P), None, ALU.mult))
            then(nc.vector.tensor_tensor(place_of[:, :, :], summed_c[:, :, :], total[:, :, :], ALU.subtract))
            then(nc.vector.tensor_tensor(spare[:, :, :], place_of[:, :, :], psum3[0], ALU.add))
            then(nc.vector.tensor_tensor(place_of[:, :, :], spare[:, :, :], filled[3][:, :].unsqueeze(1).broadcast_to((P, CHUNKS, EXPERTS)),
                                         ALU.add))
            for k in range(TOPK):
                then(nc.vector.tensor_tensor(prod[:, :, :], picks[k][:, :, :], place_of[:, :, :], ALU.mult))
                then(nc.vector.tensor_reduce(spot[:, k, :], prod[:, :, :], axis=X, op=ALU.add))
            then(nc.vector.tensor_copy(spot_i[:, :, :], spot[:, :, :]))
            then(nc.vector.tensor_scalar(spot_t[:, :, :], spot_i[:, :, :], 7, None, ALU.logical_shift_right))
            then(nc.vector.tensor_scalar(spot_r[:, :, :], spot_i[:, :, :], P - 1, None, ALU.bitwise_and))
            then(nc.vector.tensor_copy(tile_f[:, :, :], spot_t[:, :, :]))
            then(nc.vector.tensor_copy(row_f[:, :, :], spot_r[:, :, :]))
            dve.sem_inc(route_pool, 1)
            for i in range(TOPK * CHUNKS):
                k, c = i % TOPK, i // TOPK
                if i >= 4:
                    dve.wait_ge(hot_used, i - 3)
                nc.vector.tensor_scalar(hot_r[:, i % 4, :], k16("iota"), row_f[:, k, c:c + 1], None, ALU.is_equal).then_inc(hot_ready, 1)
                nc.vector.tensor_scalar(hot_t[:, i % 4, 0, :], k32("iotat"), tile_f[:, k, c:c + 1], k32("tok")[:, k:k + 1],
                                        ALU.is_equal, ALU.mult).then_inc(hot_ready, 1)
            then(nc.vector.tensor_tensor(cmp[:, :, :], k32("iotat").unsqueeze(2).broadcast_to((P, pool_width, EXPERTS - 1)),
                                         until[:, 0:EXPERTS - 1].unsqueeze(1).broadcast_to((P, pool_width, EXPERTS - 1)), ALU.is_ge))
            then(nc.vector.tensor_reduce(owner_f[:, :], cmp[:, :, :], axis=X, op=ALU.add))
            nc.vector.tensor_copy(owner[:, :], owner_f[:, :]).then_inc(owners_ready, 1)
            dve.wait_ge(hot_used, TOPK * CHUNKS)
            then(nc.vector.tensor_copy(ids2[:, :, :].rearrange("p a t -> p (a t)"), A2[:, 0:2 * pool_width]))
            then(nc.vector.tensor_tensor(idv[:, :], ids2[:, 0, :], ids2[:, 1, :], ALU.add))
            then(nc.vector.tensor_scalar(idz[:, :], idv[:, :], 0.0, float(FAR), ALU.is_equal, ALU.mult))
            then(nc.vector.scalar_tensor_tensor(sca[:, :], idv[:, :], -1.0, idz[:, :], ALU.add, ALU.add))
            then(nc.vector.tensor_scalar(gat_i[:, :], idv[:, :], -1.0, 0.0, ALU.add, ALU.max))
            nc.vector.tensor_scalar(gat[:, :], gat_i[:, :], 1, None, ALU.logical_shift_right).then_inc(ids_ready, 1)

            dve.wait_ge(owners_ready, 1)

            def rows_lo(j, i):
                dve.wait_ge(eT_hi, j + 1)
                nc.vector.tensor_tensor(eT[:, i % 2, 1, :, :].rearrange("p k t -> p (k t)"), A5[:, 0:D],
                                        eT[:, i % 2, 0, :, :].rearrange("p k t -> p (k t)"), ALU.subtract).then_inc(eT_lo, 1)

            rows_lo(0, 0)

            def tile_slot(j, i, m):
                if has(j, 0):
                    e = dve.value_load(owner[0:1, bass.ds(j, 1)], min_val=0, max_val=EXPERTS - 1)
                    dve.wait_ge(gu_ready, 2 * j + 2)
                    dve.wait_ge(e_silu, j + 1)
                    nc.vector.scalar_tensor_tensor(eg[:, i % 2, :], (A1, A3)[i % 2][:, :],
                                                   exp_scale[:, bass.ds(e, 1), 2:3].rearrange("p a b -> p (a b)"), eg[:, i % 2, :],
                                                   ALU.mult, ALU.mult).then_inc(e_act, 1)
                if has(j, -1):
                    dve.wait_ge(ea_hi, j)
                    nc.vector.tensor_tensor(eaT[:, (i - 1) % 2, 1, :, :].rearrange("p q t -> p (q t)"), A4[:, :],
                                            eaT[:, (i - 1) % 2, 0, :, :].rearrange("p q t -> p (q t)"), ALU.subtract).then_inc(ea_lo, 1)
                if has(j, 1):
                    rows_lo(j + 1, i + 1)

            run_tiles(dve, tile_slot)

            def combine(g, par, n):
                dve.wait_ge(c_in[par], (n + 1) * 48)
                for q in range(4):
                    for k in range(TOPK):
                        z_in = cs[:, par, q, :] if k == 0 else cz[:, par, q, :]
                        nc.vector.scalar_tensor_tensor(cz[:, par, q, :], cp[:, par, q, k, :],
                                                       weight[:, bass.ds(g * 4 + q, 1), k:k + 1].rearrange("p a b -> p (a b)"), z_in,
                                                       ALU.mult, ALU.add).then_inc(c_sum, 1)
                        dve.wait_ge(c_sum, g * 8 + 2 * q + k + 1)
                    nc.vector.bn_stats(cst[:, q, :], cz[:, par, q, :]).then_inc(c_stats, 1)
                for q in range(4):
                    dve.wait_ge(c_stats, g * 4 + q + 1)
                    alone(dve)
                    nc.vector.bn_aggr(cmv[:, q, :], cst[:, q, :]).then_inc(c_mv, 1)
                dve.wait_ge(c_rstd, g + 1)
                nc.vector.scalar_tensor_tensor(cr[:, :, 2], cmv[:, :, 0], -1.0, cr[:, :, 1], ALU.mult, ALU.mult).then_inc(c_shift, 1)

            with dve.Fori(0, SEQS // 2) as n:
                for par in range(2):
                    combine(n * 2 + par, par, n)

        @block.gpsimd
        def _(pool):
            pool.wait_ge(set_max, 3)
            alone(pool)
            nc.gpsimd.partition_all_reduce(gmax[:, 0:3], pmax[:, 0:3], P, ABSMAX).then_inc(set_all, 1)

            def ln1(b, c):
                t = at(b, c)
                pool.wait_ge(ln1_mv, t + 1)
                alone(pool)
                nc.gpsimd.tensor_scalar(r1[:, 0:1], mv1[:, 1:2], LN_EPS, XS ** -2, ALU.add, ALU.mult).then_inc(ln1_var, 1)
                pool.wait_ge(ln1_var, t + 1)
                nc.gpsimd.tensor_tensor(r1[:, 1:2], r1[:, 0:1], mhalf[:, 0:1], ALU.pow).then_inc(ln1_pow, 1)
                pool.wait_ge(ln1_pow, t + 1)
                if not isinstance(t, int) or t:
                    pool.wait_ge(xT_ready, t)
                alone(pool)
                nc.gpsimd.tensor_scalar(xs[:, :], xin[:, c, :], mv1[:, 0:1], r1[:, 1:2], ALU.subtract, ALU.mult).then_inc(xs_ready, 1)

            ln1(0, 0)

            def slot(b, c, front, nxt, tail, ffn):
                t = at(b, c)
                tb, tc = prev(b, c)
                tt = at(tb, tc)

                def expert_scale(j):
                    pool.wait_ge(stage_in, (b * 6 + 3 + j + 1) * 16)
                    if j == 0:
                        pool.wait_ge(exp_scaled, b + 1)
                    alone(pool)
                    nc.gpsimd.tensor_scalar(stage[:, :], stage[:, :], escale[:, 0:1], None, ALU.mult).then_inc(stage_ws, 1)

                def expert_lo(j):
                    pool.wait_ge(stage_hi, b * 3 + j + 1)
                    pool.wait_ge(stage_ws, b * 3 + j + 1)
                    at_e = bass.ds(b, 1)
                    pick = (lambda a: w1s[:, at_e, a, j, :]) if j < KT else \
                        (lambda a: w2s[:, at_e, a, :, :].rearrange("p a k n -> p (a k n)"))
                    nc.gpsimd.tensor_tensor(pick(1), stage[:, :] if j == KT else stage[:, :].unsqueeze(1), pick(0),
                                            ALU.subtract).then_inc(stage_lo, 1)

                if front and c == 2:
                    expert_scale(0)
                if front and c == 3:
                    expert_scale(2)
                if tail:
                    pool.wait_ge(summed, tt + 1)
                    alone(pool)
                    nc.gpsimd.tensor_scalar(smean, ssum, 1.0 / (4 * HD) * (NS / 2) ** -2, RMS_EPS * (NS / 2) ** -2, ALU.mult, ALU.add)\
                        .then_inc(rms_mean, 1)
                    pool.wait_ge(rms_mean, tt + 1)
                    nc.gpsimd.tensor_tensor(srms, smean, mhalf, ALU.pow).then_inc(rms_pow, 1)
                if front:
                    pool.wait_ge(qk_act, t + 1)
                    cos = k32("cos")[:, c * 8:(c + 1) * 8].unsqueeze(1).broadcast_to((P, 4 * HEADS, HD // 2))
                    nc.gpsimd.tensor_tensor(rc[:, :].rearrange("p (h e) -> p h e", e=HD // 2),
                                            qk[:, :].rearrange("p (h e) -> p h e", e=HD // 2), cos, ALU.mult).then_inc(rope_cos, 1)
                if tail:
                    pool.wait_ge(rms_pow, tt + 1)
                    y3 = y[:, :].rearrange("p (h e) -> p h e", e=HD)
                    nc.gpsimd.tensor_tensor(y3, y3, srms.unsqueeze(2).broadcast_to((P, HEADS, HD)), ALU.mult).then_inc(normed, 1)
                if front and c == 2:
                    expert_lo(0)
                if front and c == 3:
                    expert_lo(2)
                if front:
                    pool.wait_ge(rotated, 2 * t + 2)
                    nc.gpsimd.tensor_tensor(kd[:, :].rearrange("p (h e) -> p h e", e=HD), qk[:, D:].rearrange("p (h e) -> p h e", e=HD),
                                            k32("kdec").unsqueeze(2).broadcast_to((P, HEADS, HD)), ALU.mult).then_inc(k_decayed, 1)
                if front and c == 2:
                    expert_scale(1)
                if nxt:
                    ln1(*((b, c + 1) if c < CPS - 1 else (b + 1, 0)))
                if front and 1 <= c < CPS - 1:
                    pool.wait_ge(state_new, 3 * b + c)
                    nc.gpsimd.tensor_tensor(sold[:, :, :].rearrange("p k t -> p (k t)"), state[:, :, :].rearrange("p k t -> p (k t)"),
                                            k32("blocklam"), ALU.mult).then_inc(state_old, 1)
                if tail:
                    n0 = 4 * tt
                    pool.wait_ge(ln2_mv, tt + 1)
                    alone(pool)
                    nc.gpsimd.tensor_scalar(r2[:, 0:1], mv2[:, 1:2], s(C_O2), LN_EPS, ALU.mult, ALU.add).then_inc(ln2_step, 1)
                    pool.wait_ge(ln2_step, n0 + 1)
                    nc.gpsimd.tensor_tensor(r2[:, 1:2], r2[:, 0:1], mhalf[:, 0:1], ALU.pow).then_inc(ln2_step, 1)
                    pool.wait_ge(ln2_step, n0 + 2)
                    alone(pool)
                    nc.gpsimd.tensor_scalar(r2[:, 2:3], r2[:, 1:2], s(C_O), None, ALU.mult).then_inc(ln2_step, 1)
                    pool.wait_ge(ln2_step, n0 + 3)
                    alone(pool)
                    nc.gpsimd.tensor_scalar(r2[:, 3:4], mv2[:, 0:1], r2[:, 2:3], -1.0, ALU.mult, ALU.mult).then_inc(ln2_step, 1)
                    pool.wait_ge(attn_normed, tt + 1)
                    nc.gpsimd.tensor_tensor(x1[:, tc % 2, :], x1[:, tc % 2, :], xin[:, tc, :], ALU.add).then_inc(x1_ready, 1)
                if front and c == 2:
                    expert_lo(1)
                if tail:
                    pool.wait_ge(ln3_mv, tt + 1)
                    alone(pool)
                    nc.gpsimd.tensor_scalar(r3[:, 0:1], mv3[:, 1:2], LN_EPS, XS ** -2, ALU.add, ALU.mult).then_inc(ln3_step, 1)
                    pool.wait_ge(ln3_step, 2 * tt + 1)
                    nc.gpsimd.tensor_tensor(r3[:, 1:2], r3[:, 0:1], mhalf[:, 0:1], ALU.pow).then_inc(ln3_step, 1)
                    pool.wait_ge(ln3_step, 2 * tt + 2)
                    if not isinstance(tt, int) or tt >= 2:
                        pool.wait_ge(rows_out[tc % 2], 16 * ((tb * CPS + tc - tc % 2) // 2 if isinstance(tb, int) else tb * 2 + tc // 2))
                    alone(pool)
                    nc.gpsimd.tensor_scalar(rows[:, tc % 2, :], x1[:, tc % 2, :], mv3[:, 0:1], r3[:, 1:2],
                                            ALU.subtract, ALU.mult).then_inc(rows_ready, 1)
                if front and c == 1:
                    pool.wait_ge(exp_max, b + 1)
                    alone(pool)
                    nc.gpsimd.partition_all_reduce(escale[:, 4:5], escale[:, 7:8], P, ABSMAX).then_inc(exp_all, 1)

            run_slots(pool, slot)

            pool.wait_ge(route_pool, 1)
            for i in range(TOPK * CHUNKS):
                k, c = i % TOPK, i // TOPK
                if i >= 4:
                    pool.wait_ge(hot_used, i - 3)
                alone(pool)
                nc.gpsimd.tensor_scalar(hot_t[:, i % 4, 1, :], k32("iotat"), tile_f[:, k, c:c + 1], float(TOPK * C * c),
                                        ALU.is_equal, ALU.mult).then_inc(hot_pool, 1)
            pool.wait_ge(ids_ready, 1)
            for i in range(2):
                pool.wait_ge(rows_out[i], 16 * CHUNKS // 2)

            def gather(j, i, m):
                if not isinstance(j, int) or j >= 4:
                    pool.wait_ge(eT_ready, j - 3)
                    pool.wait_ge(gathered[i % 4], 16 * (m + i // 4))
                alone(pool)
                nc.gpsimd.tensor_copy(gidx[:, i % 4:i % 4 + 1], gat[:, bass.ds(j, 1)]).then_inc(index_set, 1)
                return i % 4

            def gather_start(i):
                nc.gpsimd.indirect_dma_start(out=got[i][:, :], out_offset=None, in_=rows_d[:, :],
                                             in_offset=bass.IndirectOffsetOnAxis(ap=gidx[:, i:i + 1], axis=0)).then_inc(gathered[i], 16)

            for j in range(3):
                i = gather(j, j, 0)
                pool.wait_ge(index_set, j + 1)
                alone(pool)
                gather_start(i)

            def tile_slot(j, i, m):
                base = 3 + (min(j, TILES - 3) + max(j - 3, 0) if isinstance(j, int) else j + j - 3)
                if has(j, 3):
                    gi = gather(j + 3, i + 3, m)
                    base = base + 1
                    pool.wait_ge(index_set, base)
                    alone(pool)
                    gather_start(gi)
                if has(j, -3):
                    pool.wait_ge(res_copied, j - 2)
                    alone(pool)
                    nc.gpsimd.tensor_copy(sidx[:, (i - 3) % 4:(i - 3) % 4 + 1], sca[:, bass.ds(j - 3, 1)]).then_inc(index_set, 1)
                    base = base + 1
                    pool.wait_ge(index_set, base)
                    alone(pool)
                    nc.gpsimd.indirect_dma_start(out=picked_d[:, :], in_=res[(i - 3) % 4][:, :], in_offset=None,
                                                 out_offset=bass.IndirectOffsetOnAxis(ap=sidx[:, (i - 3) % 4:(i - 3) % 4 + 1], axis=0),
                                                 bounds_check=TOKENS * TOPK - 1, oob_is_err=False).then_inc(scattered[(i - 3) % 4], 16)

            run_tiles(pool, tile_slot)
            tile_slot(TILES + 2, (TILES + 2) % 4, 0)

            def residual(g, par):
                pool.wait_ge(c_mv, g * 4 + 4)
                alone(pool)
                nc.gpsimd.tensor_scalar(cr[:, :, 0], cmv[:, :, 1], LN_EPS, None, ALU.add).then_inc(c_var, 1)
                pool.wait_ge(c_var, g + 1)
                nc.gpsimd.tensor_tensor(cr[:, :, 1], cr[:, :, 0], mhalf[:, 0:4], ALU.pow).then_inc(c_rstd, 1)
                for q in range(4):
                    pool.wait_ge(c_norm, g * 4 + q + 1)
                    nc.gpsimd.tensor_tensor(cz[:, par, q, :], cz[:, par, q, :], cx[:, par, q, :], ALU.add).then_inc(c_done, 1)

            with pool.Fori(0, SEQS // 2) as n:
                for par in range(2):
                    residual(n * 2 + par, par)


_INS = ["L0_attn_x", "L0_attn_Wq", "L0_attn_Wk", "L0_attn_Wv", "L0_attn_Wo", "L0_attn_Wg1", "L0_attn_Wg2",
        "L0_attn_norm_weight", "L0_ffn_router_w", "L0_ffn_w1", "L0_ffn_w2", "L0_ffn_w_gate", "L0_ffn_w_up",
        "L0_ffn_w_down"]


def kernel(**inputs):
    import numpy as _np
    import concourse.bacc as _bacc
    from concourse import mybir as _mybir
    from concourse.bass_utils import run_bass_kernel_spmd as _run

    nc = _bacc.Bacc("TRN2", target_bir_lowering=False, num_devices=1)
    arrays, args = {}, []
    for name in _INS:
        a = _np.ascontiguousarray(inputs[name])
        arrays[f"in_{name}"] = a
        args.append(nc.dram_tensor(f"in_{name}", a.shape, _mybir.dt.from_np(a.dtype), kind="ExternalInput").ap())
    for name, a in zip(("const32", "const16"), tables()):
        arrays[name] = a
        args.append(nc.dram_tensor(name, a.shape, _mybir.dt.from_np(a.dtype), kind="ExternalInput").ap())
    args.append(nc.dram_tensor("out_0", (SEQS, SEQ, D), F32, kind="ExternalOutput").ap())
    layer_kernel(nc, *args)
    r = _run(nc, [arrays], core_ids=[0])
    return r.results[0]["out_0"]
```

```python
from contextlib import ExitStack

import concourse.bass as bass
import numpy as np
from concourse import mybir

P = 128
SEQS, SEQ, D = 8, 512, 256
TOKENS = SEQS * SEQ
C = P
CPS = SEQ // C
CHUNKS = TOKENS // C
HEADS, HD = 16, 16
KT = D // P
EXPERTS, TOPK, INTER = 8, 2, 512
SHARED = 2 * INTER
UNITS = CHUNKS // 2
PIECES = 10
TILES = TOKENS * TOPK // P + EXPERTS - 1
LN_EPS, RMS_EPS = 1e-5, 1e-6
XS = 2.0 ** 10
NS = 2.0 ** 12
FAR = 1 << 20

F32, F16, I32, U32 = mybir.dt.float32, mybir.dt.float16, mybir.dt.int32, mybir.dt.uint32
ACT, ALU = mybir.ActivationFunctionType, mybir.AluOpType
X = mybir.AxisListType.X
ABSMAX = bass.bass_isa.ReduceOp.absmax

_F32 = [("ident", P), ("kdec", HEADS), ("cos", CPS * 8), ("sin", CPS * 8), ("iota8", EXPERTS), ("tok", TOPK),
        ("mhalf", HEADS), ("iotat", TILES + 1), ("decay", HEADS * C), ("qdec", KT * C), ("block", KT * P),
        ("blocklam", KT * P)]
_F16 = [("ident", P), ("before", P), ("ones", P), ("iota", P)]


def offsets(parts):
    out, at = {}, 0
    for name, n in parts:
        out[name] = (at, at + n)
        at += n
    return out, at


C32, N32 = offsets(_F32)
C16, N16 = offsets(_F16)
SMALL = C32["decay"][0]


def tables():
    f = np.float32
    lam = -(f(2.0) ** (f(-8.0) * (np.arange(HEADS, dtype=f) + f(1.0)) / f(HEADS)))
    i = np.arange(C, dtype=f)
    t32 = {}
    diff = i[None, :] - i[:, None]
    dec = np.where(diff[:, None, :] >= 0, np.exp(lam[None, :, None] * np.maximum(diff, 0)[:, None, :]), 0)
    t32["decay"] = dec.reshape(P, HEADS * C)
    head = (np.arange(D) // HD).reshape(KT, P).T
    t32["qdec"] = np.exp(lam[head][:, :, None] * (i[None, None, :] + f(1))).reshape(P, KT * C)
    same = (np.arange(P)[:, None] // HD == np.arange(P)[None, :] // HD).astype(f)
    t32["block"] = np.repeat(same[:, None, :], KT, 1).reshape(P, KT * P)
    t32["blocklam"] = (same[:, None, :] * np.exp(lam * f(C))[head][:, :, None]).reshape(P, KT * P)
    t32["kdec"] = np.exp(lam[None, :] * (f(C - 1) - i[:, None]))
    theta = (f(10000.0) ** (f(-2.0) * np.arange(8, dtype=f) / f(HD))).astype(f)
    ang = (np.arange(SEQ, dtype=f)[:, None] * theta[None, :]).astype(f).reshape(CPS, C, 8).transpose(1, 0, 2)
    t32["cos"], t32["sin"] = np.cos(ang).reshape(P, -1), np.sin(ang).reshape(P, -1)
    t32["ident"] = np.eye(P)
    t32["iota8"] = np.broadcast_to(np.arange(EXPERTS), (P, EXPERTS))
    t32["tok"] = 2 * np.arange(P)[:, None] + np.arange(TOPK)[None, :] + 1
    t32["mhalf"] = np.full((P, HEADS), -0.5)
    t32["iotat"] = np.broadcast_to(np.arange(TILES + 1), (P, TILES + 1))
    t16 = {"ident": np.eye(P), "before": np.triu(np.ones((P, P)), 1), "ones": np.ones((P, P)),
           "iota": np.broadcast_to(np.arange(P), (P, P))}
    return (np.concatenate([np.asarray(t32[n], f) for n, _ in _F32], 1),
            np.concatenate([np.asarray(t16[n], np.float16) for n, _ in _F16], 1))


def layer_kernel(nc, x, wq, wk, wv, wo, wg1, wg2, norm_w, router, w1, w2, w_gate, w_up, w_down, c32d, c16d, out):
    whole = ExitStack()
    first = ExitStack()

    def sb(name, shape, dt=F32, stack=whole):
        return stack.enter_context(nc.sbuf_tensor(name, shape, dt))

    def sem(name):
        return whole.enter_context(nc.semaphore(name))

    rows_d = nc.dram_tensor("rows_d", (TOKENS, D), F32, kind="Internal").ap()
    res_d = nc.dram_tensor("res_d", (TOKENS, D), F32, kind="Internal").ap()
    shared_d = nc.dram_tensor("shared_d", (TOKENS, D), F32, kind="Internal").ap()
    picked_d = nc.dram_tensor("picked_d", (TOKENS * TOPK, D), F32, kind="Internal").ap()
    xf = x.rearrange("b n d -> (b n) d")
    outf = out.rearrange("b n d -> (b n) d")

    with whole:
        c32 = sb("c32", [P, N32])
        c16 = sb("c16", [P, N16], F16)

        def k32(name):
            return c32[:, C32[name][0]:C32[name][1]]

        def k16(name):
            return c16[:, C16[name][0]:C16[name][1]]

        w1s = sb("w1s", [P, EXPERTS, 2, KT, 2 * INTER], F16)
        w2s = sb("w2s", [P, EXPERTS, 2, INTER // P, D], F16)
        exp_scale = sb("exp_scale", [P, EXPERTS, 4])
        top_v = sb("top_v", [P, CHUNKS, TOPK])
        top_i = sb("top_i", [P, CHUNKS, TOPK])
        pmax = sb("pmax", [P, 4])
        gmax = sb("gmax", [P, 4])
        pw = sb("pw", [P, 4])
        rp = sb("rp", [P, 4])
        sc = sb("sc", [P, 16])
        (S_A, C_A, C_AH, S_Q, C_S, S_O, C_O, C_O2, S_F, C_F, C_FU, C_FD, T0_, T1_) = range(14)

        def s(col):
            return sc[:, col:col + 1]

        psum = [whole.enter_context(nc.psum_tensor(f"bank{i}", [P, 512], F32)) for i in range(8)]
        A0, A1, A2, A3, A4, A5, FB0, FB1 = psum
        FB = [FB0, FB1]


        const_in = [sem(f"const_in{i}") for i in range(4)]
        set_in = [sem(f"set_in{i}") for i in range(3)]
        zeroed, nw_folded, wg1_T, wg1_copied, wg_made, wg_copied = (sem("zeroed"), sem("nw_folded"), sem("wg1_T"),
            sem("wg1_copied"), sem("wg_made"), sem("wg_copied"))
        set_max, set_all, scale_step, set_scaled, pmax_zero, set_hi, set_lo = (sem("set_max"), sem("set_all"), sem("scale_step"),
            sem("set_scaled"), sem("pmax_zero"),
            sem("set_hi"), sem("set_lo"))
        x_in = [sem(f"x_in{i}") for i in range(CPS)]
        ln1_stats, ln1_mv, ln1_var, ln1_pow, xs_ready = (sem("ln1_stats"), sem("ln1_mv"), sem("ln1_var"),
            sem("ln1_pow"), sem("xs_ready"))
        xT_ready, xT_hi, xT_lo = sem("xT_ready"), sem("xT_hi"), sem("xT_lo")
        proj_ready, qk_act, gate_act, v_copied, v_spread = (sem("proj_ready"), sem("qk_act"), sem("gate_act"),
            sem("v_copied"), sem("v_spread"))
        rope_cos, rope_sin, rotated = sem("rope_cos"), sem("rope_sin"), sem("rotated")
        qk_hi, qk_lo, stacked = sem("qk_hi"), sem("qk_lo"), sem("stacked")
        k_decayed, stack_T, kT_copied, qT_low, qT_high, q_decayed = (sem("k_decayed"), sem("stack_T"),
            sem("kT_copied"), sem("qT_low"), sem("qT_high"), sem("q_decayed"))
        scores_ready, decayed, values_done, oT_ready = (sem("scores_ready"), sem("decayed"),
            sem("values_done"), sem("oT_ready"))
        update_ready, state_old, state_masked, state_new = (sem("update_ready"), sem("state_old"),
            sem("state_masked"), sem("state_new"))
        oT_copied, o_ready, gated, squared, summed = (sem("oT_copied"), sem("o_ready"), sem("gated"),
            sem("squared"), sem("summed"))
        rms_mean, rms_pow, normed = sem("rms_mean"), sem("rms_pow"), sem("normed")
        nT_ready, nT_hi, nT_lo, attn_ready = sem("nT_ready"), sem("nT_hi"), sem("nT_lo"), sem("attn_ready")
        ln2_stats, ln2_mv, ln2_step, attn_normed, x1_ready = (sem("ln2_stats"), sem("ln2_mv"), sem("ln2_step"),
            sem("attn_normed"), sem("x1_ready"))
        ln3_stats, ln3_mv, ln3_step, rows_ready = sem("ln3_stats"), sem("ln3_mv"), sem("ln3_step"), sem("rows_ready")
        rowsT_ready, rowsT_hi, rowsT_lo = sem("rowsT_ready"), sem("rowsT_hi"), sem("rowsT_lo")
        logits_ready, logits_copied, top_step = sem("logits_ready"), sem("logits_copied"), sem("top_step")
        x1_out, rows_out = sem("x1_out"), sem("rows_out")
        shared_out = sem("shared_out")
        piece_ready, piece_act, piece_free, act_hi, act_lo = (sem("piece_ready"), sem("piece_act"),
            sem("piece_free"), sem("act_hi"), sem("act_lo"))
        stage_in, stage_max, exp_max, exp_all, exp_scaled, exp_step, stage_hi, stage_lo = (
            sem("stage_in"), sem("stage_max"), sem("exp_max"), sem("exp_all"), sem("exp_scaled"), sem("exp_step"),
            sem("stage_hi"), sem("stage_lo"))

        route, route_pe, route_act, route_pool = sem("route"), sem("route_pe"), sem("route_act"), sem("route_pool")
        hot_ready, hot_pool, hot_used, owners_ready, ids_ready = (sem("hot_ready"), sem("hot_pool"), sem("hot_used"),
            sem("owners_ready"), sem("ids_ready"))
        index_set = sem("index_set")
        gathered = [sem(f"gathered{i}") for i in range(4)]
        scattered = [sem(f"scattered{i}") for i in range(4)]
        eT_ready, eT_hi, eT_lo, gu_ready, e_silu, e_act = (sem("eT_ready"), sem("eT_hi"), sem("eT_lo"), sem("gu_ready"),
            sem("e_silu"), sem("e_act"))
        aT_ready, ea_hi, ea_lo, res_ready, res_copied = (sem("aT_ready"), sem("ea_hi"), sem("ea_lo"), sem("res_ready"),
            sem("res_copied"))
        c_in = [sem(f"c_in{i}") for i in range(2)]
        c_sum, c_stats, c_mv, c_var, c_rstd, c_shift, c_norm, c_done = (sem("c_sum"), sem("c_stats"), sem("c_mv"),
            sem("c_var"), sem("c_rstd"), sem("c_shift"), sem("c_norm"), sem("c_done"))
        c_out = [sem(f"c_out{i}") for i in range(2)]

        passed = [sem("passed_dve"), sem("passed_pool")]

        wF = sb("wF", [P, 2, 2 * KT * SHARED + SHARED // P * D + KT * EXPERTS], F16)
        rT = sb("rT", [P, 2, 2, KT, 2 * C], F16)
        sg = sb("sg", [P, 2, 2 * C])
        aT = sb("aT", [P, 2, SHARED // P, 2 * C], F16)
        ysh = sb("ysh", [P, D])

        def fb(name, shape, dt=F32):
            return sb(name, shape, dt, first)

        wA = fb("wA", [P, 2, KT, 4 * D], F16)
        wO = fb("wO", [P, 2, KT, D], F16)
        wGU = wF[:, :, 0:2 * KT * SHARED].rearrange("p a (k n) -> p a k n", k=KT)
        wDn = wF[:, :, 2 * KT * SHARED:2 * KT * SHARED + SHARED // P * D].rearrange("p a (k n) -> p a k n", n=D)
        wR = wF[:, :, 2 * KT * SHARED + SHARED // P * D:].rearrange("p a (k n) -> p a k n", n=EXPERTS)
        stage = fb("stage", [P, 1024])
        escale = fb("escale", [P, 8])
        xin = fb("xin", [P, CPS, D])
        xs = fb("xs", [P, D])
        xT = fb("xT", [P, 2, KT, C], F16)
        qk = fb("qk", [P, 2 * D])
        th = fb("th", [P, 2, D])
        vw = fb("vw", [P, 2, HEADS, 2 * HD])
        vn = fb("vn", [P, 2, D])
        rc = fb("rc", [P, 2 * D])
        rs = fb("rs", [P, 2 * D])
        st = fb("st", [P, 2, HEADS, 4, HD], F16)
        kd = fb("kd", [P, 2, D])
        qd = fb("qd", [P, KT, C])
        kT = fb("kT", [P, HEADS // 2, C], F16)
        qT = fb("qT", [P, HEADS // 2, 2, C], F16)
        sd = fb("sd", [P, 2, 4, C])
        state = fb("state", [P, KT, P])
        oT = fb("oT", [P, KT, C])
        y = fb("y", [P, D])
        sq = fb("sq", [P, D])
        nT = fb("nT", [P, 2, KT, C], F16)
        x1 = fb("x1", [P, D])
        rows = fb("rows", [P, D])
        small = fb("small", [P, 96])
        lg = fb("lg", [P, EXPERTS])
        m8 = fb("m8", [P, 8])
        i8 = fb("i8", [P, 8], U32)
        st1, mv1, r1 = small[:, 0:6], small[:, 6:8], small[:, 8:10]
        st2, mv2, r2 = small[:, 10:16], small[:, 16:18], small[:, 18:22]
        st3, mv3, r3 = small[:, 22:28], small[:, 28:30], small[:, 30:32]
        ssum, smean, srms = small[:, 32:48], small[:, 48:64], small[:, 64:80]
        mhalf = k32("mhalf")
        first.close()

        picks = [sb(f"pick{k}", [P, CHUNKS, EXPERTS]) for k in range(TOPK)]
        both = sb("both", [P, CHUNKS * EXPERTS], F16)
        counts = [sb(f"counts{i}", [P, CHUNKS, EXPERTS]) for i in range(3)]
        place_of = sb("place_of", [P, CHUNKS, EXPERTS])
        filled = [sb(f"filled{i}", [P, EXPERTS]) for i in range(4)]
        filled_i = sb("filled_i", [P, EXPERTS], I32)
        spot = sb("spot", [P, TOPK, CHUNKS])
        spot_i, spot_t, spot_r = (sb("spot_i", [P, TOPK, CHUNKS], I32), sb("spot_t", [P, TOPK, CHUNKS], I32),
                                  sb("spot_r", [P, TOPK, CHUNKS], I32))
        tile_f, row_f = sb("tile_f", [P, TOPK, CHUNKS]), sb("row_f", [P, TOPK, CHUNKS])
        prod = sb("prod", [P, CHUNKS, EXPERTS])
        diff = sb("diff", [P, CHUNKS])
        weight = sb("weight", [P, CHUNKS, TOPK])
        cmp = sb("cmp", [P, TILES + 1, EXPERTS - 1])
        owner_f, owner = sb("owner_f", [P, TILES + 1]), sb("owner", [P, TILES + 1], I32)
        hot_r = sb("hot_r", [P, 4, P], F16)
        hot_t = sb("hot_t", [P, 4, 2, TILES + 1], F16)
        ids2, idv, idz = sb("ids2", [P, 2, TILES + 1]), sb("idv", [P, TILES + 1]), sb("idz", [P, TILES + 1])
        gat_i, gat, sca = (sb("gat_i", [P, TILES + 1], I32), sb("gat", [P, TILES + 1], I32), sb("sca", [P, TILES + 1], I32))
        gidx, sidx = sb("gidx", [P, 4], I32), sb("sidx", [P, 4], I32)
        got = [sb(f"got{i}", [P, D]) for i in range(4)]
        eT = sb("eT", [P, 2, 2, KT, C], F16)
        eg = sb("eg", [P, 2, INTER])
        eaT = sb("eaT", [P, 2, 2, INTER // P, C], F16)
        res = [sb(f"res{i}", [P, D]) for i in range(4)]
        cx, cs = sb("cx", [P, 2, 4, D]), sb("cs", [P, 2, 4, D])
        cst, cmv, cr = sb("cst", [P, 4, 6]), sb("cmv", [P, 4, 2]), sb("cr", [P, 4, 3])

        def halves(ap):
            return ap.rearrange("p (h a e) -> p h a e", a=2, e=HD // 2)

        raw = w1s[:, 1:, :, :, :].rearrange("p a b c d -> p (a b c d)").bitcast(F32)
        cp = raw[:, 0:2 * 4 * TOPK * D].rearrange("p (a q k n) -> p a q k n", a=2, q=4, k=TOPK)
        cz = raw[:, 2 * 4 * TOPK * D:2 * 4 * (TOPK + 1) * D].rearrange("p (a q n) -> p a q n", a=2, q=4)
        nA, nO, nF = KT * 4 * D, KT * D, 2 * KT * SHARED + SHARED // P * D + KT * EXPERTS
        rawA, rawO, rawF = raw[:, 0:nA], raw[:, nA:nA + nO], raw[:, nA + nO:nA + nO + nF]
        rawA3 = rawA.rearrange("p (k n) -> p k n", k=KT)
        rawGU = rawF[:, 0:2 * KT * SHARED].rearrange("p (k n) -> p k n", k=KT)
        rawDn = rawF[:, 2 * KT * SHARED:2 * KT * SHARED + SHARED // P * D].rearrange("p (k n) -> p k n", n=D)
        rawR = rawF[:, 2 * KT * SHARED + SHARED // P * D:].rearrange("p (k n) -> p k n", n=EXPERTS)
        rawG1 = raw[:, nA + nO + nF:nA + nO + nF + KT * HD].rearrange("p (k e) -> p k e", e=HD)
        rest = nA + nO + nF + KT * HD
        rawG1T, rawG2, rawNW = raw[0:HD, rest:rest + D], raw[0:HD, rest + D:rest + 2 * D], raw[:, rest + 2 * D:rest + 2 * D + KT]
        row = "(k p) n -> p k n"

        block = whole.enter_context(nc.Block())

        def alone(eng):
            eng.sem_inc(passed[0] if eng.engine == nc.vector.engine else passed[1], 1)

        def at(b, c):
            return b * CPS + c

        def shift(b, c, by):
            return b + (c + by) // CPS, (c + by) % CPS

        def later(t, first=1):
            return not isinstance(t, int) or t >= first

        def pieces(b, c, place):
            if c % 2:
                unit, parity = 2 * b - 1 + c // 2, 1 - c // 2
                work = [[(unit - 1, 1 - parity, 9)], [(unit, parity, 0)], [(unit, parity, 1)], [(unit, parity, 2)],
                        [(unit, parity, 3), (unit, parity, 4)]]
                if isinstance(unit, int) and unit == 0:
                    work[0] = []
            else:
                unit, parity = 2 * b - 2 + c // 2, c // 2
                work = [[(unit, parity, 5)], [(unit, parity, 6)], [(unit, parity, 7)], [(unit, parity, 8)], []]
                if isinstance(unit, int) and unit == UNITS - 1:
                    work[4] = [(unit, parity, 9)]
            return work[place]

        def run_slots(eng, slot):
            whole_slot = {"look", "project", "attend", "norm", "route", "ffn", "expert"}

            def peeled(n):
                on = {part for part, by in (("look", 2), ("project", 1), ("attend", 0), ("norm", -1), ("route", -2))
                      if 0 <= n + by < CHUNKS}
                slot(n // CPS, n % CPS, on | ({"ffn"} if n >= 3 else set()) | ({"expert"} if 0 <= n < CHUNKS else set()))

            for n in range(-1, CPS):
                peeled(n)
            with eng.Fori(1, SEQS - 1) as b:
                for c in range(CPS):
                    slot(b, c, whole_slot)
            for n in range(CHUNKS - CPS, CHUNKS + 3):
                peeled(n)

        def run_tiles(eng, slot):
            for j in range(8):
                slot(j, j % 4, j // 4)
            with eng.Fori(2, TILES // 4) as m:
                for i in range(4):
                    slot(m * 4 + i, i, m)
            for j in range(TILES // 4 * 4, TILES + 2):
                slot(j, j % 4, j // 4)

        def has(j, shift):
            return not isinstance(j, int) or 0 <= j + shift < TILES

        @block.sync
        def _(sp):
            def load_x(b, c):
                sp.dma_start(xin[:, c, :], xf[bass.ds(at(b, c) * C, C), :]).then_inc(x_in[c], 16)

            sp.sem_inc(shared_out, 16)
            load_x(0, 0)
            sp.dma_start(c32[:, 0:SMALL], c32d[:, 0:SMALL]).then_inc(const_in[0], 16)
            sp.dma_start(rawG1, wg1.rearrange(row, p=P)).then_inc(const_in[2], 16)
            sp.dma_start(rawG2, wg2).then_inc(const_in[2], 16)
            for i, w in enumerate((wq, wk, wv)):
                sp.dma_start(rawA3[:, :, i * D:(i + 1) * D], w.rearrange(row, p=P)).then_inc(set_in[0], 16)
            load_x(0, 1)
            sp.dma_start(c16[:, :], c16d).then_inc(const_in[1], 16)
            sp.dma_start(c32[:, SMALL:], c32d[:, SMALL:]).then_inc(const_in[3], 16)
            sp.dma_start(rawO.rearrange("p (k n) -> p k n", k=KT), wo.rearrange(row, p=P)).then_inc(set_in[1], 16)
            with nc.allow_non_contiguous_dma(reason="256 values"):
                sp.dma_start(rawNW, norm_w.rearrange("(k p) -> p k", p=P)).then_inc(set_in[1], 16)
            for c in range(2, CPS):
                load_x(0, c)
            for i, w in enumerate((w_gate, w_up)):
                sp.dma_start(rawGU[:, :, i * SHARED:(i + 1) * SHARED], w.rearrange(row, p=P)).then_inc(set_in[2], 16)
            sp.dma_start(rawDn, w_down.rearrange(row, p=P)).then_inc(set_in[2], 16)
            sp.dma_start(rawR, router.rearrange(row, p=P)).then_inc(set_in[2], 16)

            def load_expert(e, i):
                if i == 0:
                    if not isinstance(e, int) or e:
                        sp.wait_ge(stage_lo, e * 3)
                elif i <= 3:
                    sp.wait_ge(stage_max, e * 3 + i)
                else:
                    sp.wait_ge(stage_lo, e * 3 + (i - 3))
                j = i % 3
                src = w1[bass.ds(e, 1), j * P:(j + 1) * P, :].rearrange("a p n -> p (a n)") if j < KT else \
                    w2[bass.ds(e, 1), :, :].rearrange("a (k p) n -> p (a k) n", p=P)
                dst = stage[:, :] if j < KT else stage[:, :].rearrange("p (k n) -> p k n", n=D)
                sp.dma_start(dst, src).then_inc(stage_in, 16)

            def store_shared(unit, i):
                sp.wait_ge(piece_free, unit * PIECES + 9 + i)
                sp.dma_start(shared_d[bass.ds(unit * 2 * C + i * C, C), :], ysh[:, :]).then_inc(shared_out, 16)

            def slot(b, c, on):
                if "ffn" in on:
                    for unit, _, p in pieces(b, c, 0):
                        if p == 9:
                            store_shared(unit, 1)
                if "expert" in on:
                    for i in ([0, 1], [2], [4], [])[c]:
                        load_expert(b, i)
                if "ffn" in on:
                    for unit, _, p in pieces(b, c, 3):
                        if p == 8:
                            store_shared(unit, 0)
                if "norm" in on:
                    tb, tc = shift(b, c, -1)
                    t = at(tb, tc)
                    sp.wait_ge(x1_ready, t + 1)
                    sp.dma_start(res_d[bass.ds(t * C, C), :], x1[:, :]).then_inc(x1_out, 16)
                    if not isinstance(tb, int) or tb < SEQS - 1:
                        load_x(tb + 1, tc)
                if "expert" in on:
                    for i in ([], [3], [5], [])[c]:
                        load_expert(b, i)
                if "norm" in on:
                    sp.wait_ge(rows_ready, t + 1)
                    sp.dma_start(rows_d[bass.ds(t * C, C), :], rows[:, :]).then_inc(rows_out, 16)
                if "ffn" in on:
                    for unit, _, p in pieces(b, c, 4):
                        if p == 9:
                            store_shared(unit, 1)

            run_slots(sp, slot)
            sp.wait_ge(x1_out, 16 * CHUNKS)
            sp.wait_ge(rows_out, 16 * CHUNKS)
            sp.wait_ge(shared_out, 16 * CHUNKS + 16)

            sp.wait_ge(ids_ready, 1)
            four = "(q p) n -> p q n"

            def load_known(g, par):
                at_g = bass.ds(g * 4 * C, 4 * C)
                sp.dma_start(cx[:, par, :, :], res_d[at_g, :].rearrange(four, p=P)).then_inc(c_in[par], 16)
                sp.dma_start(cs[:, par, :, :], shared_d[at_g, :].rearrange(four, p=P)).then_inc(c_in[par], 16)

            def load_picked(g, par):
                sp.dma_start(cp[:, par, :, :, :].rearrange("p q k n -> p q (k n)"),
                             picked_d[bass.ds(g * 8 * C, 8 * C), :].rearrange("(q p k) n -> p q (k n)", p=P, k=TOPK))\
                    .then_inc(c_in[par], 16)

            for par in range(2):
                load_known(par, par)
            for i in range(4):
                sp.wait_ge(scattered[i], 16 * ((TILES - i + 3) // 4))
            for par in range(2):
                load_picked(par, par)

            def store(g, par, n):
                sp.wait_ge(c_done, 4 * g + 4)
                sp.dma_start(outf[bass.ds(g * 4 * C, 4 * C), :].rearrange(four, p=P), cz[:, par, :, :]).then_inc(c_out[par], 16)

            with sp.Fori(0, SEQS // 2 - 1) as n:
                for par in range(2):
                    store(n * 2 + par, par, n)
                    load_known(n * 2 + par + 2, par)
                    load_picked(n * 2 + par + 2, par)
            for par in range(2):
                store(SEQS - 2 + par, par, SEQS // 2 - 1)
            for par in range(2):
                sp.wait_ge(c_out[par], 16 * SEQS // 2)

        @block.tensor
        def _(pe):
            ident, ident16 = k32("ident"), k16("ident")

            def product(bank, pairs):
                steps = [(left[a], right[b_]) for left, right in pairs for a, b_ in ((0, 0), (0, 1), (1, 0))]
                for i, (left, right) in enumerate(steps):
                    last = nc.tensor.matmul(bank, left, right, start=i == 0, stop=i == len(steps) - 1)
                return last

            pe.wait_ge(const_in[2], 32)
            pe.wait_ge(const_in[0], 16)
            for k in range(KT):
                last = nc.tensor.transpose(A0[0:HD, k * P:(k + 1) * P], rawG1[:, k, :], ident)
            last.then_inc(wg1_T, 1)
            pe.wait_ge(wg1_copied, 1)
            for k in range(KT):
                last = nc.tensor.matmul(A1[:, k * D:(k + 1) * D], rawG1T[:, k * P:(k + 1) * P], rawG2, start=True, stop=True)
            last.then_inc(wg_made, 1)

            def piece(unit, parity, p):
                n = unit * PIECES + p
                bank = FB[p % 2]
                if not (isinstance(n, int) and n < 2):
                    pe.wait_ge(piece_free, n - 1)
                if p < 8:
                    if p == 0:
                        pe.wait_ge(rowsT_lo, unit * 2 + 2)
                        if isinstance(unit, int) and unit == 0:
                            pe.wait_ge(set_lo, 3)
                    for half in range(2):
                        cols = slice(half * SHARED + p * P, half * SHARED + (p + 1) * P)
                        last = product(bank[:, half * 2 * C:(half + 1) * 2 * C],
                                       [([wGU[:, a, k, cols] for a in range(2)], [rT[:, parity, a, k, :] for a in range(2)])
                                        for k in range(KT)])
                else:
                    pe.wait_ge(act_lo, unit * 8 + 8)
                    tok = slice((p - 8) * C, (p - 7) * C)
                    last = product(bank[:, 0:D], [([aT[:, a, j, tok] for a in range(2)], [wDn[:, a, j, :] for a in range(2)])
                                                  for j in range(SHARED // P)])
                last.then_inc(piece_ready, 1)

            def slot(b, c, on):
                t, n = at(b, c), at(*shift(b, c, 1))
                tb, tc = shift(b, c, -1)
                ub, uc = shift(b, c, -2)
                tt, uu = at(tb, tc), at(ub, uc)

                def place(i):
                    if "ffn" in on:
                        for unit, parity, p in pieces(b, c, i):
                            piece(unit, parity, p)

                def scores(g):
                    if g >= 2:
                        pe.wait_ge(decayed, 4 * t + g - 1)
                    elif later(t):
                        if g == 0 and c:
                            pe.wait_ge(state_masked, 3 * b + c)
                        elif g == 1:
                            pe.wait_ge(decayed, 4 * t)
                    for j in range(2):
                        m = 2 * g + j
                        last = nc.tensor.matmul((A3, A4)[g % 2][:, j * 2 * C:(j + 1) * 2 * C], kT[:, m, :],
                                                qT[:, m, :, :].rearrange("p a t -> p (a t)"), start=True, stop=True)
                    last.then_inc(scores_ready, 1)

                def values(g):
                    k = g // 2
                    pe.wait_ge(decayed, 4 * t + g + 1)
                    for i in range(4):
                        h = 4 * g + i
                        q = 32 * ((h // 2) % 4)
                        last = nc.tensor.matmul(A0[q:q + 32, k * P:(k + 1) * P], vw[:, c % 2, h, :], sd[:, g % 2, i, :],
                                                start=(c == 0 and h % 2 == 0), stop=h % 2 == 1, skip_group_check=True)
                    last.then_inc(values_done, 1)

                if "project" in on:
                    pe.wait_ge(xs_ready, n + 1)
                    if later(t):
                        pe.wait_ge(oT_copied, t)
                    for k in range(KT):
                        last = nc.tensor.transpose(A0[:, k * P:(k + 1) * P], xs[:, k * P:(k + 1) * P], ident)
                    last.then_inc(xT_ready, 1)
                if "norm" in on:
                    pe.wait_ge(oT_copied, tt + 1)
                    if later(tt):
                        pe.wait_ge(attn_normed, tt)
                    for k in range(KT):
                        last = nc.tensor.transpose(A5[:, k * P:(k + 1) * P], oT[:, k, :], ident)
                    last.then_inc(o_ready, 1)
                place(0)
                if "route" in on:
                    pe.wait_ge(rows_ready, uu + 1)
                    if "norm" in on:
                        pe.wait_ge(gated, tt + 1)
                    else:
                        pe.wait_ge(attn_normed, uu + 1)
                    for k in range(KT):
                        last = nc.tensor.transpose(A5[:, k * P:(k + 1) * P], rows[:, k * P:(k + 1) * P], ident)
                    last.then_inc(rowsT_ready, 1)
                if "attend" in on:
                    pe.wait_ge(stacked, 3 * t + 3)
                    pe.wait_ge(v_copied, t + 1)
                    if "project" in on:
                        pe.wait_ge(xT_lo, n + 1)
                    elif later(t):
                        pe.wait_ge(oT_copied, t)
                    if isinstance(t, int) and t == 0:
                        pe.wait_ge(const_in[1], 16)
                    for half, bank in ((0, A1), (1, A2)):
                        b16 = bank[:, :].bitcast(F16)
                        for j in range(HEADS // 2):
                            nc.tensor.transpose(b16[:, j * P:(j + 1) * P],
                                                st[:, half, 2 * j:2 * j + 2, :, :].rearrange("p h a e -> p (h a e)"), ident16)
                    for k in range(KT):
                        last = nc.tensor.transpose(A0[:, k * P:(k + 1) * P], qk[:, k * P:(k + 1) * P], ident)
                    last.then_inc(stack_T, 1)
                place(1)
                if "route" in on:
                    pe.wait_ge(rowsT_lo, uu + 1)
                    if isinstance(uu, int) and uu == 0:
                        pe.wait_ge(set_lo, 3)
                    par, tok = uc // 2, slice(uc % 2 * C, (uc % 2 + 1) * C)
                    product(A5[:, 0:EXPERTS], [([rT[:, par, a, k, tok] for a in range(2)], [wR[:, a, k, :] for a in range(2)])
                                               for k in range(KT)]).then_inc(logits_ready, 1)
                if "attend" in on:
                    pe.wait_ge(kT_copied, t + 1)
                    pe.wait_ge(qT_low, t + 1)
                    pe.wait_ge(qT_high, t + 1)
                    pe.wait_ge(v_spread, t + 1)
                    if isinstance(t, int) and t == 0:
                        pe.wait_ge(zeroed, 2)
                    scores(0)
                    scores(1)
                if "project" in on:
                    pe.wait_ge(xT_lo, n + 1)
                    if isinstance(n, int) and n == 0:
                        pe.wait_ge(set_lo, 1)
                    for h, bank in enumerate((A1, A2)):
                        product(bank[:, :], [([xT[:, a, k, :] for a in range(2)],
                                              [wA[:, a, k, h * 2 * D:(h + 1) * 2 * D] for a in range(2)]) for k in range(KT)])\
                            .then_inc(proj_ready, 1)
                if "norm" in on:
                    pe.wait_ge(normed, tt + 1)
                    if "route" in on:
                        pe.wait_ge(logits_copied, uu + 1)
                    for k in range(KT):
                        last = nc.tensor.transpose(A5[:, k * P:(k + 1) * P], y[:, k * P:(k + 1) * P], ident)
                    last.then_inc(nT_ready, 1)
                place(2)
                if "attend" in on:
                    pe.wait_ge(q_decayed, t + 1)
                    if c:
                        pe.wait_ge(state_new, 3 * b + c)
                        for k in range(KT):
                            nc.tensor.matmul(A0[:, k * P:(k + 1) * P], state[:, k, :], qd[:, k, :],
                                             start=k == 0, stop=False, skip_group_check=True)
                    values(0)
                    scores(2)
                    values(1)
                    scores(3)
                    if c < CPS - 1:
                        pe.wait_ge(k_decayed, t + 1)
                        pe.wait_ge(decayed, 4 * t + 3)
                        for k in range(KT):
                            last = nc.tensor.matmul(A3[:, k * P:(k + 1) * P], kd[:, c % 2, k * P:(k + 1) * P],
                                                    vn[:, c % 2, k * P:(k + 1) * P], start=True, stop=True)
                        last.then_inc(update_ready, 1)
                if "norm" in on:
                    pe.wait_ge(nT_lo, tt + 1)
                    if isinstance(tt, int) and tt == 0:
                        pe.wait_ge(set_lo, 2)
                    product(A5[:, 0:D], [([nT[:, a, k, :] for a in range(2)], [wO[:, a, k, :] for a in range(2)])
                                         for k in range(KT)]).then_inc(attn_ready, 1)
                place(3)
                if "attend" in on:
                    values(2)
                    values(3)
                place(4)

            run_slots(pe, slot)

            pe.wait_ge(route, 3)
            n = CHUNKS * EXPERTS
            nc.tensor.matmul(A0[:, 0:n], k16("before"), both[:, :], start=True, stop=True)
            nc.tensor.matmul(A1[:, 0:n], k16("ones"), both[:, :], start=True, stop=True).then_inc(route_pe, 1)
            for i in range(TOPK * CHUNKS):
                pe.wait_ge(hot_ready, 2 * i + 2)
                pe.wait_ge(hot_pool, i + 1)
                nc.tensor.matmul(A2[:, 0:2 * (TILES + 1)], hot_r[:, i % 4, :], hot_t[:, i % 4, :, :].rearrange("p a t -> p (a t)"),
                                 start=i == 0, stop=i == TOPK * CHUNKS - 1).then_inc(hot_used, 1)

            pe.wait_ge(stage_lo, 3 * EXPERTS)
            pe.wait_ge(owners_ready, 1)
            pe.wait_ge(ids_ready, 1)

            def rows_T(j, i, m):
                pe.wait_ge(gathered[i % 4], 16 * (m + i // 4 + 1))
                if not isinstance(j, int) or j:
                    pe.wait_ge(eT_lo, j)
                for k in range(KT):
                    last = nc.tensor.transpose(A5[:, k * P:(k + 1) * P], got[i % 4][:, k * P:(k + 1) * P], ident)
                last.then_inc(eT_ready, 1)

            rows_T(0, 0, 0)

            def tile_slot(j, i, m):
                if has(j, 0):
                    e = pe.value_load(owner[0:1, bass.ds(j, 1)], min_val=0, max_val=EXPERTS - 1)
                    pe.wait_ge(eT_lo, j + 1)
                    if not isinstance(j, int) or j >= 2:
                        pe.wait_ge(e_act, j - 1)
                    for half in range(2):
                        product((A0, A1, A2, A3)[2 * (i % 2) + half][:, :],
                                [([eT[:, i % 2, a, k, :] for a in range(2)],
                                  [w1s[:, bass.ds(e, 1), a, k, half * INTER:(half + 1) * INTER] for a in range(2)])
                                 for k in range(KT)]).then_inc(gu_ready, 1)
                if has(j, -1):
                    pe.wait_ge(e_act, j)
                    if not isinstance(j, int) or j >= 2:
                        pe.wait_ge(ea_lo, j - 1)
                    for q in range(INTER // P):
                        last = nc.tensor.transpose(A4[:, q * P:(q + 1) * P], eg[:, (i - 1) % 2, q * P:(q + 1) * P], ident)
                    last.then_inc(aT_ready, 1)
                if has(j, 1):
                    rows_T(j + 1, i + 1, m)
                if has(j, -2):
                    e = pe.value_load(owner[0:1, bass.ds(j - 2, 1)], min_val=0, max_val=EXPERTS - 1)
                    pe.wait_ge(ea_lo, j - 1)
                    if isinstance(j, int) and j == 2:
                        pe.wait_ge(piece_free, UNITS * PIECES)
                    if not isinstance(j, int) or j >= 4:
                        pe.wait_ge(res_copied, j - 3)
                    product(FB[i % 2][:, 0:D], [([eaT[:, i % 2, a, q, :] for a in range(2)],
                                                 [w2s[:, bass.ds(e, 1), a, q, :] for a in range(2)])
                                                for q in range(INTER // P)]).then_inc(res_ready, 1)

            run_tiles(pe, tile_slot)

        @block.scalar
        def _(act):
            act.wait_ge(wg1_T, 1)
            nc.scalar.activation(rawG1T, A0[0:HD, 0:D], ACT.Copy).then_inc(wg1_copied, 1)
            act.wait_ge(wg_made, 1)
            nc.scalar.activation(rawA3[:, :, 3 * D:], A1[:, :].rearrange("p (k n) -> p k n", k=KT), ACT.Copy).then_inc(wg_copied, 1)

            def set_high(i):
                dst, src, col = ((wA[:, 0, :, :].rearrange("p k n -> p (k n)"), rawA, S_A),
                                 (wO[:, 0, :, :].rearrange("p k n -> p (k n)"), rawO, S_O), (wF[:, 0, :], rawF, S_F))[i]
                act.wait_ge(set_scaled, i + 1)
                nc.scalar.activation(dst, src, ACT.Copy, scale=s(col)).then_inc(set_hi, 1)

            def piece(unit, p):
                if 1 <= p <= 8:
                    act.wait_ge(piece_free, unit * PIECES + p)
                    nc.scalar.activation(aT[:, 0, p - 1, :], sg[:, (p - 1) % 2, :], ACT.Copy).then_inc(act_hi, 1)
                if p < 8:
                    act.wait_ge(piece_ready, unit * PIECES + p + 1)
                    if not (isinstance(unit, int) and unit * 8 + p < 2):
                        act.wait_ge(act_lo, unit * 8 + p - 1)
                    nc.scalar.activation(sg[:, p % 2, :], FB[p % 2][:, 0:2 * C], ACT.Silu, scale=s(C_F)).then_inc(piece_act, 1)

            def slot(b, c, on):
                t, nc_ = at(b, c), (c + 1) % CPS
                n = at(*shift(b, c, 1))
                tb, tc = shift(b, c, -1)
                ub, uc = shift(b, c, -2)
                tt, uu = at(tb, tc), at(ub, uc)
                if "project" not in on:
                    n = None

                def place(i):
                    if "ffn" in on:
                        for unit, _, p in pieces(b, c, i):
                            piece(unit, p)

                def expert_hi(j):
                    act.wait_ge(exp_scaled, b + 1)
                    act.wait_ge(stage_in, (b * 6 + 3 + j + 1) * 16)
                    dst = w1s[:, bass.ds(b, 1), 0, j, :] if j < KT else \
                        w2s[:, bass.ds(b, 1), 0, :, :].rearrange("p a k n -> p (a k n)")
                    nc.scalar.activation(dst, stage[:, :], ACT.Copy, scale=escale[:, 0:1]).then_inc(stage_hi, 1)

                if "project" in on:
                    act.wait_ge(xT_ready, n + 1)
                    nc.scalar.activation(xT[:, 0, :, :].rearrange("p k t -> p (k t)"), A0[:, 0:D], ACT.Copy).then_inc(xT_hi, 1)
                    if isinstance(n, int) and n == 0:
                        set_high(0)
                if "norm" in on:
                    act.wait_ge(gated, tt + 1)
                    nc.scalar.activation(sq[:, :], y[:, :], ACT.Square).then_inc(squared, 1)
                place(0)
                if "route" in on:
                    act.wait_ge(rowsT_ready, uu + 1)
                    nc.scalar.activation(rT[:, uc // 2, 0, :, uc % 2 * C:(uc % 2 + 1) * C],
                                         A5[:, 0:D].rearrange("p (k t) -> p k t", k=KT), ACT.Copy).then_inc(rowsT_hi, 1)
                if "attend" in on:
                    act.wait_ge(stack_T, t + 1)
                    nc.scalar.activation(kT[:, :, :].rearrange("p j t -> p (j t)"), A2[:, :].bitcast(F16), ACT.Copy).then_inc(kT_copied, 1)
                    if isinstance(t, int) and t == 0:
                        act.wait_ge(zeroed, 2)
                    act.wait_ge(qT_low, t + 1)
                    nc.scalar.activation(qT[64:128, :, 1, :], A1[:, :].bitcast(F16).rearrange("p (j t) -> p j t", t=C)[64:128, :, :],
                                         ACT.Copy).then_inc(qT_high, 1)
                place(1)
                if "expert" in on and c >= 2:
                    expert_hi(2 * (c - 2))
                if "project" in on:
                    act.wait_ge(proj_ready, 2 * n + 1)
                    if later(n):
                        act.wait_ge(k_decayed, n)
                        act.wait_ge(stack_T, n)
                    nc.scalar.activation(qk[:, :], A1[:, :], ACT.Silu, scale=s(C_A)).then_inc(qk_act, 1)
                    act.wait_ge(proj_ready, 2 * n + 2)
                    if later(n, 2):
                        act.wait_ge(v_spread, n - 1)
                    nc.scalar.activation(vn[:, nc_ % 2, :], A2[:, 0:D], ACT.Copy, scale=s(C_A)).then_inc(v_copied, 1)
                    if later(n, 2):
                        act.wait_ge(gated, n - 1)
                    nc.scalar.activation(th[:, nc_ % 2, :], A2[:, D:], ACT.Tanh, scale=s(C_AH)).then_inc(gate_act, 1)
                if "norm" in on:
                    act.wait_ge(nT_ready, tt + 1)
                    nc.scalar.activation(nT[:, 0, :, :].rearrange("p k t -> p (k t)"), A5[:, 0:D], ACT.Copy).then_inc(nT_hi, 1)
                place(2)
                if "project" in on:
                    act.wait_ge(rotated, 2 * n + 2)
                    nc.scalar.activation(st[:, :, :, 0, :].rearrange("p a h e -> p (a h) e"),
                                         qk[:, :].rearrange("p (h e) -> p h e", e=HD), ACT.Copy, scale=s(S_Q)).then_inc(qk_hi, 1)
                if isinstance(t, int) and t == 0:
                    set_high(1)
                    set_high(2)
                place(3)
                if "norm" in on:
                    act.wait_ge(ln2_step, 4 * tt + 4)
                    if later(tt):
                        act.wait_ge(x1_out, 16 * tt)
                        act.wait_ge(rows_ready, tt)
                    nc.scalar.activation(x1[:, :], A5[:, 0:D], ACT.Identity, scale=r2[:, 2:3], bias=r2[:, 3:4])\
                        .then_inc(attn_normed, 1)
                if "attend" in on:
                    act.wait_ge(values_done, 4 * t + 4)
                    if later(t):
                        act.wait_ge(o_ready, t)
                    nc.scalar.activation(oT[:, :, :].rearrange("p k t -> p (k t)"), A0[:, 0:D], ACT.Copy).then_inc(oT_copied, 1)
                if "expert" in on and c == 2:
                    expert_hi(1)
                place(4)

            run_slots(act, slot)

            act.wait_ge(route, 4)
            nc.scalar.activation(diff[:, :], diff[:, :], ACT.Tanh, scale=0.5).then_inc(route_act, 1)

            act.wait_ge(exp_scaled, EXPERTS)
            act.wait_ge(owners_ready, 1)

            def rows_hi(j, i):
                act.wait_ge(eT_ready, j + 1)
                nc.scalar.activation(eT[:, i % 2, 0, :, :].rearrange("p k t -> p (k t)"), A5[:, 0:D], ACT.Copy).then_inc(eT_hi, 1)

            rows_hi(0, 0)

            def tile_slot(j, i, m):
                if has(j, 0):
                    e = act.value_load(owner[0:1, bass.ds(j, 1)], min_val=0, max_val=EXPERTS - 1)
                    act.wait_ge(gu_ready, 2 * j + 1)
                    nc.scalar.activation(eg[:, i % 2, :], (A0, A2)[i % 2][:, :], ACT.Silu,
                                         scale=exp_scale[:, bass.ds(e, 1), 1:2].rearrange("p a b -> p (a b)")).then_inc(e_silu, 1)
                if has(j, -1):
                    act.wait_ge(aT_ready, j)
                    nc.scalar.activation(eaT[:, (i - 1) % 2, 0, :, :].rearrange("p q t -> p (q t)"), A4[:, :], ACT.Copy).then_inc(ea_hi, 1)
                if has(j, 1):
                    rows_hi(j + 1, i + 1)
                if has(j, -2):
                    e = act.value_load(owner[0:1, bass.ds(j - 2, 1)], min_val=0, max_val=EXPERTS - 1)
                    act.wait_ge(res_ready, j - 1)
                    if not isinstance(j, int) or j >= 6:
                        act.wait_ge(scattered[(i - 2) % 4], 16 * (m + (i - 2) // 4))
                    nc.scalar.activation(res[(i - 2) % 4][:, :], FB[i % 2][:, 0:D], ACT.Copy,
                                         scale=exp_scale[:, bass.ds(e, 1), 3:4].rearrange("p a b -> p (a b)")).then_inc(res_copied, 1)

            run_tiles(act, tile_slot)

            def normalize(g, par):
                act.wait_ge(c_shift, g + 1)
                for q in range(4):
                    nc.scalar.activation(cz[:, par, q, :], cz[:, par, q, :], ACT.Identity, scale=cr[:, q, 1:2],
                                         bias=cr[:, q, 2:3]).then_inc(c_norm, 1)

            with act.Fori(0, SEQS // 2) as n:
                for par in range(2):
                    normalize(n * 2 + par, par)

        @block.vector
        def _(dve):
            nc.vector.memset(pmax[:, :], 0.0).then_inc(pmax_zero, 1)
            nc.vector.memset(vw[:, :, :, :], 0.0).then_inc(zeroed, 1)
            nc.vector.memset(qT[:, :, :, :], 0.0).then_inc(zeroed, 1)
            dve.wait_ge(pmax_zero, 1)

            def ln1(b, c):
                t = at(b, c)
                dve.wait_ge(x_in[c], (b + 1) * 16)
                nc.vector.bn_stats(st1, xin[:, c, :]).then_inc(ln1_stats, 1)
                dve.wait_ge(ln1_stats, t + 1)
                alone(dve)
                nc.vector.bn_aggr(mv1, st1).then_inc(ln1_mv, 1)

            def xs_rows(b, c):
                t = at(b, c)
                dve.wait_ge(ln1_pow, t + 1)
                if later(t):
                    dve.wait_ge(xT_ready, t)
                nc.vector.tensor_scalar(xs[:, :], xin[:, c, :], mv1[:, 0:1], r1[:, 1:2], ALU.subtract, ALU.mult).then_inc(xs_ready, 1)
                dve.wait_ge(xs_ready, t + 1)

            ln1(0, 0)
            xs_rows(0, 0)

            def set_largest(i):
                nc.vector.tensor_reduce(pmax[:, i:i + 1], (rawA, rawO, rawF)[i], axis=X, op=ALU.max,
                                        apply_absolute_value=True).then_inc(set_max, 1)

            step = [0]

            def chain(ins):
                step[0] += 1
                ins.then_inc(scale_step, 1)
                dve.wait_ge(scale_step, step[0])

            def powers(a, b_):
                chain(nc.vector.tensor_scalar(gmax[:, a:b_], gmax[:, a:b_], 2.0 ** -30, 2.0 ** 30, ALU.max, ALU.min))
                chain(nc.vector.tensor_scalar(pw[:, a:b_].bitcast(I32), gmax[:, a:b_].bitcast(I32), 0x7F800000, None, ALU.bitwise_and))
                chain(nc.vector.reciprocal(rp[:, a:b_], pw[:, a:b_]))

            def times(*scales):
                for dst, src, f in scales:
                    last = nc.vector.tensor_scalar(s(dst), src, f, None, ALU.mult)
                chain(last)

            def set_low(i):
                dst, hi, src, col = (
                    (wA[:, 1, :, :].rearrange("p k n -> p (k n)"), wA[:, 0, :, :].rearrange("p k n -> p (k n)"), rawA, S_A),
                    (wO[:, 1, :, :].rearrange("p k n -> p (k n)"), wO[:, 0, :, :].rearrange("p k n -> p (k n)"), rawO, S_O),
                    (wF[:, 1, :], wF[:, 0, :], rawF, S_F))[i]
                dve.wait_ge(set_hi, i + 1)
                nc.vector.scalar_tensor_tensor(dst, src, s(col), hi, ALU.mult, ALU.subtract).then_inc(set_lo, 1)

            dve.wait_ge(set_in[0], 48)
            dve.wait_ge(wg_copied, 1)
            set_largest(0)
            dve.wait_ge(set_all, 1)
            powers(0, 1)
            times((S_A, rp[:, 0:1], 2.0 ** 14))
            dve.sem_inc(set_scaled, 1)
            chain(nc.vector.tensor_tensor(sc[:, T0_:T0_ + 1], pw[:, 0:1], pw[:, 0:1], ALU.mult))
            times((C_A, pw[:, 0:1], 2.0 ** -24), (C_AH, pw[:, 0:1], 2.0 ** -25), (S_Q, rp[:, 0:1], 2.0 ** 5), (C_S, s(T0_), 2.0 ** -10))

            def lo(unit, p):
                dve.wait_ge(act_hi, unit * 8 + p + 1)
                nc.vector.tensor_tensor(aT[:, 1, p, :], sg[:, p % 2, :], aT[:, 0, p, :], ALU.subtract).then_inc(act_lo, 1)

            def piece(unit, p):
                if 1 <= p <= 8:
                    lo(unit, p - 1)
                if p < 8:
                    dve.wait_ge(piece_act, unit * 8 + p + 1)
                    nc.vector.scalar_tensor_tensor(sg[:, p % 2, :], FB[p % 2][:, 2 * C:], s(C_FU), sg[:, p % 2, :],
                                                   ALU.mult, ALU.mult).then_inc(piece_free, 1)
                else:
                    dve.wait_ge(piece_ready, unit * PIECES + p + 1)
                    dve.wait_ge(shared_out, (unit * 2 + p - 7) * 16)
                    nc.vector.tensor_scalar(ysh[:, :], FB[p % 2][:, 0:D], s(C_FD), None, ALU.mult).then_inc(piece_free, 1)

            def slot(b, c, on):
                t, n = at(b, c), at(*shift(b, c, 1))
                nc_ = (c + 1) % CPS
                tb, tc = shift(b, c, -1)
                ub, uc = shift(b, c, -2)
                tt, uu = at(tb, tc), at(ub, uc)

                def place(i):
                    if "ffn" in on:
                        for unit, _, p in pieces(b, c, i):
                            piece(unit, p)

                def expert_max(j):
                    dve.wait_ge(stage_in, (b * 6 + j + 1) * 16)
                    nc.vector.tensor_reduce(escale[:, 4 + j:5 + j], stage[:, :], axis=X, op=ALU.max,
                                            apply_absolute_value=True).then_inc(stage_max, 1)

                def expert_lo(j):
                    dve.wait_ge(stage_hi, b * 3 + j + 1)
                    at_e = bass.ds(b, 1)
                    pick = (lambda a: w1s[:, at_e, a, j, :]) if j < KT else \
                        (lambda a: w2s[:, at_e, a, :, :].rearrange("p a k n -> p (a k n)"))
                    nc.vector.scalar_tensor_tensor(pick(1), stage[:, :] if j == KT else stage[:, :].unsqueeze(1), escale[:, 0:1],
                                                   pick(0), ALU.mult, ALU.subtract).then_inc(stage_lo, 1)

                def decay(g):
                    dve.wait_ge(scores_ready, 4 * t + g + 1)
                    if g >= 2 or later(t):
                        dve.wait_ge(values_done, 4 * t + g - 1)
                    nc.vector.scalar_tensor_tensor(sd[:, g % 2, :, :].rearrange("p h t -> p (h t)"), (A3, A4)[g % 2][:, :], s(C_S),
                                                   k32("decay")[:, 4 * g * C:4 * (g + 1) * C], ALU.mult, ALU.mult).then_inc(decayed, 1)

                if "project" in on:
                    dve.wait_ge(xT_hi, n + 1)
                    nc.vector.tensor_tensor(xT[:, 1, :, :].rearrange("p k t -> p (k t)"), A0[:, 0:D],
                                            xT[:, 0, :, :].rearrange("p k t -> p (k t)"), ALU.subtract).then_inc(xT_lo, 1)
                    if isinstance(n, int) and n == 0:
                        set_low(0)
                if "norm" in on:
                    dve.wait_ge(o_ready, tt + 1)
                    dve.wait_ge(gate_act, tt + 1)
                    nc.vector.scalar_tensor_tensor(y[:, :], th[:, tc % 2, :], 1.0, A5[:, 0:D], ALU.add, ALU.mult).then_inc(gated, 1)
                place(0)
                if "norm" in on:
                    dve.wait_ge(squared, tt + 1)
                    nc.vector.tensor_reduce(ssum, sq[:, :].rearrange("p (h e) -> p h e", e=HD), axis=X, op=ALU.add).then_inc(summed, 1)
                if "route" in on:
                    dve.wait_ge(rowsT_hi, uu + 1)
                    tok = slice(uc % 2 * C, (uc % 2 + 1) * C)
                    nc.vector.tensor_tensor(rT[:, uc // 2, 1, :, tok], A5[:, 0:D].rearrange("p (k t) -> p k t", k=KT),
                                            rT[:, uc // 2, 0, :, tok], ALU.subtract).then_inc(rowsT_lo, 1)
                if "attend" in on:
                    dve.wait_ge(stack_T, t + 1)
                    if isinstance(t, int) and t == 0:
                        dve.wait_ge(zeroed, 2)
                        dve.wait_ge(const_in[3], 16)
                    b16 = A1[:, :].bitcast(F16).rearrange("p (j t) -> p j t", t=C)
                    nc.vector.tensor_copy(qT[0:64, :, 0, :], b16[0:64, :, :]).then_inc(qT_low, 1)
                    nc.vector.tensor_tensor(qd[:, :, :].rearrange("p k t -> p (k t)"), A0[:, 0:D], k32("qdec"), ALU.mult)\
                        .then_inc(q_decayed, 1)
                place(1)
                if "route" in on:
                    dve.wait_ge(logits_ready, uu + 1)
                    nc.vector.tensor_scalar(lg[:, :], A5[:, 0:EXPERTS], s(C_F), None, ALU.mult).then_inc(logits_copied, 1)
                    dve.wait_ge(logits_copied, uu + 1)
                    alone(dve)
                    nc.vector.max(m8[:, :], lg[:, :]).then_inc(top_step, 1)
                    dve.wait_ge(top_step, 3 * uu + 1)
                    alone(dve)
                    nc.vector.max_index(i8[:, :], m8[:, :], lg[:, :]).then_inc(top_step, 1)
                    nc.vector.tensor_copy(top_v[:, bass.ds(uu, 1), :], m8[:, 0:TOPK].unsqueeze(1))
                    dve.wait_ge(top_step, 3 * uu + 2)
                    nc.vector.tensor_copy(top_i[:, bass.ds(uu, 1), :], i8[:, 0:TOPK].unsqueeze(1)).then_inc(top_step, 1)
                if "attend" in on:
                    decay(0)
                    decay(1)
                if "look" in on:
                    ln1(*shift(b, c, 2))
                if "expert" in on:
                    if c <= 1:
                        expert_max(2 * c)
                    if c == 1:
                        dve.wait_ge(stage_max, b * 3 + 3)
                        nc.vector.tensor_reduce(escale[:, 7:8], escale[:, 4:7], axis=X, op=ALU.max).then_inc(exp_max, 1)
                    if c >= 2:
                        expert_lo(2 * (c - 2))
                if isinstance(t, int) and t == 0:
                    dve.wait_ge(set_in[1], 32)
                    for k in range(KT):
                        nc.vector.tensor_scalar(rawO[:, k * D:(k + 1) * D], rawO[:, k * D:(k + 1) * D], rawNW[:, k:k + 1], None,
                                                ALU.mult).then_inc(nw_folded, 1)
                    dve.wait_ge(nw_folded, 2)
                    set_largest(1)
                    dve.wait_ge(set_in[2], 64)
                    set_largest(2)
                if "project" in on:
                    dve.wait_ge(qk_act, n + 1)
                    a, r, o4 = halves(qk[:, :]), halves(rs[:, :]), halves(rc[:, :])
                    sin = k32("sin")[:, nc_ * 8:(nc_ + 1) * 8].unsqueeze(1).broadcast_to((P, 2 * HEADS, HD // 2))
                    nc.vector.tensor_tensor(r[:, :, 0, :], a[:, :, 1, :], sin, ALU.mult).then_inc(rope_sin, 1)
                    nc.vector.tensor_tensor(r[:, :, 1, :], a[:, :, 0, :], sin, ALU.mult).then_inc(rope_sin, 1)
                    dve.wait_ge(v_copied, n + 1)
                    if isinstance(n, int) and n == 0:
                        dve.wait_ge(zeroed, 2)
                    nc.vector.tensor_copy(
                        vw[:, nc_ % 2, :, :].rearrange("p (j a) (b e) -> p j (a b) e", a=2, b=2)[:, :, 0:4:3, :],
                        vn[:, nc_ % 2, :].rearrange("p (j a e) -> p j a e", a=2, e=HD)).then_inc(v_spread, 1)
                if "norm" in on:
                    dve.wait_ge(nT_hi, tt + 1)
                    nc.vector.tensor_tensor(nT[:, 1, :, :].rearrange("p k t -> p (k t)"), A5[:, 0:D],
                                            nT[:, 0, :, :].rearrange("p k t -> p (k t)"), ALU.subtract).then_inc(nT_lo, 1)
                place(2)
                if "attend" in on:
                    decay(2)
                    decay(3)
                if "project" in on:
                    dve.wait_ge(rope_cos, n + 1)
                    dve.wait_ge(rope_sin, 2 * n + 2)
                    nc.vector.tensor_tensor(a[:, :, 0, :], o4[:, :, 0, :], r[:, :, 0, :], ALU.subtract).then_inc(rotated, 1)
                    nc.vector.tensor_tensor(a[:, :, 1, :], o4[:, :, 1, :], r[:, :, 1, :], ALU.add).then_inc(rotated, 1)
                if "look" in on:
                    xs_rows(*shift(b, c, 2))
                if "norm" in on:
                    dve.wait_ge(attn_ready, tt + 1)
                    nc.vector.bn_stats(st2, A5[:, 0:D]).then_inc(ln2_stats, 1)
                    dve.wait_ge(ln2_stats, tt + 1)
                    alone(dve)
                    nc.vector.bn_aggr(mv2, st2).then_inc(ln2_mv, 1)
                if "project" in on:
                    dve.wait_ge(qk_hi, n + 1)
                    flat = st[:, :, :, :, :].rearrange("p a h i e -> p (a h) i e")
                    nc.vector.scalar_tensor_tensor(flat[:, :, 1, :], qk[:, :].rearrange("p (h e) -> p h e", e=HD), s(S_Q),
                                                   flat[:, :, 0, :], ALU.mult, ALU.subtract).then_inc(qk_lo, 1)
                    nc.vector.tensor_copy(st[:, 0, :, 3, :], st[:, 0, :, 0, :]).then_inc(stacked, 1)
                    dve.wait_ge(qk_lo, n + 1)
                    nc.vector.tensor_copy(st[:, 0, :, 2, :], st[:, 0, :, 1, :]).then_inc(stacked, 1)
                    nc.vector.tensor_copy(st[:, 1, :, 2:4, :], st[:, 1, :, 0:2, :]).then_inc(stacked, 1)
                place(3)
                if isinstance(t, int) and t == 0:
                    dve.wait_ge(set_all, 2)
                    powers(1, 3)
                    chain(nc.vector.tensor_tensor(sc[:, T1_:T1_ + 1], pw[:, 2:3], pw[:, 2:3], ALU.mult))
                    times((S_O, rp[:, 1:2], 2.0 ** 14), (C_O, pw[:, 1:2], 2.0 ** -26), (S_F, rp[:, 2:3], 2.0 ** 14),
                          (C_F, pw[:, 2:3], 2.0 ** -24), (C_FU, rp[:, 2:3], 2.0 ** -27))
                    chain(nc.vector.tensor_tensor(s(C_O2), s(C_O), s(C_O), ALU.mult))
                    chain(nc.vector.scalar_tensor_tensor(s(C_FD), s(T1_), 2.0 ** -11, pw[:, 2:3], ALU.mult, ALU.mult))
                    dve.sem_inc(set_scaled, 2)
                    set_low(1)
                    set_low(2)
                if "attend" in on and c < CPS - 1:
                    dve.wait_ge(update_ready, 3 * b + c + 1)
                    kept = state[:, :, :].rearrange("p k t -> p (k t)")
                    if c == 0:
                        nc.vector.tensor_tensor(kept, A3[:, 0:D], k32("block"), ALU.mult).then_inc(state_masked, 1)
                        dve.wait_ge(state_masked, 3 * b + 1)
                        dve.sem_inc(state_new, 1)
                    else:
                        nc.vector.tensor_tensor(sq[:, :], A3[:, 0:D], k32("block"), ALU.mult).then_inc(state_masked, 1)
                        dve.wait_ge(state_masked, 3 * b + c + 1)
                        dve.wait_ge(state_old, 2 * b + c)
                        nc.vector.tensor_tensor(kept, kept, sq[:, :], ALU.add).then_inc(state_new, 1)
                if "norm" in on:
                    dve.wait_ge(x1_ready, tt + 1)
                    nc.vector.bn_stats(st3, x1[:, :]).then_inc(ln3_stats, 1)
                    dve.wait_ge(ln3_stats, tt + 1)
                    alone(dve)
                    nc.vector.bn_aggr(mv3, st3).then_inc(ln3_mv, 1)
                if "expert" in on and c == 0:
                    expert_max(1)
                if "expert" in on and c == 2:
                    expert_lo(1)
                if "expert" in on and c == 1:
                    e = escale
                    n0 = b * 5
                    dve.wait_ge(exp_all, b + 1)

                    def link(i, ins):
                        ins.then_inc(exp_step, 1)
                        dve.wait_ge(exp_step, n0 + i)

                    link(1, nc.vector.tensor_scalar(e[:, 4:5], e[:, 4:5], 2.0 ** -30, 2.0 ** 30, ALU.max, ALU.min))
                    link(2, nc.vector.tensor_scalar(e[:, 5:6].bitcast(I32), e[:, 4:5].bitcast(I32), 0x7F800000, None, ALU.bitwise_and))
                    link(3, nc.vector.reciprocal(e[:, 6:7], e[:, 5:6]))
                    nc.vector.tensor_scalar(e[:, 0:1], e[:, 6:7], 2.0 ** 14, None, ALU.mult)
                    nc.vector.tensor_scalar(e[:, 1:2], e[:, 5:6], 2.0 ** -24, None, ALU.mult)
                    nc.vector.tensor_scalar(e[:, 2:3], e[:, 6:7], 2.0 ** -27, None, ALU.mult)
                    link(4, nc.vector.tensor_tensor(e[:, 3:4], e[:, 5:6], e[:, 5:6], ALU.mult))
                    link(5, nc.vector.scalar_tensor_tensor(e[:, 3:4], e[:, 3:4], 2.0 ** -11, e[:, 5:6], ALU.mult, ALU.mult))
                    nc.vector.tensor_copy(exp_scale[:, bass.ds(b, 1), :], e[:, 0:4].unsqueeze(1)).then_inc(exp_scaled, 1)
                if "norm" in on:
                    dve.wait_ge(ln3_step, 2 * tt + 2)
                    if later(tt):
                        dve.wait_ge(rows_out, 16 * tt)
                    nc.vector.tensor_scalar(rows[:, :], x1[:, :], mv3[:, 0:1], r3[:, 1:2],
                                            ALU.subtract, ALU.mult).then_inc(rows_ready, 1)
                place(4)

            run_slots(dve, slot)

            pool_width = TILES + 1
            done = [0]

            def then(ins, after=True):
                done[0] += 1
                ins.then_inc(route, 1)
                if after:
                    dve.wait_ge(route, done[0])

            dve.wait_ge(top_step, 3 * CHUNKS)
            for k in range(TOPK):
                then(nc.vector.tensor_tensor(picks[k][:, :, :], k32("iota8").unsqueeze(1).broadcast_to((P, CHUNKS, EXPERTS)),
                                             top_i[:, :, k].unsqueeze(2).broadcast_to((P, CHUNKS, EXPERTS)), ALU.is_equal))
            then(nc.vector.tensor_tensor(both[:, :].rearrange("p (c e) -> p c e", e=EXPERTS), picks[0][:, :, :], picks[1][:, :, :],
                                         ALU.add))
            then(nc.vector.tensor_tensor(diff[:, :], top_v[:, :, 0], top_v[:, :, 1], ALU.subtract))
            dve.wait_ge(route_act, 1)
            then(nc.vector.tensor_scalar(weight[:, :, 0], diff[:, :], 0.5, 0.5, ALU.mult, ALU.add))
            then(nc.vector.tensor_scalar(weight[:, :, 1], diff[:, :], -0.5, 0.5, ALU.mult, ALU.add))
            dve.wait_ge(route_pe, 1)
            total, a, b_ = counts
            psum3 = [bank[:, 0:CHUNKS * EXPERTS].rearrange("p (c e) -> p c e", e=EXPERTS) for bank in (A0, A1)]
            then(nc.vector.tensor_copy(total[:, :, :], psum3[1]))

            def running(src, bufs, n):
                step = 1
                k = 0
                while step < n:
                    dst = bufs[k % 2]
                    then(nc.vector.tensor_copy(dst[:, 0:step], src[:, 0:step]))
                    then(nc.vector.tensor_tensor(dst[:, step:n], src[:, step:n], src[:, 0:n - step], ALU.add))
                    src, step, k = dst, step * 2, k + 1
                return src

            summed_c = running(total, (a, b_), CHUNKS)
            spare = a if summed_c is b_ else b_
            count = summed_c[:, CHUNKS - 1, :]
            then(nc.vector.tensor_scalar(filled_i[:, :], count, float(P - 1), None, ALU.add))
            then(nc.vector.tensor_scalar(filled_i[:, :], filled_i[:, :], 7, None, ALU.logical_shift_right))
            then(nc.vector.tensor_copy(filled[0][:, :], filled_i[:, :]))
            until = running(filled[0], (filled[1], filled[2]), EXPERTS)
            then(nc.vector.tensor_tensor(filled[3][:, :], until[:, :], filled[0][:, :], ALU.subtract))
            then(nc.vector.tensor_scalar(filled[3][:, :], filled[3][:, :], float(P), None, ALU.mult))
            then(nc.vector.tensor_tensor(place_of[:, :, :], summed_c[:, :, :], total[:, :, :], ALU.subtract))
            then(nc.vector.tensor_tensor(spare[:, :, :], place_of[:, :, :], psum3[0], ALU.add))
            then(nc.vector.tensor_tensor(place_of[:, :, :], spare[:, :, :], filled[3][:, :].unsqueeze(1).broadcast_to((P, CHUNKS, EXPERTS)),
                                         ALU.add))
            for k in range(TOPK):
                then(nc.vector.tensor_tensor(prod[:, :, :], picks[k][:, :, :], place_of[:, :, :], ALU.mult))
                then(nc.vector.tensor_reduce(spot[:, k, :], prod[:, :, :], axis=X, op=ALU.add))
            then(nc.vector.tensor_copy(spot_i[:, :, :], spot[:, :, :]))
            then(nc.vector.tensor_scalar(spot_t[:, :, :], spot_i[:, :, :], 7, None, ALU.logical_shift_right))
            then(nc.vector.tensor_scalar(spot_r[:, :, :], spot_i[:, :, :], P - 1, None, ALU.bitwise_and))
            then(nc.vector.tensor_copy(tile_f[:, :, :], spot_t[:, :, :]))
            then(nc.vector.tensor_copy(row_f[:, :, :], spot_r[:, :, :]))
            dve.sem_inc(route_pool, 1)
            for i in range(TOPK * CHUNKS):
                k, c = i % TOPK, i // TOPK
                if i >= 4:
                    dve.wait_ge(hot_used, i - 3)
                nc.vector.tensor_scalar(hot_r[:, i % 4, :], k16("iota"), row_f[:, k, c:c + 1], None, ALU.is_equal).then_inc(hot_ready, 1)
                nc.vector.tensor_scalar(hot_t[:, i % 4, 0, :], k32("iotat"), tile_f[:, k, c:c + 1], k32("tok")[:, k:k + 1],
                                        ALU.is_equal, ALU.mult).then_inc(hot_ready, 1)
            then(nc.vector.tensor_tensor(cmp[:, :, :], k32("iotat").unsqueeze(2).broadcast_to((P, pool_width, EXPERTS - 1)),
                                         until[:, 0:EXPERTS - 1].unsqueeze(1).broadcast_to((P, pool_width, EXPERTS - 1)), ALU.is_ge))
            then(nc.vector.tensor_reduce(owner_f[:, :], cmp[:, :, :], axis=X, op=ALU.add))
            nc.vector.tensor_copy(owner[:, :], owner_f[:, :]).then_inc(owners_ready, 1)
            dve.wait_ge(hot_used, TOPK * CHUNKS)
            then(nc.vector.tensor_copy(ids2[:, :, :].rearrange("p a t -> p (a t)"), A2[:, 0:2 * pool_width]))
            then(nc.vector.tensor_tensor(idv[:, :], ids2[:, 0, :], ids2[:, 1, :], ALU.add))
            then(nc.vector.tensor_scalar(idz[:, :], idv[:, :], 0.0, float(FAR), ALU.is_equal, ALU.mult))
            then(nc.vector.scalar_tensor_tensor(sca[:, :], idv[:, :], -1.0, idz[:, :], ALU.add, ALU.add))
            then(nc.vector.tensor_scalar(gat_i[:, :], idv[:, :], -1.0, 0.0, ALU.add, ALU.max))
            nc.vector.tensor_scalar(gat[:, :], gat_i[:, :], 1, None, ALU.logical_shift_right).then_inc(ids_ready, 1)

            dve.wait_ge(owners_ready, 1)

            def rows_lo(j, i):
                dve.wait_ge(eT_hi, j + 1)
                nc.vector.tensor_tensor(eT[:, i % 2, 1, :, :].rearrange("p k t -> p (k t)"), A5[:, 0:D],
                                        eT[:, i % 2, 0, :, :].rearrange("p k t -> p (k t)"), ALU.subtract).then_inc(eT_lo, 1)

            rows_lo(0, 0)

            def tile_slot(j, i, m):
                if has(j, 0):
                    e = dve.value_load(owner[0:1, bass.ds(j, 1)], min_val=0, max_val=EXPERTS - 1)
                    dve.wait_ge(gu_ready, 2 * j + 2)
                    dve.wait_ge(e_silu, j + 1)
                    nc.vector.scalar_tensor_tensor(eg[:, i % 2, :], (A1, A3)[i % 2][:, :],
                                                   exp_scale[:, bass.ds(e, 1), 2:3].rearrange("p a b -> p (a b)"), eg[:, i % 2, :],
                                                   ALU.mult, ALU.mult).then_inc(e_act, 1)
                if has(j, -1):
                    dve.wait_ge(ea_hi, j)
                    nc.vector.tensor_tensor(eaT[:, (i - 1) % 2, 1, :, :].rearrange("p q t -> p (q t)"), A4[:, :],
                                            eaT[:, (i - 1) % 2, 0, :, :].rearrange("p q t -> p (q t)"), ALU.subtract).then_inc(ea_lo, 1)
                if has(j, 1):
                    rows_lo(j + 1, i + 1)

            run_tiles(dve, tile_slot)

            def combine(g, par, n):
                dve.wait_ge(c_in[par], (n + 1) * 48)
                for q in range(4):
                    for k in range(TOPK):
                        z_in = cs[:, par, q, :] if k == 0 else cz[:, par, q, :]
                        nc.vector.scalar_tensor_tensor(cz[:, par, q, :], cp[:, par, q, k, :],
                                                       weight[:, bass.ds(g * 4 + q, 1), k:k + 1].rearrange("p a b -> p (a b)"), z_in,
                                                       ALU.mult, ALU.add).then_inc(c_sum, 1)
                        dve.wait_ge(c_sum, g * 8 + 2 * q + k + 1)
                    nc.vector.bn_stats(cst[:, q, :], cz[:, par, q, :]).then_inc(c_stats, 1)
                for q in range(4):
                    dve.wait_ge(c_stats, g * 4 + q + 1)
                    alone(dve)
                    nc.vector.bn_aggr(cmv[:, q, :], cst[:, q, :]).then_inc(c_mv, 1)
                dve.wait_ge(c_rstd, g + 1)
                nc.vector.scalar_tensor_tensor(cr[:, :, 2], cmv[:, :, 0], -1.0, cr[:, :, 1], ALU.mult, ALU.mult).then_inc(c_shift, 1)

            with dve.Fori(0, SEQS // 2) as n:
                for par in range(2):
                    combine(n * 2 + par, par, n)

        @block.gpsimd
        def _(pool):
            def ln1(b, c):
                t = at(b, c)
                pool.wait_ge(ln1_mv, t + 1)
                if later(t):
                    pool.wait_ge(xs_ready, t)
                alone(pool)
                nc.gpsimd.tensor_scalar(r1[:, 0:1], mv1[:, 1:2], LN_EPS, XS ** -2, ALU.add, ALU.mult).then_inc(ln1_var, 1)
                pool.wait_ge(ln1_var, t + 1)
                nc.gpsimd.tensor_tensor(r1[:, 1:2], r1[:, 0:1], mhalf[:, 0:1], ALU.pow).then_inc(ln1_pow, 1)

            pool.wait_ge(const_in[0], 16)
            ln1(0, 0)
            pool.wait_ge(set_max, 1)
            alone(pool)
            nc.gpsimd.partition_all_reduce(gmax[:, 0:1], pmax[:, 0:1], P, ABSMAX).then_inc(set_all, 1)

            def slot(b, c, on):
                t, n = at(b, c), at(*shift(b, c, 1))
                nc_ = (c + 1) % CPS
                tb, tc = shift(b, c, -1)
                tt = at(tb, tc)
                if "norm" in on:
                    pool.wait_ge(summed, tt + 1)
                    alone(pool)
                    nc.gpsimd.tensor_scalar(smean, ssum, 1.0 / (4 * HD) * (NS / 2) ** -2, RMS_EPS * (NS / 2) ** -2, ALU.mult, ALU.add)\
                        .then_inc(rms_mean, 1)
                    pool.wait_ge(rms_mean, tt + 1)
                    nc.gpsimd.tensor_tensor(srms, smean, mhalf, ALU.pow).then_inc(rms_pow, 1)
                    pool.wait_ge(rms_pow, tt + 1)
                    y3 = y[:, :].rearrange("p (h e) -> p h e", e=HD)
                    nc.gpsimd.tensor_tensor(y3, y3, srms.unsqueeze(2).broadcast_to((P, HEADS, HD)), ALU.mult).then_inc(normed, 1)
                if isinstance(t, int) and t == 0:
                    pool.wait_ge(const_in[3], 16)
                if "expert" in on and c == 1:
                    pool.wait_ge(exp_max, b + 1)
                    alone(pool)
                    nc.gpsimd.partition_all_reduce(escale[:, 4:5], escale[:, 7:8], P, ABSMAX).then_inc(exp_all, 1)
                if "look" in on:
                    ln1(*shift(b, c, 2))
                if "project" in on:
                    pool.wait_ge(qk_act, n + 1)
                    if later(n):
                        pool.wait_ge(rotated, 2 * n)
                    cos = k32("cos")[:, nc_ * 8:(nc_ + 1) * 8].unsqueeze(1).broadcast_to((P, 4 * HEADS, HD // 2))
                    nc.gpsimd.tensor_tensor(rc[:, :].rearrange("p (h e) -> p h e", e=HD // 2),
                                            qk[:, :].rearrange("p (h e) -> p h e", e=HD // 2), cos, ALU.mult).then_inc(rope_cos, 1)
                    pool.wait_ge(rotated, 2 * n + 2)
                    nc.gpsimd.tensor_tensor(kd[:, nc_ % 2, :].rearrange("p (h e) -> p h e", e=HD), qk[:, D:].rearrange("p (h e) -> p h e", e=HD),
                                            k32("kdec").unsqueeze(2).broadcast_to((P, HEADS, HD)), ALU.mult).then_inc(k_decayed, 1)
                if "attend" in on and 1 <= c < CPS - 1:
                    pool.wait_ge(update_ready, 3 * b + c + 1)
                    nc.gpsimd.tensor_tensor(state[:, :, :].rearrange("p k t -> p (k t)"), state[:, :, :].rearrange("p k t -> p (k t)"),
                                            k32("blocklam"), ALU.mult).then_inc(state_old, 1)
                if "norm" in on:
                    n0 = 4 * tt
                    pool.wait_ge(ln2_mv, tt + 1)
                    alone(pool)
                    nc.gpsimd.tensor_scalar(r2[:, 0:1], mv2[:, 1:2], s(C_O2), LN_EPS, ALU.mult, ALU.add).then_inc(ln2_step, 1)
                    pool.wait_ge(ln2_step, n0 + 1)
                    nc.gpsimd.tensor_tensor(r2[:, 1:2], r2[:, 0:1], mhalf[:, 0:1], ALU.pow).then_inc(ln2_step, 1)
                    pool.wait_ge(ln2_step, n0 + 2)
                    alone(pool)
                    nc.gpsimd.tensor_scalar(r2[:, 2:3], r2[:, 1:2], s(C_O), None, ALU.mult).then_inc(ln2_step, 1)
                    pool.wait_ge(ln2_step, n0 + 3)
                    alone(pool)
                    nc.gpsimd.tensor_scalar(r2[:, 3:4], mv2[:, 0:1], r2[:, 2:3], -1.0, ALU.mult, ALU.mult).then_inc(ln2_step, 1)
                if isinstance(t, int) and t == 0:
                    pool.wait_ge(set_max, 3)
                    alone(pool)
                    nc.gpsimd.partition_all_reduce(gmax[:, 1:3], pmax[:, 1:3], P, ABSMAX).then_inc(set_all, 1)
                if "norm" in on:
                    pool.wait_ge(attn_normed, tt + 1)
                    nc.gpsimd.tensor_tensor(x1[:, :], x1[:, :], xin[:, tc, :], ALU.add).then_inc(x1_ready, 1)
                    pool.wait_ge(ln3_mv, tt + 1)
                    alone(pool)
                    nc.gpsimd.tensor_scalar(r3[:, 0:1], mv3[:, 1:2], LN_EPS, XS ** -2, ALU.add, ALU.mult).then_inc(ln3_step, 1)
                    pool.wait_ge(ln3_step, 2 * tt + 1)
                    nc.gpsimd.tensor_tensor(r3[:, 1:2], r3[:, 0:1], mhalf[:, 0:1], ALU.pow).then_inc(ln3_step, 1)

            run_slots(pool, slot)

            pool.wait_ge(route_pool, 1)
            for i in range(TOPK * CHUNKS):
                k, c = i % TOPK, i // TOPK
                if i >= 4:
                    pool.wait_ge(hot_used, i - 3)
                alone(pool)
                nc.gpsimd.tensor_scalar(hot_t[:, i % 4, 1, :], k32("iotat"), tile_f[:, k, c:c + 1], float(TOPK * C * c),
                                        ALU.is_equal, ALU.mult).then_inc(hot_pool, 1)
            pool.wait_ge(ids_ready, 1)
            pool.wait_ge(rows_out, 16 * CHUNKS)

            def gather(j, i, m):
                if not isinstance(j, int) or j >= 4:
                    pool.wait_ge(eT_ready, j - 3)
                    pool.wait_ge(gathered[i % 4], 16 * (m + i // 4))
                alone(pool)
                nc.gpsimd.tensor_copy(gidx[:, i % 4:i % 4 + 1], gat[:, bass.ds(j, 1)]).then_inc(index_set, 1)
                return i % 4

            def gather_start(i):
                nc.gpsimd.indirect_dma_start(out=got[i][:, :], out_offset=None, in_=rows_d[:, :],
                                             in_offset=bass.IndirectOffsetOnAxis(ap=gidx[:, i:i + 1], axis=0)).then_inc(gathered[i], 16)

            for j in range(3):
                i = gather(j, j, 0)
                pool.wait_ge(index_set, j + 1)
                alone(pool)
                gather_start(i)

            def tile_slot(j, i, m):
                base = 3 + (min(j, TILES - 3) + max(j - 3, 0) if isinstance(j, int) else j + j - 3)
                if has(j, 3):
                    gi = gather(j + 3, i + 3, m)
                    base = base + 1
                    pool.wait_ge(index_set, base)
                    alone(pool)
                    gather_start(gi)
                if has(j, -3):
                    pool.wait_ge(res_copied, j - 2)
                    alone(pool)
                    nc.gpsimd.tensor_copy(sidx[:, (i - 3) % 4:(i - 3) % 4 + 1], sca[:, bass.ds(j - 3, 1)]).then_inc(index_set, 1)
                    base = base + 1
                    pool.wait_ge(index_set, base)
                    alone(pool)
                    nc.gpsimd.indirect_dma_start(out=picked_d[:, :], in_=res[(i - 3) % 4][:, :], in_offset=None,
                                                 out_offset=bass.IndirectOffsetOnAxis(ap=sidx[:, (i - 3) % 4:(i - 3) % 4 + 1], axis=0),
                                                 bounds_check=TOKENS * TOPK - 1, oob_is_err=False).then_inc(scattered[(i - 3) % 4], 16)

            run_tiles(pool, tile_slot)
            tile_slot(TILES + 2, (TILES + 2) % 4, 0)

            def residual(g, par):
                pool.wait_ge(c_mv, g * 4 + 4)
                alone(pool)
                nc.gpsimd.tensor_scalar(cr[:, :, 0], cmv[:, :, 1], LN_EPS, None, ALU.add).then_inc(c_var, 1)
                pool.wait_ge(c_var, g + 1)
                nc.gpsimd.tensor_tensor(cr[:, :, 1], cr[:, :, 0], mhalf[:, 0:4], ALU.pow).then_inc(c_rstd, 1)
                for q in range(4):
                    pool.wait_ge(c_norm, g * 4 + q + 1)
                    nc.gpsimd.tensor_tensor(cz[:, par, q, :], cz[:, par, q, :], cx[:, par, q, :], ALU.add).then_inc(c_done, 1)

            with pool.Fori(0, SEQS // 2) as n:
                for par in range(2):
                    residual(n * 2 + par, par)


_INS = ["L0_attn_x", "L0_attn_Wq", "L0_attn_Wk", "L0_attn_Wv", "L0_attn_Wo", "L0_attn_Wg1", "L0_attn_Wg2",
        "L0_attn_norm_weight", "L0_ffn_router_w", "L0_ffn_w1", "L0_ffn_w2", "L0_ffn_w_gate", "L0_ffn_w_up",
        "L0_ffn_w_down"]


def kernel(**inputs):
    import numpy as _np
    import concourse.bacc as _bacc
    from concourse import mybir as _mybir
    from concourse.bass_utils import run_bass_kernel_spmd as _run

    nc = _bacc.Bacc("TRN2", target_bir_lowering=False, num_devices=1)
    arrays, args = {}, []
    for name in _INS:
        a = _np.ascontiguousarray(inputs[name])
        arrays[f"in_{name}"] = a
        args.append(nc.dram_tensor(f"in_{name}", a.shape, _mybir.dt.from_np(a.dtype), kind="ExternalInput").ap())
    for name, a in zip(("const32", "const16"), tables()):
        arrays[name] = a
        args.append(nc.dram_tensor(name, a.shape, _mybir.dt.from_np(a.dtype), kind="ExternalInput").ap())
    args.append(nc.dram_tensor("out_0", (SEQS, SEQ, D), F32, kind="ExternalOutput").ap())
    layer_kernel(nc, *args)
    r = _run(nc, [arrays], core_ids=[0])
    return r.results[0]["out_0"]
```

```python
from contextlib import ExitStack

import concourse.bass as bass
import numpy as np
from concourse import mybir

P = 128
SEQS, SEQ, D = 8, 512, 256
TOKENS = SEQS * SEQ
C = P
CPS = SEQ // C
CHUNKS = TOKENS // C
HEADS, HD = 16, 16
KT = D // P
EXPERTS, TOPK, INTER = 8, 2, 512
SHARED = 2 * INTER
UNITS = CHUNKS // 2
PIECES = 10
TILES = TOKENS * TOPK // P + EXPERTS - 1
LN_EPS, RMS_EPS = 1e-5, 1e-6
XS = 2.0 ** 10
NS = 2.0 ** 12
FAR = 1 << 20

F32, F16, I32, U32 = mybir.dt.float32, mybir.dt.float16, mybir.dt.int32, mybir.dt.uint32
ACT, ALU = mybir.ActivationFunctionType, mybir.AluOpType
X = mybir.AxisListType.X
ABSMAX = bass.bass_isa.ReduceOp.absmax

_F32 = [("ident", P), ("kdec", HEADS), ("cos", CPS * 8), ("sin", CPS * 8), ("iota8", EXPERTS), ("tok", TOPK),
        ("mhalf", HEADS), ("iotat", TILES + 1), ("decay", HEADS * C), ("qdec", KT * C), ("block", KT * P),
        ("blocklam", KT * P)]
_F16 = [("ident", P), ("before", P), ("ones", P), ("iota", P)]


def offsets(parts):
    out, at = {}, 0
    for name, n in parts:
        out[name] = (at, at + n)
        at += n
    return out, at


C32, N32 = offsets(_F32)
C16, N16 = offsets(_F16)
SMALL = C32["decay"][0]


def tables():
    f = np.float32
    lam = -(f(2.0) ** (f(-8.0) * (np.arange(HEADS, dtype=f) + f(1.0)) / f(HEADS)))
    i = np.arange(C, dtype=f)
    t32 = {}
    diff = i[None, :] - i[:, None]
    dec = np.where(diff[:, None, :] >= 0, np.exp(lam[None, :, None] * np.maximum(diff, 0)[:, None, :]), 0)
    t32["decay"] = dec.reshape(P, HEADS * C)
    head = (np.arange(D) // HD).reshape(KT, P).T
    t32["qdec"] = np.exp(lam[head][:, :, None] * (i[None, None, :] + f(1))).reshape(P, KT * C)
    same = (np.arange(P)[:, None] // HD == np.arange(P)[None, :] // HD).astype(f)
    t32["block"] = np.repeat(same[:, None, :], KT, 1).reshape(P, KT * P)
    t32["blocklam"] = (same[:, None, :] * np.exp(lam * f(C))[head][:, :, None]).reshape(P, KT * P)
    t32["kdec"] = np.exp(lam[None, :] * (f(C - 1) - i[:, None]))
    theta = (f(10000.0) ** (f(-2.0) * np.arange(8, dtype=f) / f(HD))).astype(f)
    ang = (np.arange(SEQ, dtype=f)[:, None] * theta[None, :]).astype(f).reshape(CPS, C, 8).transpose(1, 0, 2)
    t32["cos"], t32["sin"] = np.cos(ang).reshape(P, -1), np.sin(ang).reshape(P, -1)
    t32["ident"] = np.eye(P)
    t32["iota8"] = np.broadcast_to(np.arange(EXPERTS), (P, EXPERTS))
    t32["tok"] = 2 * np.arange(P)[:, None] + np.arange(TOPK)[None, :] + 1
    t32["mhalf"] = np.full((P, HEADS), -0.5)
    t32["iotat"] = np.broadcast_to(np.arange(TILES + 1), (P, TILES + 1))
    t16 = {"ident": np.eye(P), "before": np.triu(np.ones((P, P)), 1), "ones": np.ones((P, P)),
           "iota": np.broadcast_to(np.arange(P), (P, P))}
    return (np.concatenate([np.asarray(t32[n], f) for n, _ in _F32], 1),
            np.concatenate([np.asarray(t16[n], np.float16) for n, _ in _F16], 1))


def layer_kernel(nc, x, wq, wk, wv, wo, wg1, wg2, norm_w, router, w1, w2, w_gate, w_up, w_down, c32d, c16d, out):
    whole = ExitStack()
    first = ExitStack()

    def sb(name, shape, dt=F32, stack=whole):
        return stack.enter_context(nc.sbuf_tensor(name, shape, dt))

    def sem(name):
        return whole.enter_context(nc.semaphore(name))

    rows_d = nc.dram_tensor("rows_d", (TOKENS, D), F32, kind="Internal").ap()
    res_d = nc.dram_tensor("res_d", (TOKENS, D), F32, kind="Internal").ap()
    shared_d = nc.dram_tensor("shared_d", (TOKENS, D), F32, kind="Internal").ap()
    picked_d = nc.dram_tensor("picked_d", (TOKENS * TOPK, D), F32, kind="Internal").ap()
    xf = x.rearrange("b n d -> (b n) d")
    outf = out.rearrange("b n d -> (b n) d")

    with whole:
        c32 = sb("c32", [P, N32])
        c16 = sb("c16", [P, N16], F16)

        def k32(name):
            return c32[:, C32[name][0]:C32[name][1]]

        def k16(name):
            return c16[:, C16[name][0]:C16[name][1]]

        w1s = sb("w1s", [P, EXPERTS, 2, KT, 2 * INTER], F16)
        w2s = sb("w2s", [P, EXPERTS, 2, INTER // P, D], F16)
        exp_scale = sb("exp_scale", [P, EXPERTS, 4])
        top_v = sb("top_v", [P, CHUNKS, TOPK])
        top_i = sb("top_i", [P, CHUNKS, TOPK])
        pmax = sb("pmax", [P, 4])
        gmax = sb("gmax", [P, 4])
        pw = sb("pw", [P, 4])
        rp = sb("rp", [P, 4])
        sc = sb("sc", [P, 16])
        (S_A, C_A, C_AH, S_Q, C_S, S_O, C_O, C_O2, S_F, C_F, C_FU, C_FD, T0_, T1_) = range(14)

        def s(col):
            return sc[:, col:col + 1]

        psum = [whole.enter_context(nc.psum_tensor(f"bank{i}", [P, 512], F32)) for i in range(8)]
        A0, A1, A2, A3, A4, A5, FB0, FB1 = psum
        FB = [FB0, FB1]

        const_in = [sem(f"const_in{i}") for i in range(4)]
        set_in = [sem(f"set_in{i}") for i in range(3)]
        zeroed, nw_folded, wg1_T, wg1_copied, wg_made, wg_copied = (sem("zeroed"), sem("nw_folded"), sem("wg1_T"),
            sem("wg1_copied"), sem("wg_made"), sem("wg_copied"))
        set_max, set_all, scale_step, set_scaled, pmax_zero, set_hi, set_lo = (sem("set_max"), sem("set_all"), sem("scale_step"),
            sem("set_scaled"), sem("pmax_zero"),
            sem("set_hi"), sem("set_lo"))
        x_in = [sem(f"x_in{i}") for i in range(CPS)]
        ln1_stats, ln1_mv, ln1_var, ln1_pow, ln1_shift, xs_ready = (sem("ln1_stats"), sem("ln1_mv"), sem("ln1_var"),
            sem("ln1_pow"), sem("ln1_shift"), sem("xs_ready"))
        xT_ready, xT_hi, xT_lo = sem("xT_ready"), sem("xT_hi"), sem("xT_lo")
        proj_ready, qk_act, gate_act, v_copied, v_spread = (sem("proj_ready"), sem("qk_act"), sem("gate_act"),
            sem("v_copied"), sem("v_spread"))
        rope_cos, rope_sin, rotated = sem("rope_cos"), sem("rope_sin"), sem("rotated")
        qk_hi, qk_lo, stacked = sem("qk_hi"), sem("qk_lo"), sem("stacked")
        k_decayed, stack_T, kstack_T, kT_copied, qT_low, qT_high, q_decayed = (sem("k_decayed"), sem("stack_T"), sem("kstack_T"),
            sem("kT_copied"), sem("qT_low"), sem("qT_high"), sem("q_decayed"))
        scores_ready, decayed, values_done = sem("scores_ready"), sem("decayed"), sem("values_done")
        update_ready, state_old, state_masked, state_new = (sem("update_ready"), sem("state_old"),
            sem("state_masked"), sem("state_new"))
        oT_copied, o_ready, gated, squared, summed = (sem("oT_copied"), sem("o_ready"), sem("gated"),
            sem("squared"), sem("summed"))
        rms_mean, rms_pow, normed = sem("rms_mean"), sem("rms_pow"), sem("normed")
        nT_ready, nT_hi, nT_lo, attn_ready = sem("nT_ready"), sem("nT_hi"), sem("nT_lo"), sem("attn_ready")
        ln2_stats, ln2_mv, ln2_step, attn_normed, x1_ready = (sem("ln2_stats"), sem("ln2_mv"), sem("ln2_step"),
            sem("attn_normed"), sem("x1_ready"))
        ln3_stats, ln3_mv, ln3_step, rows_ready = sem("ln3_stats"), sem("ln3_mv"), sem("ln3_step"), sem("rows_ready")
        rowsT_ready, rowsT_hi, rowsT_lo = sem("rowsT_ready"), sem("rowsT_hi"), sem("rowsT_lo")
        logits_ready, logits_copied, top_step = sem("logits_ready"), sem("logits_copied"), sem("top_step")
        x1_out, rows_out = sem("x1_out"), sem("rows_out")
        shared_out = sem("shared_out")
        piece_ready, piece_act, piece_free, act_hi, act_lo = (sem("piece_ready"), sem("piece_act"),
            sem("piece_free"), sem("act_hi"), sem("act_lo"))
        stage_in, stage_max, exp_max, exp_all, exp_scaled, exp_step, stage_hi, stage_lo = (
            sem("stage_in"), sem("stage_max"), sem("exp_max"), sem("exp_all"), sem("exp_scaled"), sem("exp_step"),
            sem("stage_hi"), sem("stage_lo"))

        route, route_pe, route_act = sem("route"), sem("route_pe"), sem("route_act")
        hot_ready, hot_used, owners_ready, ids_ready, spots_ready = (sem("hot_ready"), sem("hot_used"),
            sem("owners_ready"), sem("ids_ready"), sem("spots_ready"))
        index_set = sem("index_set")
        gathered = [sem(f"gathered{i}") for i in range(4)]
        scattered = [sem(f"scattered{i}") for i in range(4)]
        eT_ready, eT_hi, eT_lo, gu_ready, e_silu, e_act = (sem("eT_ready"), sem("eT_hi"), sem("eT_lo"), sem("gu_ready"),
            sem("e_silu"), sem("e_act"))
        aT_ready, ea_hi, ea_lo, res_ready, res_copied = (sem("aT_ready"), sem("ea_hi"), sem("ea_lo"), sem("res_ready"),
            sem("res_copied"))
        known_in, c_out = sem("known_in"), sem("c_out")
        picked_in = [sem(f"picked_in{i}") for i in range(4)]
        c_sum, c_stats, c_mv, c_var, c_rstd, c_shift, c_norm, c_done = (sem("c_sum"), sem("c_stats"), sem("c_mv"),
            sem("c_var"), sem("c_rstd"), sem("c_shift"), sem("c_norm"), sem("c_done"))

        passed = [sem("passed_dve"), sem("passed_pool")]

        def fb(name, shape, dt=F32):
            return sb(name, shape, dt, first)

        wA = fb("wA", [P, 2, KT, 4 * D], F16)
        wO = fb("wO", [P, 2, KT, D], F16)
        stage = fb("stage", [P, 1024])
        escale = fb("escale", [P, 8])
        xin = fb("xin", [P, CPS, D])
        xs = fb("xs", [P, D])
        xT = fb("xT", [P, 2, KT, C], F16)
        qk = fb("qk", [P, 2 * D])
        th = fb("th", [P, 2, D])
        vw = fb("vw", [P, 2, HEADS, 2 * HD])
        vn = fb("vn", [P, 2, D])
        rc = fb("rc", [P, 2 * D])
        rs = fb("rs", [P, 2 * D])
        st = fb("st", [P, 2, HEADS, 4, HD], F16)
        kd = fb("kd", [P, 2, D])
        qd = fb("qd", [P, KT, C])
        kT = fb("kT", [P, HEADS // 2, C], F16)
        qT = fb("qT", [P, HEADS // 2, 2, C], F16)
        sd = fb("sd", [P, 2, 4, C])
        state = fb("state", [P, KT, P])
        oT = fb("oT", [P, KT, C])
        y = fb("y", [P, D])
        sq = fb("sq", [P, D])
        nT = fb("nT", [P, 2, KT, C], F16)
        x1 = fb("x1", [P, D])
        rows = fb("rows", [P, D])
        small = fb("small", [P, 96])
        lg = fb("lg", [P, EXPERTS])
        m8 = fb("m8", [P, 8])
        i8 = fb("i8", [P, 8], U32)
        wF = fb("wF", [P, 2, 2 * KT * SHARED + SHARED // P * D + KT * EXPERTS], F16)
        rT = fb("rT", [P, 2, 2, KT, 2 * C], F16)
        sg = fb("sg", [P, 2, 2 * C])
        aT = fb("aT", [P, 2, SHARED // P, 2 * C], F16)
        ysh = fb("ysh", [P, D])
        wGU = wF[:, :, 0:2 * KT * SHARED].rearrange("p a (k n) -> p a k n", k=KT)
        wDn = wF[:, :, 2 * KT * SHARED:2 * KT * SHARED + SHARED // P * D].rearrange("p a (k n) -> p a k n", n=D)
        wR = wF[:, :, 2 * KT * SHARED + SHARED // P * D:].rearrange("p a (k n) -> p a k n", n=EXPERTS)
        st1, mv1, r1 = small[:, 0:6], small[:, 6:8], small[:, 80:83]
        st2, mv2, r2 = small[:, 10:16], small[:, 16:18], small[:, 18:22]
        st3, mv3, r3 = small[:, 22:28], small[:, 28:30], small[:, 83:86]
        ssum, smean, srms = small[:, 32:48], small[:, 48:64], small[:, 64:80]
        mhalf = k32("mhalf")
        first.close()

        picks = [sb(f"pick{k}", [P, CHUNKS, EXPERTS]) for k in range(TOPK)]
        both = sb("both", [P, CHUNKS * EXPERTS], F16)
        counts = [sb(f"counts{i}", [P, CHUNKS, EXPERTS]) for i in range(3)]
        place_of = sb("place_of", [P, CHUNKS, EXPERTS])
        filled = [sb(f"filled{i}", [P, EXPERTS]) for i in range(4)]
        filled_i = sb("filled_i", [P, EXPERTS], I32)
        spot = sb("spot", [P, TOPK, CHUNKS])
        spot_i, spot_t, spot_r = (sb("spot_i", [P, TOPK, CHUNKS], I32), sb("spot_t", [P, TOPK, CHUNKS], I32),
                                  sb("spot_r", [P, TOPK, CHUNKS], I32))
        tile_f, row_f = sb("tile_f", [P, TOPK, CHUNKS]), sb("row_f", [P, TOPK, CHUNKS])
        prod = sb("prod", [P, CHUNKS, EXPERTS])
        diff = sb("diff", [P, CHUNKS])
        weight = sb("weight", [P, CHUNKS, TOPK])
        owner_f, owner = sb("owner_f", [P, TILES + 1]), sb("owner", [P, TILES + 1], I32)
        hot_r = sb("hot_r", [P, 4, P], F16)
        hot_t = sb("hot_t", [P, 4, 2, TILES + 1], F16)
        ids2, idv, idz = sb("ids2", [P, 2, TILES + 1]), sb("idv", [P, TILES + 1]), sb("idz", [P, TILES + 1])
        gat_i, gat, sca = (sb("gat_i", [P, TILES + 1], I32), sb("gat", [P, TILES + 1], I32), sb("sca", [P, TILES + 1], I32))
        gidx, sidx = sb("gidx", [P, 4], I32), sb("sidx", [P, 4], I32)
        got = [sb(f"got{i}", [P, D]) for i in range(4)]
        eT = sb("eT", [P, 2, 2, KT, C], F16)
        eg = sb("eg", [P, 2, INTER])
        eaT = sb("eaT", [P, 2, 2, INTER // P, C], F16)
        cmp = eaT[:, :, :, :, :].rearrange("p a b q t -> p (a b q t)").bitcast(F32)[:, 0:(TILES + 1) * (EXPERTS - 1)]\
            .rearrange("p (t e) -> p t e", e=EXPERTS - 1)
        res = [sb(f"res{i}", [P, D]) for i in range(4)]
        vals = sb("vals", [P, CHUNKS, TOPK, 2])
        cst = picks[0][:, :, 0:6]
        cmv, cr = picks[1][:, :, 0:2], picks[1][:, :, 2:6]
        cx, cs = sb("cx", [P, CHUNKS, D]), sb("cs", [P, CHUNKS, D])

        def halves(ap):
            return ap.rearrange("p (h a e) -> p h a e", a=2, e=HD // 2)

        raw = w1s[:, 1:, :, :, :].rearrange("p a b c d -> p (a b c d)").bitcast(F32)
        cp = w1s[:, :, :, :, :].rearrange("p a b c d -> p (a b c d)").bitcast(F32)\
            .rearrange("p (c k n) -> p c k n", c=CHUNKS, k=TOPK)
        nA, nO, nF = KT * 4 * D, KT * D, 2 * KT * SHARED + SHARED // P * D + KT * EXPERTS
        rawA, rawO, rawF = raw[:, 0:nA], raw[:, nA:nA + nO], raw[:, nA + nO:nA + nO + nF]
        rawA3 = rawA.rearrange("p (k n) -> p k n", k=KT)
        rawGU = rawF[:, 0:2 * KT * SHARED].rearrange("p (k n) -> p k n", k=KT)
        rawDn = rawF[:, 2 * KT * SHARED:2 * KT * SHARED + SHARED // P * D].rearrange("p (k n) -> p k n", n=D)
        rawR = rawF[:, 2 * KT * SHARED + SHARED // P * D:].rearrange("p (k n) -> p k n", n=EXPERTS)
        rawG1 = raw[:, nA + nO + nF:nA + nO + nF + KT * HD].rearrange("p (k e) -> p k e", e=HD)
        rest = nA + nO + nF + KT * HD
        rawG1T, rawG2, rawNW = raw[0:HD, rest:rest + D], raw[0:HD, rest + D:rest + 2 * D], raw[:, rest + 2 * D:rest + 2 * D + KT]
        row = "(k p) n -> p k n"

        block = whole.enter_context(nc.Block())

        def alone(eng):
            eng.sem_inc(passed[0] if eng.engine == nc.vector.engine else passed[1], 1)

        def at(b, c):
            return b * CPS + c

        def shift(b, c, by):
            return b + (c + by) // CPS, (c + by) % CPS

        SET_SPLIT = (2, 3, 7)

        def set_parts(i):
            n, width = ((2, nA), (1, nO), (4, nF))[i]
            return [slice(p * width // n, (p + 1) * width // n) for p in range(n)]

        def later(t, first=1):
            return not isinstance(t, int) or t >= first

        ODD = [[9], [0], [1], [2], [3], [4]]
        EVEN = [[5], [6], [7], ["split"], [8], []]
        carried = [p for p in ("split", 8, 9) if p in sum(ODD, [])]

        def pieces(b, c, place):
            if c % 2:
                unit, parity = 2 * b - 1 + c // 2, 1 - c // 2
                first = isinstance(unit, int) and unit == 0
                return [(unit - 1, 1 - parity, p) if p in carried else (unit, parity, p)
                        for p in ODD[place] if not (first and p in carried)]
            unit, parity = 2 * b - 2 + c // 2, c // 2
            final = isinstance(unit, int) and unit == UNITS - 1 and place == 5
            return [(unit, parity, p) for p in EVEN[place] + (carried if final else [])]

        def run_slots(eng, slot, end=CHUNKS + 3):
            whole_slot = {"look", "project", "attend", "norm", "route", "ffn", "expert"}

            def peeled(n):
                on = {part for part, by in (("look", 2), ("project", 1), ("attend", 0), ("norm", -1), ("route", -2))
                      if 0 <= n + by < CHUNKS}
                slot(n // CPS, n % CPS, on | ({"ffn"} if n >= 3 else set()) | ({"expert"} if 0 <= n < CHUNKS else set()))

            for n in range(-1, CPS):
                peeled(n)
            with eng.Fori(1, SEQS - 1) as b:
                for c in range(CPS):
                    slot(b, c, whole_slot)
            for n in range(CHUNKS - CPS, end):
                peeled(n)

        def run_tiles(eng, slot):
            for j in range(8):
                slot(j, j % 4, j // 4)
            with eng.Fori(2, TILES // 4) as m:
                for i in range(4):
                    slot(m * 4 + i, i, m)
            for j in range(TILES // 4 * 4, TILES + 2):
                slot(j, j % 4, j // 4)

        def has(j, shift):
            return not isinstance(j, int) or 0 <= j + shift < TILES

        @block.sync
        def _(sp):
            def load_x(b, c):
                sp.dma_start(xin[:, c, :], xf[bass.ds(at(b, c) * C, C), :]).then_inc(x_in[c], 16)

            sp.sem_inc(shared_out, 16)
            load_x(0, 0)
            sp.dma_start(c32[:, 0:SMALL], c32d[:, 0:SMALL]).then_inc(const_in[0], 16)
            sp.dma_start(rawG1, wg1.rearrange(row, p=P)).then_inc(const_in[2], 16)
            sp.dma_start(rawG2, wg2).then_inc(const_in[2], 16)
            for i, w in enumerate((wq, wk, wv)):
                sp.dma_start(rawA3[:, :, i * D:(i + 1) * D], w.rearrange(row, p=P)).then_inc(set_in[0], 16)
            load_x(0, 1)
            sp.dma_start(c16[:, :], c16d).then_inc(const_in[1], 16)
            sp.dma_start(c32[:, SMALL:], c32d[:, SMALL:]).then_inc(const_in[3], 16)
            sp.dma_start(rawO.rearrange("p (k n) -> p k n", k=KT), wo.rearrange(row, p=P)).then_inc(set_in[1], 16)
            with nc.allow_non_contiguous_dma(reason="256 values"):
                sp.dma_start(rawNW, norm_w.rearrange("(k p) -> p k", p=P)).then_inc(set_in[1], 16)
            for c in range(2, CPS):
                load_x(0, c)
            for i, w in enumerate((w_gate, w_up)):
                sp.dma_start(rawGU[:, :, i * SHARED:(i + 1) * SHARED], w.rearrange(row, p=P)).then_inc(set_in[2], 16)
            sp.dma_start(rawDn, w_down.rearrange(row, p=P)).then_inc(set_in[2], 16)
            sp.dma_start(rawR, router.rearrange(row, p=P)).then_inc(set_in[2], 16)

            def load_expert(e, i):
                if i == 0:
                    if not isinstance(e, int) or e:
                        sp.wait_ge(stage_lo, e * 3)
                elif i <= 3:
                    sp.wait_ge(stage_max, e * 3 + i)
                else:
                    sp.wait_ge(stage_lo, e * 3 + (i - 3))
                j = i % 3
                src = w1[bass.ds(e, 1), j * P:(j + 1) * P, :].rearrange("a p n -> p (a n)") if j < KT else \
                    w2[bass.ds(e, 1), :, :].rearrange("a (k p) n -> p (a k) n", p=P)
                dst = stage[:, :] if j < KT else stage[:, :].rearrange("p (k n) -> p k n", n=D)
                sp.dma_start(dst, src).then_inc(stage_in, 16)

            def store_shared(unit, i):
                sp.wait_ge(piece_free, unit * PIECES + 9 + i)
                sp.dma_start(shared_d[bass.ds(unit * 2 * C + i * C, C), :], ysh[:, :]).then_inc(shared_out, 16)

            def slot(b, c, on):
                if "ffn" in on:
                    for place in range(3):
                        for unit, _, p in pieces(b, c, place):
                            if p in (8, 9):
                                store_shared(unit, p - 8)
                if "route" in on:
                    u = at(*shift(b, c, -2))
                    sp.wait_ge(rows_ready, u + 1)
                    sp.dma_start(rows_d[bass.ds(u * C, C), :], rows[:, :]).then_inc(rows_out, 16)
                if "expert" in on:
                    for i in ([0, 1], [2], [], [5])[c]:
                        load_expert(b, i)
                if "norm" in on:
                    tb, tc = shift(b, c, -1)
                    t = at(tb, tc)
                    sp.wait_ge(x1_ready, t + 1)
                    sp.dma_start(res_d[bass.ds(t * C, C), :], x1[:, :]).then_inc(x1_out, 16)
                    if not isinstance(tb, int) or tb < SEQS - 1:
                        load_x(tb + 1, tc)
                if "ffn" in on:
                    for place in range(3, 6):
                        for unit, _, p in pieces(b, c, place):
                            if p in (8, 9):
                                store_shared(unit, p - 8)
                if "expert" in on:
                    for i in ([], [3], [4], [])[c]:
                        load_expert(b, i)

            run_slots(sp, slot)
            sp.wait_ge(x1_out, 16 * CHUNKS)
            sp.wait_ge(rows_out, 16 * CHUNKS)
            sp.wait_ge(shared_out, 16 * CHUNKS + 16)

            sp.wait_ge(ids_ready, 1)
            four = "(q p) n -> p q n"

            with sp.Fori(0, SEQS) as g:
                at_g = bass.ds(g * 4 * C, 4 * C)
                sp.dma_start(cx[:, bass.ds(g * 4, 4), :], res_d[at_g, :].rearrange(four, p=P)).then_inc(known_in, 16)
                sp.dma_start(cs[:, bass.ds(g * 4, 4), :], shared_d[at_g, :].rearrange(four, p=P)).then_inc(known_in, 16)
            for i in range(4):
                sp.wait_ge(scattered[i], 16 * ((TILES - i + 3) // 4))
            for g in range(SEQS):
                if g >= 4:
                    sp.wait_ge(picked_in[g % 4], 16)
                sp.dma_start(cp[:, g * 4:g * 4 + 4, :, :].rearrange("p q k n -> p q (k n)"),
                             picked_d[g * 8 * C:(g + 1) * 8 * C, :].rearrange("(q p k) n -> p q (k n)", p=P, k=TOPK))\
                    .then_inc(picked_in[g % 4], 16)
            with sp.Fori(0, SEQS) as g:
                sp.wait_ge(c_done, g * 4 + 4)
                sp.dma_start(outf[bass.ds(g * 4 * C, 4 * C), :].rearrange(four, p=P), cs[:, bass.ds(g * 4, 4), :]).then_inc(c_out, 16)
            sp.wait_ge(c_out, 16 * SEQS)

        @block.tensor
        def _(pe):
            ident, ident16 = k32("ident"), k16("ident")

            def product(bank, pairs):
                steps = [(left[a], right[b_]) for left, right in pairs for a, b_ in ((0, 0), (0, 1), (1, 0))]
                for i, (left, right) in enumerate(steps):
                    last = nc.tensor.matmul(bank, left, right, start=i == 0, stop=i == len(steps) - 1)
                return last

            pe.wait_ge(const_in[2], 32)
            pe.wait_ge(const_in[0], 16)
            for k in range(KT):
                last = nc.tensor.transpose(A0[0:HD, k * P:(k + 1) * P], rawG1[:, k, :], ident)
            last.then_inc(wg1_T, 1)
            pe.wait_ge(wg1_copied, 1)
            for k in range(KT):
                last = nc.tensor.matmul(A1[:, k * D:(k + 1) * D], rawG1T[:, k * P:(k + 1) * P], rawG2, start=True, stop=True)
            last.then_inc(wg_made, 1)

            def piece(unit, parity, p):
                if p == "split":
                    return
                n = unit * PIECES + p
                bank = FB[p % 2]
                if not (isinstance(n, int) and n < 2):
                    pe.wait_ge(piece_free, n - 1)
                if p < 8:
                    if p == 0:
                        pe.wait_ge(rowsT_lo, unit * 2 + 2)
                        if isinstance(unit, int) and unit == 0:
                            pe.wait_ge(set_lo, SET_SPLIT[2])
                    for half in range(2):
                        cols = slice(half * SHARED + p * P, half * SHARED + (p + 1) * P)
                        last = product(bank[:, half * 2 * C:(half + 1) * 2 * C],
                                       [([wGU[:, a, k, cols] for a in range(2)], [rT[:, parity, a, k, :] for a in range(2)])
                                        for k in range(KT)])
                else:
                    pe.wait_ge(act_lo, unit * 8 + 8)
                    tok = slice((p - 8) * C, (p - 7) * C)
                    last = product(bank[:, 0:D], [([aT[:, a, j, tok] for a in range(2)], [wDn[:, a, j, :] for a in range(2)])
                                                  for j in range(SHARED // P)])
                last.then_inc(piece_ready, 1)

            def slot(b, c, on):
                t, n = at(b, c), at(*shift(b, c, 1))
                tb, tc = shift(b, c, -1)
                ub, uc = shift(b, c, -2)
                tt, uu = at(tb, tc), at(ub, uc)

                def place(i):
                    if "ffn" in on:
                        for unit, parity, p in pieces(b, c, i):
                            piece(unit, parity, p)

                def scores(g):
                    if g >= 2:
                        pe.wait_ge(decayed, 4 * t + g - 1)
                    elif later(t):
                        if g == 0 and c:
                            pe.wait_ge(state_masked, 3 * b + c)
                        elif g == 1:
                            pe.wait_ge(decayed, 4 * t)
                    for j in range(2):
                        m = 2 * g + j
                        last = nc.tensor.matmul((A3, A4)[g % 2][:, j * 2 * C:(j + 1) * 2 * C], kT[:, m, :],
                                                qT[:, m, :, :].rearrange("p a t -> p (a t)"), start=True, stop=True)
                    last.then_inc(scores_ready, 1)

                def values(g):
                    k = g // 2
                    pe.wait_ge(decayed, 4 * t + g + 1)
                    for i in range(4):
                        h = 4 * g + i
                        q = 32 * ((h // 2) % 4)
                        last = nc.tensor.matmul(A0[q:q + 32, k * P:(k + 1) * P], vw[:, c % 2, h, :], sd[:, g % 2, i, :],
                                                start=(c == 0 and h % 2 == 0), stop=h % 2 == 1, skip_group_check=True)
                    last.then_inc(values_done, 1)

                if "project" in on:
                    pe.wait_ge(xs_ready, n + 1)
                    if later(t):
                        pe.wait_ge(oT_copied, t)
                    for k in range(KT):
                        last = nc.tensor.transpose(A0[:, k * P:(k + 1) * P], xs[:, k * P:(k + 1) * P], ident)
                    last.then_inc(xT_ready, 1)
                if "norm" in on:
                    pe.wait_ge(oT_copied, tt + 1)
                    if later(tt):
                        pe.wait_ge(attn_normed, tt)
                    for k in range(KT):
                        last = nc.tensor.transpose(A5[:, k * P:(k + 1) * P], oT[:, k, :], ident)
                    last.then_inc(o_ready, 1)
                place(0)
                if "route" in on:
                    pe.wait_ge(rows_ready, uu + 1)
                    if "norm" in on:
                        pe.wait_ge(gated, tt + 1)
                    else:
                        pe.wait_ge(attn_normed, uu + 1)
                    for k in range(KT):
                        last = nc.tensor.transpose(A5[:, k * P:(k + 1) * P], rows[:, k * P:(k + 1) * P], ident)
                    last.then_inc(rowsT_ready, 1)
                if "attend" in on:
                    pe.wait_ge(stacked, 3 * t + 3)
                    pe.wait_ge(v_copied, t + 1)
                    if "project" in on:
                        pe.wait_ge(xT_lo, n + 1)
                    elif later(t):
                        pe.wait_ge(oT_copied, t)
                    if isinstance(t, int) and t == 0:
                        pe.wait_ge(const_in[1], 16)
                    for half, bank in ((1, A2), (0, A1)):
                        b16 = bank[:, :].bitcast(F16)
                        for j in range(HEADS // 2):
                            last = nc.tensor.transpose(b16[:, j * P:(j + 1) * P],
                                                       st[:, half, 2 * j:2 * j + 2, :, :].rearrange("p h a e -> p (h a e)"), ident16)
                        if half:
                            last.then_inc(kstack_T, 1)
                    for k in range(KT):
                        last = nc.tensor.transpose(A0[:, k * P:(k + 1) * P], qk[:, k * P:(k + 1) * P], ident)
                    last.then_inc(stack_T, 1)
                place(1)
                if "route" in on:
                    pe.wait_ge(rowsT_lo, uu + 1)
                    if isinstance(uu, int) and uu == 0:
                        pe.wait_ge(set_lo, SET_SPLIT[2])
                    par, tok = uc // 2, slice(uc % 2 * C, (uc % 2 + 1) * C)
                    product(A5[:, 0:EXPERTS], [([rT[:, par, a, k, tok] for a in range(2)], [wR[:, a, k, :] for a in range(2)])
                                               for k in range(KT)]).then_inc(logits_ready, 1)
                if "attend" in on:
                    pe.wait_ge(kT_copied, t + 1)
                    pe.wait_ge(qT_low, t + 1)
                    pe.wait_ge(qT_high, t + 1)
                    if isinstance(t, int) and t == 0:
                        pe.wait_ge(zeroed, 2)
                    scores(0)
                    scores(1)
                if "project" in on:
                    pe.wait_ge(xT_lo, n + 1)
                    if isinstance(n, int) and n == 0:
                        pe.wait_ge(set_lo, SET_SPLIT[0])
                    for h, bank in enumerate((A1, A2)):
                        product(bank[:, :], [([xT[:, a, k, :] for a in range(2)],
                                              [wA[:, a, k, h * 2 * D:(h + 1) * 2 * D] for a in range(2)]) for k in range(KT)])\
                            .then_inc(proj_ready, 1)
                if "norm" in on:
                    pe.wait_ge(normed, tt + 1)
                    if "route" in on:
                        pe.wait_ge(logits_copied, uu + 1)
                    for k in range(KT):
                        last = nc.tensor.transpose(A5[:, k * P:(k + 1) * P], y[:, k * P:(k + 1) * P], ident)
                    last.then_inc(nT_ready, 1)
                place(2)
                if "attend" in on:
                    pe.wait_ge(q_decayed, t + 1)
                    pe.wait_ge(v_spread, t + 1)
                    if c:
                        pe.wait_ge(state_new, 3 * b + c)
                        for k in range(KT):
                            nc.tensor.matmul(A0[:, k * P:(k + 1) * P], state[:, k, :], qd[:, k, :],
                                             start=k == 0, stop=False, skip_group_check=True)
                    values(0)
                    scores(2)
                if "attend" in on:
                    values(1)
                    scores(3)
                if "norm" in on:
                    pe.wait_ge(nT_lo, tt + 1)
                    if isinstance(tt, int) and tt == 0:
                        pe.wait_ge(set_lo, SET_SPLIT[1])
                    product(A5[:, 0:D], [([nT[:, a, k, :] for a in range(2)], [wO[:, a, k, :] for a in range(2)])
                                         for k in range(KT)]).then_inc(attn_ready, 1)
                place(3)
                if "attend" in on:
                    if c < CPS - 1:
                        pe.wait_ge(k_decayed, t + 1)
                        pe.wait_ge(decayed, 4 * t + 3)
                        for k in range(KT):
                            last = nc.tensor.matmul(A3[:, k * P:(k + 1) * P], kd[:, c % 2, k * P:(k + 1) * P],
                                                    vn[:, c % 2, k * P:(k + 1) * P], start=True, stop=True)
                        last.then_inc(update_ready, 1)
                    values(2)
                    values(3)
                place(4)
                place(5)

            run_slots(pe, slot, CHUNKS + 2)

            pe.wait_ge(route, 3)
            n = CHUNKS * EXPERTS
            nc.tensor.matmul(A0[:, 0:n], k16("before"), both[:, :], start=True, stop=True)
            nc.tensor.matmul(A1[:, 0:n], k16("ones"), both[:, :], start=True, stop=True).then_inc(route_pe, 1)
            slot(SEQS, 2, {"ffn"})
            for i in range(TOPK * CHUNKS):
                pe.wait_ge(hot_ready, 2 * i + 2)
                nc.tensor.matmul(A2[:, 0:2 * (TILES + 1)], hot_r[:, i % 4, :], hot_t[:, i % 4, :, :].rearrange("p a t -> p (a t)"),
                                 start=i == 0, stop=i == TOPK * CHUNKS - 1).then_inc(hot_used, 1)

            pe.wait_ge(stage_lo, 3 * EXPERTS)
            pe.wait_ge(owners_ready, 1)
            pe.wait_ge(ids_ready, 1)

            def rows_T(j, i, m):
                pe.wait_ge(gathered[i % 4], 16 * (m + i // 4 + 1))
                if not isinstance(j, int) or j:
                    pe.wait_ge(eT_lo, j)
                for k in range(KT):
                    last = nc.tensor.transpose(A5[:, k * P:(k + 1) * P], got[i % 4][:, k * P:(k + 1) * P], ident)
                last.then_inc(eT_ready, 1)

            rows_T(0, 0, 0)

            def tile_slot(j, i, m):
                if has(j, 0):
                    e = pe.value_load(owner[0:1, bass.ds(j, 1)], min_val=0, max_val=EXPERTS - 1)
                    pe.wait_ge(eT_lo, j + 1)
                    if not isinstance(j, int) or j >= 2:
                        pe.wait_ge(e_act, j - 1)
                    for half in range(2):
                        product((A0, A1, A2, A3)[2 * (i % 2) + half][:, :],
                                [([eT[:, i % 2, a, k, :] for a in range(2)],
                                  [w1s[:, bass.ds(e, 1), a, k, half * INTER:(half + 1) * INTER] for a in range(2)])
                                 for k in range(KT)]).then_inc(gu_ready, 1)
                if has(j, 1):
                    rows_T(j + 1, i + 1, m)
                if has(j, -1):
                    pe.wait_ge(e_act, j)
                    if not isinstance(j, int) or j >= 2:
                        pe.wait_ge(ea_lo, j - 1)
                    for q in range(INTER // P):
                        last = nc.tensor.transpose(A4[:, q * P:(q + 1) * P], eg[:, (i - 1) % 2, q * P:(q + 1) * P], ident)
                    last.then_inc(aT_ready, 1)
                if has(j, -2):
                    e = pe.value_load(owner[0:1, bass.ds(j - 2, 1)], min_val=0, max_val=EXPERTS - 1)
                    pe.wait_ge(ea_lo, j - 1)
                    if isinstance(j, int) and j == 2:
                        pe.wait_ge(piece_free, UNITS * PIECES)
                    if not isinstance(j, int) or j >= 4:
                        pe.wait_ge(res_copied, j - 3)
                    product(FB[i % 2][:, 0:D], [([eaT[:, i % 2, a, q, :] for a in range(2)],
                                                 [w2s[:, bass.ds(e, 1), a, q, :] for a in range(2)])
                                                for q in range(INTER // P)]).then_inc(res_ready, 1)

            run_tiles(pe, tile_slot)

        @block.scalar
        def _(act):
            act.wait_ge(wg1_T, 1)
            nc.scalar.activation(rawG1T, A0[0:HD, 0:D], ACT.Copy).then_inc(wg1_copied, 1)
            act.wait_ge(wg_made, 1)
            nc.scalar.activation(rawA3[:, :, 3 * D:], A1[:, :].rearrange("p (k n) -> p k n", k=KT), ACT.Copy).then_inc(wg_copied, 1)

            def set_high(i):
                dst, src, col = ((wA[:, 0, :, :].rearrange("p k n -> p (k n)"), rawA, S_A),
                                 (wO[:, 0, :, :].rearrange("p k n -> p (k n)"), rawO, S_O), (wF[:, 0, :], rawF, S_F))[i]
                act.wait_ge(set_scaled, i + 1)
                for part in set_parts(i):
                    nc.scalar.activation(dst[:, part], src[:, part], ACT.Copy, scale=s(col)).then_inc(set_hi, 1)

            def xs_rows(b, c):
                t = at(b, c)
                act.wait_ge(ln1_shift, t + 1)
                if later(t):
                    act.wait_ge(xT_ready, t)
                nc.scalar.activation(xs[:, :], xin[:, c, :], ACT.Identity, scale=r1[:, 1:2], bias=r1[:, 2:3]).then_inc(xs_ready, 1)

            xs_rows(0, 0)

            def piece(unit, p):
                split = p == "split"
                if p == "split" or 1 <= p < 8:
                    p = 8 if p == "split" else p
                    act.wait_ge(piece_free, unit * PIECES + p)
                    nc.scalar.activation(aT[:, 0, p - 1, :], sg[:, (p - 1) % 2, :], ACT.Copy).then_inc(act_hi, 1)
                if p < 8:
                    act.wait_ge(piece_ready, unit * PIECES + p + 1)
                    if not (isinstance(unit, int) and unit * 8 + p < 2):
                        act.wait_ge(act_lo, unit * 8 + p - 1)
                    nc.scalar.activation(sg[:, p % 2, :], FB[p % 2][:, 0:2 * C], ACT.Silu, scale=s(C_F)).then_inc(piece_act, 1)
                elif not split:
                    act.wait_ge(piece_ready, unit * PIECES + p + 1)
                    act.wait_ge(shared_out, (unit * 2 + p - 7) * 16)
                    nc.scalar.activation(ysh[:, :], FB[p % 2][:, 0:D], ACT.Copy, scale=s(C_FD)).then_inc(piece_free, 1)

            def slot(b, c, on):
                t, following = at(b, c), (c + 1) % CPS
                n = at(*shift(b, c, 1))
                tb, tc = shift(b, c, -1)
                ub, uc = shift(b, c, -2)
                tt, uu = at(tb, tc), at(ub, uc)

                def place(i):
                    if "ffn" in on:
                        for unit, _, p in pieces(b, c, i):
                            piece(unit, p)

                def expert_hi(j):
                    act.wait_ge(exp_scaled, b + 1)
                    act.wait_ge(stage_in, (b * 6 + 3 + j + 1) * 16)
                    dst = w1s[:, bass.ds(b, 1), 0, j, :] if j < KT else \
                        w2s[:, bass.ds(b, 1), 0, :, :].rearrange("p a k n -> p (a k n)")
                    nc.scalar.activation(dst, stage[:, :], ACT.Copy, scale=escale[:, 0:1]).then_inc(stage_hi, 1)

                if "project" in on:
                    act.wait_ge(xT_ready, n + 1)
                    nc.scalar.activation(xT[:, 0, :, :].rearrange("p k t -> p (k t)"), A0[:, 0:D], ACT.Copy).then_inc(xT_hi, 1)
                    if isinstance(n, int) and n == 0:
                        set_high(0)
                if "route" in on:
                    act.wait_ge(ln3_step, 3 * uu + 3)
                    if later(uu):
                        act.wait_ge(rows_out, 16 * uu)
                    nc.scalar.activation(rows[:, :], x1[:, :], ACT.Identity, scale=r3[:, 1:2], bias=r3[:, 2:3])\
                        .then_inc(rows_ready, 1)
                place(0)
                if "norm" in on:
                    act.wait_ge(gated, tt + 1)
                    nc.scalar.activation(sq[:, :], y[:, :], ACT.Square).then_inc(squared, 1)
                if "route" in on:
                    act.wait_ge(rowsT_ready, uu + 1)
                    nc.scalar.activation(rT[:, uc // 2, 0, :, uc % 2 * C:(uc % 2 + 1) * C],
                                         A5[:, 0:D].rearrange("p (k t) -> p k t", k=KT), ACT.Copy).then_inc(rowsT_hi, 1)
                if "attend" in on:
                    act.wait_ge(kstack_T, t + 1)
                    nc.scalar.activation(kT[:, :, :].rearrange("p j t -> p (j t)"), A2[:, :].bitcast(F16), ACT.Copy).then_inc(kT_copied, 1)
                    if isinstance(t, int) and t == 0:
                        act.wait_ge(zeroed, 2)
                    act.wait_ge(qT_low, t + 1)
                    nc.scalar.activation(qT[64:128, :, 1, :], A1[:, :].bitcast(F16).rearrange("p (j t) -> p j t", t=C)[64:128, :, :],
                                         ACT.Copy).then_inc(qT_high, 1)
                if "expert" in on and c == 3:
                    expert_hi(1)
                place(1)
                if "project" in on:
                    act.wait_ge(proj_ready, 2 * n + 1)
                    if later(n):
                        act.wait_ge(k_decayed, n)
                        act.wait_ge(stack_T, n)
                    nc.scalar.activation(qk[:, :], A1[:, :], ACT.Silu, scale=s(C_A)).then_inc(qk_act, 1)
                    act.wait_ge(proj_ready, 2 * n + 2)
                    nc.scalar.activation(vn[:, following % 2, :], A2[:, 0:D], ACT.Copy, scale=s(C_A)).then_inc(v_copied, 1)
                    if isinstance(n, int) and n == 0:
                        act.wait_ge(zeroed, 2)
                    nc.scalar.activation(vw[:, following % 2, :, :].rearrange("p (j a) (b e) -> p j (a b) e", a=2, b=2)[:, :, 0:4:3, :],
                                         A2[:, 0:D].rearrange("p (j a e) -> p j a e", a=2, e=HD), ACT.Copy, scale=s(C_A))\
                        .then_inc(v_spread, 1)
                    if later(n, 2):
                        act.wait_ge(gated, n - 1)
                    nc.scalar.activation(th[:, following % 2, :], A2[:, D:], ACT.Tanh, scale=s(C_AH)).then_inc(gate_act, 1)
                if "norm" in on:
                    act.wait_ge(nT_ready, tt + 1)
                    nc.scalar.activation(nT[:, 0, :, :].rearrange("p k t -> p (k t)"), A5[:, 0:D], ACT.Copy).then_inc(nT_hi, 1)
                place(2)
                if "look" in on:
                    xs_rows(*shift(b, c, 2))
                if "expert" in on and c >= 2:
                    expert_hi(2 * (c - 2))
                place(3)
                if "project" in on:
                    act.wait_ge(rotated, 2 * n + 2)
                    nc.scalar.activation(st[:, :, :, 0, :].rearrange("p a h e -> p (a h) e"),
                                         qk[:, :].rearrange("p (h e) -> p h e", e=HD), ACT.Copy, scale=s(S_Q)).then_inc(qk_hi, 1)
                if "norm" in on:
                    act.wait_ge(ln2_step, 4 * tt + 4)
                    if later(tt):
                        act.wait_ge(x1_out, 16 * tt)
                        act.wait_ge(rows_ready, tt)
                    nc.scalar.activation(x1[:, :], A5[:, 0:D], ACT.Identity, scale=r2[:, 2:3], bias=r2[:, 3:4])\
                        .then_inc(attn_normed, 1)
                if isinstance(t, int) and t == 0:
                    set_high(1)
                    set_high(2)
                if "attend" in on:
                    act.wait_ge(values_done, 4 * t + 4)
                    if later(t):
                        act.wait_ge(o_ready, t)
                    nc.scalar.activation(oT[:, :, :].rearrange("p k t -> p (k t)"), A0[:, 0:D], ACT.Copy).then_inc(oT_copied, 1)
                place(4)
                place(5)

            run_slots(act, slot)

            act.wait_ge(route, 4)
            nc.scalar.activation(diff[:, :], diff[:, :], ACT.Tanh, scale=0.5).then_inc(route_act, 1)

            act.wait_ge(exp_scaled, EXPERTS)
            act.wait_ge(owners_ready, 1)

            def rows_hi(j, i):
                act.wait_ge(eT_ready, j + 1)
                nc.scalar.activation(eT[:, i % 2, 0, :, :].rearrange("p k t -> p (k t)"), A5[:, 0:D], ACT.Copy).then_inc(eT_hi, 1)

            rows_hi(0, 0)

            def tile_slot(j, i, m):
                if has(j, 0):
                    e = act.value_load(owner[0:1, bass.ds(j, 1)], min_val=0, max_val=EXPERTS - 1)
                    act.wait_ge(gu_ready, 2 * j + 1)
                    nc.scalar.activation(eg[:, i % 2, :], (A0, A2)[i % 2][:, :], ACT.Silu,
                                         scale=exp_scale[:, bass.ds(e, 1), 1:2].rearrange("p a b -> p (a b)")).then_inc(e_silu, 1)
                if has(j, 1):
                    rows_hi(j + 1, i + 1)
                if has(j, -1):
                    act.wait_ge(aT_ready, j)
                    nc.scalar.activation(eaT[:, (i - 1) % 2, 0, :, :].rearrange("p q t -> p (q t)"), A4[:, :], ACT.Copy).then_inc(ea_hi, 1)
                if has(j, -2):
                    e = act.value_load(owner[0:1, bass.ds(j - 2, 1)], min_val=0, max_val=EXPERTS - 1)
                    act.wait_ge(res_ready, j - 1)
                    if not isinstance(j, int) or j >= 6:
                        act.wait_ge(scattered[(i - 2) % 4], 16 * (m + (i - 2) // 4))
                    nc.scalar.activation(res[(i - 2) % 4][:, :], FB[i % 2][:, 0:D], ACT.Copy,
                                         scale=exp_scale[:, bass.ds(e, 1), 3:4].rearrange("p a b -> p (a b)")).then_inc(res_copied, 1)

            run_tiles(act, tile_slot)

            def normalize(g, i):
                act.wait_ge(c_shift, g + 5)
                for q in range(4):
                    z = cs[:, bass.ds(g * 4 + q, 1), :].rearrange("p a n -> p (a n)")
                    nc.scalar.activation(z, z, ACT.Identity, scale=cr[:, 4 * i + q, 1:2], bias=cr[:, 4 * i + q, 3:4])\
                        .then_inc(c_norm, 1)

            with act.Fori(0, SEQS // 4) as n:
                for i in range(4):
                    normalize(n * 4 + i, i)

        @block.vector
        def _(dve):
            nc.vector.memset(pmax[:, :], 0.0).then_inc(pmax_zero, 1)
            nc.vector.memset(vw[:, :, :, :], 0.0).then_inc(zeroed, 1)
            nc.vector.memset(qT[:, :, :, :], 0.0).then_inc(zeroed, 1)
            dve.wait_ge(pmax_zero, 1)

            def ln1(b, c):
                t = at(b, c)
                dve.wait_ge(x_in[c], (b + 1) * 16)
                nc.vector.bn_stats(st1, xin[:, c, :]).then_inc(ln1_stats, 1)
                dve.wait_ge(ln1_stats, t + 1)
                alone(dve)
                nc.vector.bn_aggr(mv1, st1).then_inc(ln1_mv, 1)

            ln1(0, 0)

            def set_largest(i):
                nc.vector.tensor_reduce(pmax[:, i:i + 1], (rawA, rawO, rawF)[i], axis=X, op=ALU.max,
                                        apply_absolute_value=True).then_inc(set_max, 1)

            step = [0]

            def chain(ins):
                step[0] += 1
                ins.then_inc(scale_step, 1)
                dve.wait_ge(scale_step, step[0])

            def powers(a, b_):
                chain(nc.vector.tensor_scalar(gmax[:, a:b_], gmax[:, a:b_], 2.0 ** -30, 2.0 ** 30, ALU.max, ALU.min))
                chain(nc.vector.tensor_scalar(pw[:, a:b_].bitcast(I32), gmax[:, a:b_].bitcast(I32), 0x7F800000, None, ALU.bitwise_and))
                chain(nc.vector.reciprocal(rp[:, a:b_], pw[:, a:b_]))

            def times(*scales):
                for dst, src, f in scales:
                    last = nc.vector.tensor_scalar(s(dst), src, f, None, ALU.mult)
                chain(last)

            def set_low(i):
                dst, hi, src, col = (
                    (wA[:, 1, :, :].rearrange("p k n -> p (k n)"), wA[:, 0, :, :].rearrange("p k n -> p (k n)"), rawA, S_A),
                    (wO[:, 1, :, :].rearrange("p k n -> p (k n)"), wO[:, 0, :, :].rearrange("p k n -> p (k n)"), rawO, S_O),
                    (wF[:, 1, :], wF[:, 0, :], rawF, S_F))[i]
                for n, part in enumerate(set_parts(i)):
                    dve.wait_ge(set_hi, SET_SPLIT[i] - len(set_parts(i)) + n + 1)
                    nc.vector.scalar_tensor_tensor(dst[:, part], src[:, part], s(col), hi[:, part], ALU.mult, ALU.subtract)\
                        .then_inc(set_lo, 1)

            dve.wait_ge(set_in[0], 48)
            dve.wait_ge(wg_copied, 1)
            set_largest(0)
            dve.wait_ge(set_all, 1)
            powers(0, 1)
            times((S_A, rp[:, 0:1], 2.0 ** 14))
            dve.sem_inc(set_scaled, 1)
            chain(nc.vector.tensor_tensor(sc[:, T0_:T0_ + 1], pw[:, 0:1], pw[:, 0:1], ALU.mult))
            times((C_A, pw[:, 0:1], 2.0 ** -24), (C_AH, pw[:, 0:1], 2.0 ** -25), (S_Q, rp[:, 0:1], 2.0 ** 5), (C_S, s(T0_), 2.0 ** -10))

            def lo(unit, p):
                dve.wait_ge(act_hi, unit * 8 + p + 1)
                nc.vector.tensor_tensor(aT[:, 1, p, :], sg[:, p % 2, :], aT[:, 0, p, :], ALU.subtract).then_inc(act_lo, 1)

            def piece(unit, p):
                if p == "split":
                    lo(unit, 7)
                elif 1 <= p < 8:
                    lo(unit, p - 1)
                if p != "split" and p < 8:
                    dve.wait_ge(piece_act, unit * 8 + p + 1)
                    nc.vector.scalar_tensor_tensor(sg[:, p % 2, :], FB[p % 2][:, 2 * C:], s(C_FU), sg[:, p % 2, :],
                                                   ALU.mult, ALU.mult).then_inc(piece_free, 1)

            def slot(b, c, on):
                t, n = at(b, c), at(*shift(b, c, 1))
                following = (c + 1) % CPS
                tb, tc = shift(b, c, -1)
                ub, uc = shift(b, c, -2)
                tt, uu = at(tb, tc), at(ub, uc)

                def place(i):
                    if "ffn" in on:
                        for unit, _, p in pieces(b, c, i):
                            piece(unit, p)

                def expert_max(j):
                    dve.wait_ge(stage_in, (b * 6 + j + 1) * 16)
                    nc.vector.tensor_reduce(escale[:, 4 + j:5 + j], stage[:, :], axis=X, op=ALU.max,
                                            apply_absolute_value=True).then_inc(stage_max, 1)

                def expert_lo(j):
                    dve.wait_ge(stage_hi, b * 3 + j + 1)
                    at_e = bass.ds(b, 1)
                    pick = (lambda a: w1s[:, at_e, a, j, :]) if j < KT else \
                        (lambda a: w2s[:, at_e, a, :, :].rearrange("p a k n -> p (a k n)"))
                    nc.vector.scalar_tensor_tensor(pick(1), stage[:, :] if j == KT else stage[:, :].unsqueeze(1), escale[:, 0:1],
                                                   pick(0), ALU.mult, ALU.subtract).then_inc(stage_lo, 1)

                def decay(g):
                    dve.wait_ge(scores_ready, 4 * t + g + 1)
                    if g >= 2 or later(t):
                        dve.wait_ge(values_done, 4 * t + g - 1)
                    nc.vector.scalar_tensor_tensor(sd[:, g % 2, :, :].rearrange("p h t -> p (h t)"), (A3, A4)[g % 2][:, :], s(C_S),
                                                   k32("decay")[:, 4 * g * C:4 * (g + 1) * C], ALU.mult, ALU.mult).then_inc(decayed, 1)

                if "norm" in on:
                    dve.wait_ge(o_ready, tt + 1)
                    dve.wait_ge(gate_act, tt + 1)
                    nc.vector.scalar_tensor_tensor(y[:, :], th[:, tc % 2, :], 1.0, A5[:, 0:D], ALU.add, ALU.mult).then_inc(gated, 1)
                if "project" in on:
                    dve.wait_ge(xT_hi, n + 1)
                    nc.vector.tensor_tensor(xT[:, 1, :, :].rearrange("p k t -> p (k t)"), A0[:, 0:D],
                                            xT[:, 0, :, :].rearrange("p k t -> p (k t)"), ALU.subtract).then_inc(xT_lo, 1)
                    if isinstance(n, int) and n == 0:
                        set_low(0)
                place(0)
                if "norm" in on:
                    dve.wait_ge(squared, tt + 1)
                    nc.vector.tensor_reduce(ssum, sq[:, :].rearrange("p (h e) -> p h e", e=HD), axis=X, op=ALU.add).then_inc(summed, 1)
                if "route" in on:
                    dve.wait_ge(rowsT_hi, uu + 1)
                    tok = slice(uc % 2 * C, (uc % 2 + 1) * C)
                    nc.vector.tensor_tensor(rT[:, uc // 2, 1, :, tok], A5[:, 0:D].rearrange("p (k t) -> p k t", k=KT),
                                            rT[:, uc // 2, 0, :, tok], ALU.subtract).then_inc(rowsT_lo, 1)
                if "attend" in on:
                    dve.wait_ge(stack_T, t + 1)
                    if isinstance(t, int) and t == 0:
                        dve.wait_ge(zeroed, 2)
                        dve.wait_ge(const_in[3], 16)
                    b16 = A1[:, :].bitcast(F16).rearrange("p (j t) -> p j t", t=C)
                    nc.vector.tensor_copy(qT[0:64, :, 0, :], b16[0:64, :, :]).then_inc(qT_low, 1)
                    nc.vector.tensor_tensor(qd[:, :, :].rearrange("p k t -> p (k t)"), A0[:, 0:D], k32("qdec"), ALU.mult)\
                        .then_inc(q_decayed, 1)
                if "look" in on:
                    ln1(*shift(b, c, 2))
                if "route" in on:
                    dve.wait_ge(logits_ready, uu + 1)
                    nc.vector.tensor_scalar(lg[:, :], A5[:, 0:EXPERTS], s(C_F), None, ALU.mult).then_inc(logits_copied, 1)
                    dve.wait_ge(logits_copied, uu + 1)
                    alone(dve)
                    nc.vector.max(m8[:, :], lg[:, :]).then_inc(top_step, 1)
                    dve.wait_ge(top_step, 3 * uu + 1)
                    alone(dve)
                    nc.vector.max_index(i8[:, :], m8[:, :], lg[:, :]).then_inc(top_step, 1)
                    nc.vector.tensor_copy(top_v[:, bass.ds(uu, 1), :], m8[:, 0:TOPK].unsqueeze(1))
                    dve.wait_ge(top_step, 3 * uu + 2)
                    nc.vector.tensor_copy(top_i[:, bass.ds(uu, 1), :], i8[:, 0:TOPK].unsqueeze(1)).then_inc(top_step, 1)
                place(1)
                if isinstance(t, int) and t == 0:
                    dve.wait_ge(set_in[1], 32)
                    for k in range(KT):
                        nc.vector.tensor_scalar(rawO[:, k * D:(k + 1) * D], rawO[:, k * D:(k + 1) * D], rawNW[:, k:k + 1], None,
                                                ALU.mult).then_inc(nw_folded, 1)
                    dve.wait_ge(nw_folded, 2)
                    set_largest(1)
                    dve.wait_ge(set_in[2], 64)
                    set_largest(2)
                if "expert" in on and c == 0:
                    expert_max(0)
                if "expert" in on and c == 2:
                    e = escale
                    n0 = b * 5
                    dve.wait_ge(exp_all, b + 1)

                    def link(i, ins):
                        ins.then_inc(exp_step, 1)
                        dve.wait_ge(exp_step, n0 + i)

                    link(1, nc.vector.tensor_scalar(e[:, 4:5], e[:, 4:5], 2.0 ** -30, 2.0 ** 30, ALU.max, ALU.min))
                    link(2, nc.vector.tensor_scalar(e[:, 5:6].bitcast(I32), e[:, 4:5].bitcast(I32), 0x7F800000, None, ALU.bitwise_and))
                    link(3, nc.vector.reciprocal(e[:, 6:7], e[:, 5:6]))
                    nc.vector.tensor_scalar(e[:, 0:1], e[:, 6:7], 2.0 ** 14, None, ALU.mult)
                    nc.vector.tensor_scalar(e[:, 1:2], e[:, 5:6], 2.0 ** -24, None, ALU.mult)
                    nc.vector.tensor_scalar(e[:, 2:3], e[:, 6:7], 2.0 ** -27, None, ALU.mult)
                    link(4, nc.vector.tensor_tensor(e[:, 3:4], e[:, 5:6], e[:, 5:6], ALU.mult))
                    link(5, nc.vector.scalar_tensor_tensor(e[:, 3:4], e[:, 3:4], 2.0 ** -11, e[:, 5:6], ALU.mult, ALU.mult))
                    nc.vector.tensor_copy(exp_scale[:, bass.ds(b, 1), :], e[:, 0:4].unsqueeze(1)).then_inc(exp_scaled, 1)
                if "expert" in on and c == 3:
                    expert_lo(1)
                if "attend" in on:
                    decay(0)
                    decay(1)
                if "project" in on:
                    dve.wait_ge(qk_act, n + 1)
                    a, r, o4 = halves(qk[:, :]), halves(rs[:, :]), halves(rc[:, :])
                    sin = k32("sin")[:, following * 8:(following + 1) * 8].unsqueeze(1).broadcast_to((P, 2 * HEADS, HD // 2))
                    nc.vector.tensor_tensor(r[:, :, 0, :], a[:, :, 1, :], sin, ALU.mult).then_inc(rope_sin, 1)
                if "norm" in on:
                    dve.wait_ge(nT_hi, tt + 1)
                    nc.vector.tensor_tensor(nT[:, 1, :, :].rearrange("p k t -> p (k t)"), A5[:, 0:D],
                                            nT[:, 0, :, :].rearrange("p k t -> p (k t)"), ALU.subtract).then_inc(nT_lo, 1)
                place(2)
                if "attend" in on:
                    decay(2)
                    decay(3)
                if "norm" in on:
                    dve.wait_ge(attn_ready, tt + 1)
                    nc.vector.bn_stats(st2, A5[:, 0:D]).then_inc(ln2_stats, 1)
                    dve.wait_ge(ln2_stats, tt + 1)
                    alone(dve)
                    nc.vector.bn_aggr(mv2, st2).then_inc(ln2_mv, 1)
                if "project" in on:
                    dve.wait_ge(rope_cos, n + 1)
                    dve.wait_ge(rope_sin, 2 * n + 2)
                    nc.vector.tensor_tensor(a[:, :, 0, :], o4[:, :, 0, :], r[:, :, 0, :], ALU.subtract).then_inc(rotated, 1)
                    nc.vector.tensor_tensor(a[:, :, 1, :], o4[:, :, 1, :], r[:, :, 1, :], ALU.add).then_inc(rotated, 1)
                place(3)
                if "project" in on:
                    dve.wait_ge(qk_hi, n + 1)
                    flat = st[:, :, :, :, :].rearrange("p a h i e -> p (a h) i e")
                    nc.vector.scalar_tensor_tensor(flat[:, :, 1, :], qk[:, :].rearrange("p (h e) -> p h e", e=HD), s(S_Q),
                                                   flat[:, :, 0, :], ALU.mult, ALU.subtract).then_inc(qk_lo, 1)
                    nc.vector.tensor_copy(st[:, 0, :, 3, :], st[:, 0, :, 0, :]).then_inc(stacked, 1)
                    dve.wait_ge(qk_lo, n + 1)
                    nc.vector.tensor_copy(st[:, 0, :, 2, :], st[:, 0, :, 1, :]).then_inc(stacked, 1)
                    nc.vector.tensor_copy(st[:, 1, :, 2:4, :], st[:, 1, :, 0:2, :]).then_inc(stacked, 1)
                if isinstance(t, int) and t == 0:
                    dve.wait_ge(set_all, 2)
                    powers(1, 3)
                    chain(nc.vector.tensor_tensor(sc[:, T1_:T1_ + 1], pw[:, 2:3], pw[:, 2:3], ALU.mult))
                    times((S_O, rp[:, 1:2], 2.0 ** 14), (C_O, pw[:, 1:2], 2.0 ** -26), (S_F, rp[:, 2:3], 2.0 ** 14),
                          (C_F, pw[:, 2:3], 2.0 ** -24), (C_FU, rp[:, 2:3], 2.0 ** -27))
                    chain(nc.vector.tensor_tensor(s(C_O2), s(C_O), s(C_O), ALU.mult))
                    chain(nc.vector.scalar_tensor_tensor(s(C_FD), s(T1_), 2.0 ** -11, pw[:, 2:3], ALU.mult, ALU.mult))
                    dve.sem_inc(set_scaled, 2)
                    set_low(1)
                    set_low(2)
                if "attend" in on and c < CPS - 1:
                    dve.wait_ge(update_ready, 3 * b + c + 1)
                    kept = state[:, :, :].rearrange("p k t -> p (k t)")
                    if c == 0:
                        nc.vector.tensor_tensor(kept, A3[:, 0:D], k32("block"), ALU.mult).then_inc(state_masked, 1)
                        dve.wait_ge(state_masked, 3 * b + 1)
                        dve.sem_inc(state_new, 1)
                    else:
                        nc.vector.tensor_tensor(sq[:, :], A3[:, 0:D], k32("block"), ALU.mult).then_inc(state_masked, 1)
                        dve.wait_ge(state_masked, 3 * b + c + 1)
                        dve.wait_ge(state_old, 2 * b + c)
                        nc.vector.tensor_tensor(kept, kept, sq[:, :], ALU.add).then_inc(state_new, 1)
                place(4)
                if "norm" in on:
                    dve.wait_ge(x1_ready, tt + 1)
                    nc.vector.bn_stats(st3, x1[:, :]).then_inc(ln3_stats, 1)
                    dve.wait_ge(ln3_stats, tt + 1)
                    alone(dve)
                    nc.vector.bn_aggr(mv3, st3).then_inc(ln3_mv, 1)
                place(5)
                if "expert" in on:
                    if c <= 1:
                        expert_max(c + 1)
                    if c == 1:
                        dve.wait_ge(stage_max, b * 3 + 3)
                        nc.vector.tensor_reduce(escale[:, 7:8], escale[:, 4:7], axis=X, op=ALU.max).then_inc(exp_max, 1)
                    if c >= 2:
                        expert_lo(2 * (c - 2))

            run_slots(dve, slot, CHUNKS + 2)

            width = TILES + 1
            done = [0]

            def then(ins, after=True):
                done[0] += 1
                ins.then_inc(route, 1)
                if after:
                    dve.wait_ge(route, done[0])

            dve.wait_ge(top_step, 3 * CHUNKS)
            for k in range(TOPK):
                then(nc.vector.tensor_tensor(picks[k][:, :, :], k32("iota8").unsqueeze(1).broadcast_to((P, CHUNKS, EXPERTS)),
                                             top_i[:, :, k].unsqueeze(2).broadcast_to((P, CHUNKS, EXPERTS)), ALU.is_equal))
            then(nc.vector.tensor_tensor(both[:, :].rearrange("p (c e) -> p c e", e=EXPERTS), picks[0][:, :, :], picks[1][:, :, :],
                                         ALU.add))
            then(nc.vector.tensor_tensor(diff[:, :], top_v[:, :, 0], top_v[:, :, 1], ALU.subtract))
            dve.wait_ge(route_pe, 1)
            total, a, b_ = counts
            psum3 = [bank[:, 0:CHUNKS * EXPERTS].rearrange("p (c e) -> p c e", e=EXPERTS) for bank in (A0, A1)]
            then(nc.vector.tensor_copy(total[:, :, :], psum3[1]))
            left = [work for place in range(6) for work in pieces(SEQS, 2, place) if work[2] not in (8, 9)]

            def piece_left():
                if left:
                    piece(left[0][0], left.pop(0)[2])

            piece_left()

            def running(src, bufs, n):
                step = 1
                k = 0
                while step < n:
                    dst = bufs[k % 2]
                    then(nc.vector.tensor_copy(dst[:, 0:step], src[:, 0:step]))
                    then(nc.vector.tensor_tensor(dst[:, step:n], src[:, step:n], src[:, 0:n - step], ALU.add))
                    src, step, k = dst, step * 2, k + 1
                    piece_left()
                return src

            summed_c = running(total, (a, b_), CHUNKS)
            while left:
                piece_left()
            spare = a if summed_c is b_ else b_
            count = summed_c[:, CHUNKS - 1, :]
            then(nc.vector.tensor_scalar(filled_i[:, :], count, float(P - 1), None, ALU.add))
            then(nc.vector.tensor_scalar(filled_i[:, :], filled_i[:, :], 7, None, ALU.logical_shift_right))
            then(nc.vector.tensor_copy(filled[0][:, :], filled_i[:, :]))
            until = running(filled[0], (filled[1], filled[2]), EXPERTS)
            then(nc.vector.tensor_tensor(filled[3][:, :], until[:, :], filled[0][:, :], ALU.subtract))
            then(nc.vector.tensor_scalar(filled[3][:, :], filled[3][:, :], float(P), None, ALU.mult))
            then(nc.vector.tensor_tensor(place_of[:, :, :], summed_c[:, :, :], total[:, :, :], ALU.subtract))
            then(nc.vector.tensor_tensor(spare[:, :, :], place_of[:, :, :], psum3[0], ALU.add))
            then(nc.vector.tensor_tensor(place_of[:, :, :], spare[:, :, :], filled[3][:, :].unsqueeze(1).broadcast_to((P, CHUNKS, EXPERTS)),
                                         ALU.add))
            for k in range(TOPK):
                then(nc.vector.tensor_tensor(prod[:, :, :], picks[k][:, :, :], place_of[:, :, :], ALU.mult))
                then(nc.vector.tensor_reduce(spot[:, k, :], prod[:, :, :], axis=X, op=ALU.add))
            then(nc.vector.tensor_copy(spot_i[:, :, :], spot[:, :, :]))
            then(nc.vector.tensor_scalar(spot_t[:, :, :], spot_i[:, :, :], 7, None, ALU.logical_shift_right))
            then(nc.vector.tensor_scalar(spot_r[:, :, :], spot_i[:, :, :], P - 1, None, ALU.bitwise_and))
            then(nc.vector.tensor_copy(tile_f[:, :, :], spot_t[:, :, :]))
            then(nc.vector.tensor_copy(row_f[:, :, :], spot_r[:, :, :]))
            then(nc.vector.tensor_copy(vals[:, :, :, 0], k32("tok").unsqueeze(1).broadcast_to((P, CHUNKS, TOPK))))
            then(nc.vector.tensor_scalar(vals[:, :, :, 1], k32("iotat")[:, 0:CHUNKS].unsqueeze(2).broadcast_to((P, CHUNKS, TOPK)),
                                         float(TOPK * C), None, ALU.mult))
            for i in range(TOPK * CHUNKS):
                k, c = i % TOPK, i // TOPK
                if i >= 4:
                    dve.wait_ge(hot_used, i - 3)
                nc.vector.tensor_scalar(hot_r[:, i % 4, :], k16("iota"), row_f[:, k, c:c + 1], None, ALU.is_equal).then_inc(hot_ready, 1)
                nc.vector.scalar_tensor_tensor(hot_t[:, i % 4, :, :], k32("iotat").unsqueeze(1).broadcast_to((P, 2, TILES + 1)),
                                               tile_f[:, k, c:c + 1], vals[:, c, k, :].unsqueeze(2).broadcast_to((P, 2, TILES + 1)),
                                               ALU.is_equal, ALU.mult).then_inc(hot_ready, 1)
            then(nc.vector.tensor_tensor(cmp[:, :, :], k32("iotat").unsqueeze(2).broadcast_to((P, width, EXPERTS - 1)),
                                         until[:, 0:EXPERTS - 1].unsqueeze(1).broadcast_to((P, width, EXPERTS - 1)), ALU.is_ge))
            then(nc.vector.tensor_reduce(owner_f[:, :], cmp[:, :, :], axis=X, op=ALU.add))
            nc.vector.tensor_copy(owner[:, :], owner_f[:, :]).then_inc(owners_ready, 1)
            dve.wait_ge(hot_used, TOPK * CHUNKS)
            then(nc.vector.tensor_copy(ids2[:, :, :].rearrange("p a t -> p (a t)"), A2[:, 0:2 * width]))
            then(nc.vector.tensor_tensor(idv[:, :], ids2[:, 0, :], ids2[:, 1, :], ALU.add))
            then(nc.vector.tensor_scalar(gat_i[:, :], idv[:, :], -1.0, 0.0, ALU.add, ALU.max))
            nc.vector.tensor_scalar(gat[:, :], gat_i[:, :], 1, None, ALU.logical_shift_right).then_inc(ids_ready, 1)
            then(nc.vector.tensor_scalar(idz[:, :], idv[:, :], 0.0, float(FAR), ALU.is_equal, ALU.mult))
            nc.vector.scalar_tensor_tensor(sca[:, :], idv[:, :], -1.0, idz[:, :], ALU.add, ALU.add).then_inc(spots_ready, 1)

            dve.wait_ge(route_act, 1)
            then(nc.vector.tensor_scalar(weight[:, :, 0], diff[:, :], 0.5, 0.5, ALU.mult, ALU.add))
            then(nc.vector.tensor_scalar(weight[:, :, 1], diff[:, :], -0.5, 0.5, ALU.mult, ALU.add))

            dve.wait_ge(owners_ready, 1)

            def rows_lo(j, i):
                dve.wait_ge(eT_hi, j + 1)
                nc.vector.tensor_tensor(eT[:, i % 2, 1, :, :].rearrange("p k t -> p (k t)"), A5[:, 0:D],
                                        eT[:, i % 2, 0, :, :].rearrange("p k t -> p (k t)"), ALU.subtract).then_inc(eT_lo, 1)

            rows_lo(0, 0)

            def tile_slot(j, i, m):
                if has(j, 0):
                    e = dve.value_load(owner[0:1, bass.ds(j, 1)], min_val=0, max_val=EXPERTS - 1)
                    dve.wait_ge(gu_ready, 2 * j + 2)
                    dve.wait_ge(e_silu, j + 1)
                    nc.vector.scalar_tensor_tensor(eg[:, i % 2, :], (A1, A3)[i % 2][:, :],
                                                   exp_scale[:, bass.ds(e, 1), 2:3].rearrange("p a b -> p (a b)"), eg[:, i % 2, :],
                                                   ALU.mult, ALU.mult).then_inc(e_act, 1)
                if has(j, 1):
                    rows_lo(j + 1, i + 1)
                if has(j, -1):
                    dve.wait_ge(ea_hi, j)
                    nc.vector.tensor_tensor(eaT[:, (i - 1) % 2, 1, :, :].rearrange("p q t -> p (q t)"), A4[:, :],
                                            eaT[:, (i - 1) % 2, 0, :, :].rearrange("p q t -> p (q t)"), ALU.subtract).then_inc(ea_lo, 1)

            run_tiles(dve, tile_slot)

            def combine(g, i, n):
                dve.wait_ge(picked_in[i], (n + 1) * 16)
                for k in range(TOPK):
                    for q in range(4):
                        ch = bass.ds(g * 4 + q, 1)
                        if k:
                            dve.wait_ge(c_sum, g * 8 + q + 1)
                        z = cs[:, ch, :].rearrange("p a n -> p (a n)")
                        nc.vector.scalar_tensor_tensor(z, cp[:, ch, k, :].rearrange("p a n -> p (a n)"),
                                                       weight[:, ch, k:k + 1].rearrange("p a b -> p (a b)"), z,
                                                       ALU.mult, ALU.add).then_inc(c_sum, 1)
                for q in range(4):
                    ch = bass.ds(g * 4 + q, 1)
                    dve.wait_ge(c_sum, g * 8 + 5 + q)
                    alone(dve)
                    nc.vector.bn_stats(cst[:, 4 * i + q, :],
                                       cs[:, ch, :].rearrange("p a n -> p (a n)")).then_inc(c_stats, 1)
                dve.wait_ge(c_shift, g + 1)
                for q in range(4):
                    dve.wait_ge(c_stats, g * 4 + q + 1)
                    alone(dve)
                    nc.vector.bn_aggr(cmv[:, 4 * i + q, :], cst[:, 4 * i + q, :]).then_inc(c_mv, 1)

            dve.wait_ge(known_in, 32 * SEQS)
            with dve.Fori(0, SEQS // 4) as n:
                for i in range(4):
                    combine(n * 4 + i, i, n)

        @block.gpsimd
        def _(pool):
            def ln1(b, c):
                t = at(b, c)
                pool.wait_ge(ln1_mv, t + 1)
                if later(t):
                    pool.wait_ge(xs_ready, t)
                alone(pool)
                nc.gpsimd.tensor_scalar(r1[:, 0:1], mv1[:, 1:2], LN_EPS, XS ** -2, ALU.add, ALU.mult).then_inc(ln1_var, 1)
                pool.wait_ge(ln1_var, t + 1)
                nc.gpsimd.tensor_tensor(r1[:, 1:2], r1[:, 0:1], mhalf[:, 0:1], ALU.pow).then_inc(ln1_pow, 1)
                pool.wait_ge(ln1_pow, t + 1)
                alone(pool)
                nc.gpsimd.tensor_scalar(r1[:, 2:3], mv1[:, 0:1], r1[:, 1:2], -1.0, ALU.mult, ALU.mult).then_inc(ln1_shift, 1)

            pool.wait_ge(const_in[0], 16)
            ln1(0, 0)
            pool.wait_ge(set_max, 1)
            alone(pool)
            nc.gpsimd.partition_all_reduce(gmax[:, 0:1], pmax[:, 0:1], P, ABSMAX).then_inc(set_all, 1)

            def slot(b, c, on):
                t, n = at(b, c), at(*shift(b, c, 1))
                following = (c + 1) % CPS
                tb, tc = shift(b, c, -1)
                tt = at(tb, tc)
                if "norm" in on:
                    pool.wait_ge(summed, tt + 1)
                    alone(pool)
                    nc.gpsimd.tensor_scalar(smean, ssum, 1.0 / (4 * HD) * (NS / 2) ** -2, RMS_EPS * (NS / 2) ** -2, ALU.mult, ALU.add)\
                        .then_inc(rms_mean, 1)
                    pool.wait_ge(rms_mean, tt + 1)
                    nc.gpsimd.tensor_tensor(srms, smean, mhalf, ALU.pow).then_inc(rms_pow, 1)
                    pool.wait_ge(rms_pow, tt + 1)
                    y3 = y[:, :].rearrange("p (h e) -> p h e", e=HD)
                    nc.gpsimd.tensor_tensor(y3, y3, srms.unsqueeze(2).broadcast_to((P, HEADS, HD)), ALU.mult).then_inc(normed, 1)
                if isinstance(t, int) and t == 0:
                    pool.wait_ge(const_in[3], 16)
                if "look" in on:
                    ln1(*shift(b, c, 2))
                if "project" in on:
                    pool.wait_ge(qk_act, n + 1)
                    if later(n):
                        pool.wait_ge(rotated, 2 * n)
                    cos = k32("cos")[:, following * 8:(following + 1) * 8].unsqueeze(1).broadcast_to((P, 4 * HEADS, HD // 2))
                    nc.gpsimd.tensor_tensor(rc[:, :].rearrange("p (h e) -> p h e", e=HD // 2),
                                            qk[:, :].rearrange("p (h e) -> p h e", e=HD // 2), cos, ALU.mult).then_inc(rope_cos, 1)
                    a, r = halves(qk[:, :]), halves(rs[:, :])
                    sin = k32("sin")[:, following * 8:(following + 1) * 8].unsqueeze(1).broadcast_to((P, 2 * HEADS, HD // 2))
                    nc.gpsimd.tensor_tensor(r[:, :, 1, :], a[:, :, 0, :], sin, ALU.mult).then_inc(rope_sin, 1)
                if "norm" in on:
                    n0 = 4 * tt
                    pool.wait_ge(ln2_mv, tt + 1)
                    alone(pool)
                    nc.gpsimd.tensor_scalar(r2[:, 0:1], mv2[:, 1:2], s(C_O2), LN_EPS, ALU.mult, ALU.add).then_inc(ln2_step, 1)
                    pool.wait_ge(ln2_step, n0 + 1)
                    nc.gpsimd.tensor_tensor(r2[:, 1:2], r2[:, 0:1], mhalf[:, 0:1], ALU.pow).then_inc(ln2_step, 1)
                    pool.wait_ge(ln2_step, n0 + 2)
                    alone(pool)
                    nc.gpsimd.tensor_scalar(r2[:, 2:3], r2[:, 1:2], s(C_O), None, ALU.mult).then_inc(ln2_step, 1)
                    pool.wait_ge(ln2_step, n0 + 3)
                    alone(pool)
                    nc.gpsimd.tensor_scalar(r2[:, 3:4], mv2[:, 0:1], r2[:, 2:3], -1.0, ALU.mult, ALU.mult).then_inc(ln2_step, 1)
                if "attend" in on and 1 <= c < CPS - 1:
                    pool.wait_ge(update_ready, 3 * b + c + 1)
                    nc.gpsimd.tensor_tensor(state[:, :, :].rearrange("p k t -> p (k t)"), state[:, :, :].rearrange("p k t -> p (k t)"),
                                            k32("blocklam"), ALU.mult).then_inc(state_old, 1)
                if "norm" in on:
                    pool.wait_ge(attn_normed, tt + 1)
                    nc.gpsimd.tensor_tensor(x1[:, :], x1[:, :], xin[:, tc, :], ALU.add).then_inc(x1_ready, 1)
                    pool.wait_ge(ln3_mv, tt + 1)
                    if later(tt):
                        pool.wait_ge(rows_ready, tt)
                    alone(pool)
                    nc.gpsimd.tensor_scalar(r3[:, 0:1], mv3[:, 1:2], LN_EPS, XS ** -2, ALU.add, ALU.mult).then_inc(ln3_step, 1)
                    pool.wait_ge(ln3_step, 3 * tt + 1)
                    nc.gpsimd.tensor_tensor(r3[:, 1:2], r3[:, 0:1], mhalf[:, 0:1], ALU.pow).then_inc(ln3_step, 1)
                    pool.wait_ge(ln3_step, 3 * tt + 2)
                    alone(pool)
                    nc.gpsimd.tensor_scalar(r3[:, 2:3], mv3[:, 0:1], r3[:, 1:2], -1.0, ALU.mult, ALU.mult).then_inc(ln3_step, 1)
                if "project" in on:
                    pool.wait_ge(rotated, 2 * n + 2)
                    nc.gpsimd.tensor_tensor(kd[:, following % 2, :].rearrange("p (h e) -> p h e", e=HD), qk[:, D:].rearrange("p (h e) -> p h e", e=HD),
                                            k32("kdec").unsqueeze(2).broadcast_to((P, HEADS, HD)), ALU.mult).then_inc(k_decayed, 1)
                if isinstance(t, int) and t == 0:
                    pool.wait_ge(set_max, 3)
                    alone(pool)
                    nc.gpsimd.partition_all_reduce(gmax[:, 1:3], pmax[:, 1:3], P, ABSMAX).then_inc(set_all, 1)
                if "expert" in on and c == 1:
                    pool.wait_ge(exp_max, b + 1)
                    alone(pool)
                    nc.gpsimd.partition_all_reduce(escale[:, 4:5], escale[:, 7:8], P, ABSMAX).then_inc(exp_all, 1)

            run_slots(pool, slot)

            pool.wait_ge(ids_ready, 1)
            pool.wait_ge(rows_out, 16 * CHUNKS)

            def gather(j, i, m):
                if not isinstance(j, int) or j >= 4:
                    pool.wait_ge(eT_ready, j - 3)
                    pool.wait_ge(gathered[i % 4], 16 * (m + i // 4))
                alone(pool)
                nc.gpsimd.tensor_copy(gidx[:, i % 4:i % 4 + 1], gat[:, bass.ds(j, 1)]).then_inc(index_set, 1)
                return i % 4

            def gather_start(i):
                nc.gpsimd.indirect_dma_start(out=got[i][:, :], out_offset=None, in_=rows_d[:, :],
                                             in_offset=bass.IndirectOffsetOnAxis(ap=gidx[:, i:i + 1], axis=0)).then_inc(gathered[i], 16)

            for j in range(3):
                i = gather(j, j, 0)
                pool.wait_ge(index_set, j + 1)
                alone(pool)
                gather_start(i)

            pool.wait_ge(spots_ready, 1)

            def tile_slot(j, i, m):
                base = 3 + (min(j, TILES - 3) + max(j - 3, 0) if isinstance(j, int) else j + j - 3)
                if has(j, 3):
                    gi = gather(j + 3, i + 3, m)
                    base = base + 1
                    pool.wait_ge(index_set, base)
                    alone(pool)
                    gather_start(gi)
                if has(j, -3):
                    pool.wait_ge(res_copied, j - 2)
                    alone(pool)
                    nc.gpsimd.tensor_copy(sidx[:, (i - 3) % 4:(i - 3) % 4 + 1], sca[:, bass.ds(j - 3, 1)]).then_inc(index_set, 1)
                    base = base + 1
                    pool.wait_ge(index_set, base)
                    alone(pool)
                    nc.gpsimd.indirect_dma_start(out=picked_d[:, :], in_=res[(i - 3) % 4][:, :], in_offset=None,
                                                 out_offset=bass.IndirectOffsetOnAxis(ap=sidx[:, (i - 3) % 4:(i - 3) % 4 + 1], axis=0),
                                                 bounds_check=TOKENS * TOPK - 1, oob_is_err=False).then_inc(scattered[(i - 3) % 4], 16)

            run_tiles(pool, tile_slot)
            tile_slot(TILES + 2, (TILES + 2) % 4, 0)

            pool.wait_ge(known_in, 32 * SEQS)
            pool.sem_inc(c_shift, 4)
            pool.sem_inc(c_norm, 16)

            def residual(g, i):
                at_i = slice(4 * i, 4 * i + 4)
                pool.wait_ge(c_norm, g * 4 + 4)
                pool.wait_ge(c_mv, g * 4 + 4)
                alone(pool)
                nc.gpsimd.tensor_scalar(cr[:, at_i, 0], cmv[:, at_i, 1], LN_EPS, None, ALU.add).then_inc(c_var, 1)
                nc.gpsimd.tensor_scalar(cr[:, at_i, 2], cmv[:, at_i, 0], -1.0, None, ALU.mult).then_inc(c_var, 1)
                pool.wait_ge(c_var, g * 2 + 1)
                nc.gpsimd.tensor_tensor(cr[:, at_i, 1], cr[:, at_i, 0], mhalf[:, 0:4], ALU.pow).then_inc(c_rstd, 1)
                pool.wait_ge(c_var, g * 2 + 2)
                pool.wait_ge(c_rstd, g + 1)
                nc.gpsimd.tensor_tensor(cr[:, at_i, 3], cr[:, at_i, 2], cr[:, at_i, 1], ALU.mult).then_inc(c_shift, 1)
                for q in range(4):
                    ch = bass.ds(g * 4 + q, 1)
                    pool.wait_ge(c_norm, g * 4 + q + 17)
                    nc.gpsimd.tensor_tensor(cs[:, ch, :], cs[:, ch, :], cx[:, ch, :], ALU.add).then_inc(c_done, 1)

            with pool.Fori(0, SEQS // 4) as n:
                for i in range(4):
                    residual(n * 4 + i, i)


_INS = ["L0_attn_x", "L0_attn_Wq", "L0_attn_Wk", "L0_attn_Wv", "L0_attn_Wo", "L0_attn_Wg1", "L0_attn_Wg2",
        "L0_attn_norm_weight", "L0_ffn_router_w", "L0_ffn_w1", "L0_ffn_w2", "L0_ffn_w_gate", "L0_ffn_w_up",
        "L0_ffn_w_down"]


def kernel(**inputs):
    import numpy as _np
    import concourse.bacc as _bacc
    from concourse import mybir as _mybir
    from concourse.bass_utils import run_bass_kernel_spmd as _run

    nc = _bacc.Bacc("TRN2", target_bir_lowering=False, num_devices=1)
    arrays, args = {}, []
    for name in _INS:
        a = _np.ascontiguousarray(inputs[name])
        arrays[f"in_{name}"] = a
        args.append(nc.dram_tensor(f"in_{name}", a.shape, _mybir.dt.from_np(a.dtype), kind="ExternalInput").ap())
    for name, a in zip(("const32", "const16"), tables()):
        arrays[name] = a
        args.append(nc.dram_tensor(name, a.shape, _mybir.dt.from_np(a.dtype), kind="ExternalInput").ap())
    args.append(nc.dram_tensor("out_0", (SEQS, SEQ, D), F32, kind="ExternalOutput").ap())
    layer_kernel(nc, *args)
    r = _run(nc, [arrays], core_ids=[0])
    return r.results[0]["out_0"]
```
